# Optimizing a Trainium2 kernel written in Bass

```python
import numpy as np
import jax
import jax.numpy as jnp

def _softmax(x, axis=-1):
    return jax.nn.softmax(x, axis=axis)

def _gelu(x):
    return jax.nn.gelu(x, approximate=True)

def _silu(x):
    return jax.nn.silu(x)

def _sigmoid(x):
    return jax.nn.sigmoid(x)

def _layernorm(x, axis=-1, eps=1e-05):
    m = jnp.mean(x, axis=axis, keepdims=True)
    v = jnp.var(x, axis=axis, keepdims=True)
    return (x - m) / jnp.sqrt(v + eps)

def _scatter_add(tgt, idx, src, axis=0):
    return tgt.at[idx].add(src)

def _segment_sum(src, seg, n):
    return jax.ops.segment_sum(src, seg, n)
kernel_name = 'mk_sandwich_d1_jaxref_r4_2899e7'

def setup_inputs(seed: int=0):
    np.random.seed(seed)
    _w = jnp.asarray

    def _L0_attn_setup():
        import jax, jax.numpy as jnp
        import numpy as np
        B, S, DIM, HD = (64, 200, 256, 128)
        BASE = 10000.0

        def _rope(t, cos, sin):
            tr = t[..., 0::2]
            ti = t[..., 1::2]
            rr = tr * cos - ti * sin
            ri = tr * sin + ti * cos
            return jnp.stack([rr, ri], axis=-1).reshape(t.shape)
        key = jax.random.key(seed)
        ks = jax.random.split(key, 5)
        x = jax.random.normal(ks[0], (B, S, DIM), jnp.float32)
        si = DIM ** (-0.5)
        so = HD ** (-0.5)
        wq = jax.random.normal(ks[1], (HD, DIM), jnp.float32) * si
        wk = jax.random.normal(ks[2], (HD, DIM), jnp.float32) * si
        wv = jax.random.normal(ks[3], (HD, DIM), jnp.float32) * si
        wo = jax.random.normal(ks[4], (DIM, HD), jnp.float32) * so
        return {'x': x, 'wq': wq, 'wk': wk, 'wv': wv, 'wo': wo}
    _L0_attn_in = _L0_attn_setup()

    def _L0_ffn_setup():
        import jax, jax.numpy as jnp
        import numpy as np
        EPS = 1e-09
        RMS_EPS = 1e-06
        TOP_K = 2
        LOOPS = 2

        def _rmsnorm(x, w):
            var = jnp.mean(x * x, axis=-1, keepdims=True)
            return x * jax.lax.rsqrt(var + RMS_EPS) * w

        def _swiglu(x, w1, w3, w2):
            h = jax.nn.silu(x @ w1) * (x @ w3)
            return h @ w2
        key = jax.random.key(seed)
        ks = jax.random.split(key, 5)
        B, S, D, F, E = (4, 512, 256, 512, 8)
        z = jax.random.normal(ks[0], (B, S, D), dtype=jnp.float32)
        norm_w = jnp.ones((D,), dtype=jnp.float32)
        router_w = jax.random.normal(ks[1], (D, E), dtype=jnp.float32) * 0.02
        w1 = jax.random.normal(ks[2], (E, D, F), dtype=jnp.float32) * 0.02
        w3 = jax.random.normal(ks[3], (E, D, F), dtype=jnp.float32) * 0.02
        w2 = jax.random.normal(ks[4], (E, F, D), dtype=jnp.float32) * 0.02
        return {'z': z, 'norm_w': norm_w, 'router_w': router_w, 'w1': w1, 'w3': w3, 'w2': w2}
    _L0_ffn_in = _L0_ffn_setup()
    _d = {'L0_attn_x': _L0_attn_in['x'], 'L0_attn_wq': _L0_attn_in['wq'], 'L0_attn_wk': _L0_attn_in['wk'], 'L0_attn_wv': _L0_attn_in['wv'], 'L0_attn_wo': _L0_attn_in['wo'], 'L0_ffn_norm_w': _L0_ffn_in['norm_w'], 'L0_ffn_router_w': _L0_ffn_in['router_w'], 'L0_ffn_w1': _L0_ffn_in['w1'], 'L0_ffn_w3': _L0_ffn_in['w3'], 'L0_ffn_w2': _L0_ffn_in['w2']}
    _x0 = _d['L0_attn_x']
    _d['L0_attn_x'] = jax.random.normal(jax.random.fold_in(jax.random.key(seed), 1), (2, 2048, 256), dtype=_x0.dtype)
    del _x0
    return _d

def reference(L0_attn_x, L0_attn_wq, L0_attn_wk, L0_attn_wv, L0_attn_wo, L0_ffn_norm_w, L0_ffn_router_w, L0_ffn_w1, L0_ffn_w3, L0_ffn_w2):

    def _L0_attn_ref(x, wq, wk, wv, wo):
        import jax, jax.numpy as jnp
        import numpy as np
        B, S, DIM, HD = (64, 200, 256, 128)
        BASE = 10000.0

        def _rope(t, cos, sin):
            tr = t[..., 0::2]
            ti = t[..., 1::2]
            rr = tr * cos - ti * sin
            ri = tr * sin + ti * cos
            return jnp.stack([rr, ri], axis=-1).reshape(t.shape)
        hd = wq.shape[0]
        seq = x.shape[1]
        q = jnp.einsum('bsd,hd->bsh', x, wq)
        k = jnp.einsum('bsd,hd->bsh', x, wk)
        v = jnp.einsum('bsd,hd->bsh', x, wv)
        inv_freq = 1.0 / BASE ** (jnp.arange(0, hd, 2, dtype=jnp.float32) / hd)
        t = jnp.arange(seq - 1, dtype=jnp.float32)
        ang = t[:, None] * inv_freq[None, :]
        cos, sin = (jnp.cos(ang), jnp.sin(ang))
        apply_rope = lambda z: jnp.concatenate([z[:, :1], _rope(z[:, 1:], cos, sin)], axis=1)
        q = apply_rope(q)
        k = apply_rope(k)
        scale = float(np.sqrt(hd))
        w = jax.nn.softmax(jnp.einsum('bqh,bkh->bqk', q, k) / scale, axis=-1)
        out = jnp.einsum('bqk,bkh->bqh', w, v)
        return jnp.einsum('bsh,dh->bsd', out, wo)

    def _L0_ffn_ref(z, norm_w, router_w, w1, w3, w2):
        import jax, jax.numpy as jnp
        import numpy as np
        EPS = 1e-09
        RMS_EPS = 1e-06
        TOP_K = 2
        LOOPS = 2

        def _rmsnorm(x, w):
            var = jnp.mean(x * x, axis=-1, keepdims=True)
            return x * jax.lax.rsqrt(var + RMS_EPS) * w

        def _swiglu(x, w1, w3, w2):
            h = jax.nn.silu(x @ w1) * (x @ w3)
            return h @ w2
        B, S, D = z.shape
        E = router_w.shape[-1]
        T = B * S
        for _ in range(LOOPS):
            z_norm = _rmsnorm(z, norm_w)
            logits = z_norm @ router_w
            scores = jax.nn.softmax(logits, axis=-1)
            topk_vals, topk_idx = jax.lax.top_k(scores, TOP_K)
            topk_vals = topk_vals / (jnp.sum(topk_vals, axis=-1, keepdims=True) + EPS)
            cw = jnp.sum(jax.nn.one_hot(topk_idx, E, dtype=z.dtype) * topk_vals[..., None], axis=-2)
            flat_z = z_norm.reshape(T, D)
            flat_cw = cw.reshape(T, E)
            mixed = jnp.zeros((T, D), dtype=z.dtype)
            for e in range(E):
                mixed = mixed + flat_cw[:, e:e + 1] * _swiglu(flat_z, w1[e], w3[e], w2[e])
            z = z + mixed.reshape(B, S, D)
        return z
    x = L0_attn_x
    x = x + _layernorm(_L0_attn_ref(_layernorm(x, axis=-1), L0_attn_wq, L0_attn_wk, L0_attn_wv, L0_attn_wo), axis=-1)
    x = x + _layernorm(_L0_ffn_ref(_layernorm(x, axis=-1), L0_ffn_norm_w, L0_ffn_router_w, L0_ffn_w1, L0_ffn_w3, L0_ffn_w2), axis=-1)
    return x

_drawn_inputs = setup_inputs


def setup_inputs(seed=0):
    import zlib

    import numpy as np

    out = dict(_drawn_inputs(seed))
    spreads = {'L0_ffn_norm_w': (1.0, 0.6)}
    factors = {'L0_ffn_router_w': 4.253, 'L0_ffn_w1': 3.705, 'L0_ffn_w3': 3.655, 'L0_ffn_w2': 3.656}
    for name, (base, spread) in spreads.items():
        noise = np.random.default_rng([zlib.crc32(name.encode()), seed]).standard_normal(out[name].shape)
        drawn = base * np.exp(spread * noise) if base else spread * noise
        out[name] = jnp.asarray(drawn.astype(out[name].dtype))
    for name, factor in factors.items():
        out[name] = (out[name] * factor).astype(out[name].dtype)
    return out
```

```python
from contextlib import ExitStack

import concourse.bass as bass
import numpy as np
from concourse import mybir

ALU = mybir.AluOpType
ACT = mybir.ActivationFunctionType
AX = mybir.AxisListType
F32 = mybir.dt.float32
F16 = mybir.dt.float16
I32 = mybir.dt.int32
U32 = mybir.dt.uint32
ABSMAX = bass.bass_isa.ReduceOp.absmax

P = 128
B, S, D, HD = 2, 2048, 256, 128
NE, FF, LOOPS = 8, 512, 2
DC, FC = D // P, FF // P
NT = S // P
PAIRS = NT // 2
KB = S // 512
TILES = 2 * S // P + NE - 1
ROWS = TILES * P
ZW = D + 4
GROUP = 512
NG = (2 * DC * FF + FC * D) // GROUP
EW = NG * 2 * GROUP

LN_EPS, RMS_EPS, GATE_EPS = 1e-5, 1e-6, 1e-9
W_EXP = 9
X_SCALE = 2.0**11
QKV_SCALE = 2.0**-15
P_SCALE = 2.0**14
ARENA = 19700
EXP_BITS = 0x7F800000
ROPE_BASE = 10000.0


def rope_table():
    inv = np.float32(1.0) / np.float32(ROPE_BASE) ** (np.arange(0, HD, 2, dtype=np.float32) / np.float32(HD))
    ang = np.arange(S - 1, dtype=np.float32)[:, None] * inv[None, :]
    cos = np.concatenate([np.ones((1, HD // 2), np.float32), np.cos(ang)])
    sin = np.concatenate([np.zeros((1, HD // 2), np.float32), np.sin(ang)])
    return (np.stack([cos, sin, cos], axis=1) * np.float32(QKV_SCALE)).astype(np.float32)


def sandwich_kernel(nc, x, wq, wk, wv, wo, norm_w, router_w, w1, w3, w2, rope, out, sorted_rows, expert_rows):
    with ExitStack() as ctx:

        def sb(name, shape, dt=F32):
            return ctx.enter_context(nc.sbuf_tensor(name, shape, dt))

        def sem(name):
            return ctx.enter_context(nc.semaphore(name))

        w_raw = sb("w_raw", [P, NE * NG * GROUP])
        w_split = w_raw[:, :].bitcast(F16)
        x_sb = sb("x_sb", [P, B * NT * D])
        ident = sb("ident", [P, P])
        before = sb("before", [P, P])
        ones = sb("ones", [P, P])
        neg_half = sb("neg_half", [P, NT])
        norm_c = sb("norm_c", [P, DC])
        router_c = sb("router_c", [P, DC, NE])
        amax_a = sb("amax_a", [P, 4])
        pow_a = sb("pow_a", [P, 4])
        scale_a = sb("scale_a", [P, 4])
        amax_g = sb("amax_g", [P, NE, NG])
        amax_f = sb("amax_f", [P, 8])
        pow_f = sb("pow_f", [P, 3])
        scale_f = sb("scale_f", [P, 3])
        scale_wn = sb("scale_wn", [P, 2 * DC])
        alpha = sb("alpha", [P, 1])
        neg_alpha = sb("neg_alpha", [P, 1])
        attn_eps = sb("attn_eps", [P, 1])
        silu_scale = sb("silu_scale", [P, 1])
        gate_scale = sb("gate_scale", [P, 1])
        y_unscale = sb("y_unscale", [P, 1])

        arena = sb("arena", [P, ARENA])
        used = [0]

        def take(words):
            a = arena[:, used[0] : used[0] + words]
            used[0] += words
            assert used[0] <= ARENA, used[0]
            return a

        qkT = take(2 * 2 * S // 2).bitcast(F16).rearrange("p (l m s) -> p l m s", l=2, m=2)
        v_sb = take(NT * 2 * HD // 2).bitcast(F16)
        v_tiles = v_sb.rearrange("p (t l h) -> p t l h", t=NT, l=2)
        probs = take(S)
        pT = take(2 * S // 2).bitcast(F16).rearrange("p (l s) -> p l s", l=2)
        tab = take(NT * 3 * HD // 2)
        rot = take(2 * 2 * 2 * HD).rearrange("p (u m n) -> p u m n", u=2, m=2)
        qk_tok = take(2 * 2 * HD).rearrange("p (u n) -> p u n", u=2)
        xn = take(2 * D).rearrange("p (u d) -> p u d", u=2)
        xT = take(2 * 2 * D // 2).bitcast(F16).rearrange("p (l u c t) -> p l u c t", l=2, u=2, c=DC)
        o_tok = take(HD)
        o_part = take(HD)
        oT = take(2 * P // 2).bitcast(F16).rearrange("p (l t) -> p l t", l=2)
        y_norm = take(D)
        w_tmp = take(2 * GROUP).rearrange("p (u n) -> p u n", u=2)
        zeros = take(3 * ZW)
        attn_raw = probs[:, 0 : 4 * D].rearrange("p (m n) -> p m n", m=4)
        wqkvT = take(DC * 2 * 3 * HD // 2).bitcast(F16).rearrange("p (c l n) -> p c l n", c=DC, l=2)
        woT = take(2 * D // 2).bitcast(F16).rearrange("p (l n) -> p l n", l=2)
        stats = take(NT * 6).rearrange("p (t k) -> p t k", t=NT)
        mean_x = take(NT)
        rstd_x = take(NT)
        tmp_x = take(4 * NT).rearrange("p (k t) -> p k t", k=4)
        row_max = take(2)
        neg_max = take(1)
        row_sum = take(2)
        row_rec = take(1)
        y_stats = take(6)
        y_mv = take(2)
        y_var = take(1)
        y_negmean = take(1)
        y_rstd = take(1)
        y_shift = take(1)

        psum_s = ctx.enter_context(nc.psum_tensor("psum_s", [P, S], F32))
        psum_t = [ctx.enter_context(nc.psum_tensor(f"psum_t{i}", [P, 512], F32)) for i in range(2)]
        psum_o = ctx.enter_context(nc.psum_tensor("psum_o", [P, 512], F32))
        psum_y = ctx.enter_context(nc.psum_tensor("psum_y", [P, 512], F32))

        s_x = [sem(f"x_loaded{i}") for i in range(4)]
        s_attn_w = sem("attn_weights_loaded")
        s_small = sem("small_inputs_loaded")
        s_tab = sem("rope_loaded")
        s_raw = [sem(f"expert_loaded{e}") for e in range(NE)]
        s_zero_fill = sem("sorted_rows_zeroed")
        s_const = sem("constants_ready")
        s_amax_a = sem("attn_amax_parts")
        s_all_a = sem("attn_amax_ready")
        s_scale_a = sem("attn_scales_ready")
        s_wt = sem("attn_weights_turned")
        s_wt_hi = sem("attn_weights_hi")
        s_wt_lo = sem("attn_weights_lo")
        s_amax_f = sem("expert_amax_parts")
        s_all_f = sem("expert_amax_ready")
        s_scale_f = sem("expert_scales_ready")
        s_wsplit = sem("expert_weights_steps")
        s_dve = sem("vector_steps")
        s_var_x = sem("ln_variance_ready")
        s_rstd_x = sem("ln_rstd_ready")
        s_xn = sem("xn_ready")
        s_tx = sem("xn_turned")
        s_xt_hi = sem("xT_hi")
        s_xt_lo = sem("xT_lo")
        s_qkv = sem("qkv_ready")
        s_v_hi = sem("v_hi")
        s_rot = sem("qkv_bank_read")
        s_qk = sem("qk_rotated")
        s_tqk = sem("qk_turned")
        s_qk_hi = sem("qkT_hi")
        s_qk_lo = sem("qkT_lo")
        s_scores = sem("scores_ready")
        s_max = sem("row_max_parts")
        s_negmax = sem("neg_max_ready")
        s_exp = sem("probs_ready")
        s_tp = sem("probs_turned")
        s_p_hi = sem("pT_hi")
        s_p_lo = sem("pT_lo")
        s_pv = sem("weighted_values_ready")
        s_sum = sem("row_sum_ready")
        s_rec = sem("row_rec_ready")
        s_o_part = sem("o_part_ready")
        s_o = sem("o_ready")
        s_to = sem("o_turned")
        s_o_hi = sem("oT_hi")
        s_o_lo = sem("oT_lo")
        s_proj = sem("projection_ready")
        s_ystat = sem("y_stats_ready")
        s_ymv = sem("y_mean_var_ready")
        s_held = sem("waits_held")
        s_yvar = sem("y_var_ready")
        s_yrstd = sem("y_rstd_ready")
        s_yshift = sem("y_shift_ready")
        s_ynorm = sem("y_norm_ready")
        s_x1 = sem("x1_ready")

        dve_steps = [0]

        def tile_of(j):
            return bass.ds(j * D, D)

        block_stack = ctx.enter_context(ExitStack())
        block = block_stack.enter_context(nc.Block())


        @block.sync
        def _(sp):
            x_view = x.rearrange("b (t p) d -> p (b t) d", p=P)
            x_dst = x_sb[:, :].rearrange("p (t d) -> p t d", d=D)
            q = B * NT // 4
            sp.dma_start(x_dst[:, 0:q, :], x_view[:, 0:q, :]).then_inc(s_x[0], 16)
            for m, w in enumerate((wq, wk, wv)):
                sp.dma_start(attn_raw[:, m, :], w).then_inc(s_attn_w, 16)
            sp.dma_start(attn_raw[:, 3, :].rearrange("p (c h) -> p c h", c=DC),
                         wo.rearrange("(c p) h -> p c h", p=P)).then_inc(s_attn_w, 16)
            for c in range(1, 4):
                sp.dma_start(x_dst[:, c * q : (c + 1) * q, :], x_view[:, c * q : (c + 1) * q, :]).then_inc(s_x[c], 16)
                if c == 1:
                    sp.dma_start(tab.rearrange("p (t k) -> p t k", t=NT),
                                 rope.rearrange("(t p) c k -> p t (c k)", p=P)).then_inc(s_tab, 16)
                    with nc.allow_non_contiguous_dma(reason="256 values"):
                        sp.dma_start(norm_c[:, :], norm_w.rearrange("(c p) -> p c", p=P)).then_inc(s_small, 16)
                    sp.dma_start(router_c[:, :, :], router_w.rearrange("(c p) e -> p c e", p=P)).then_inc(s_small, 16)
            for e in range(NE):
                at = e * NG * GROUP
                for w, chunks, width in ((w1, DC, FF), (w3, DC, FF), (w2, FC, D)):
                    n = chunks * width
                    sp.dma_start(w_raw[:, at : at + n].rearrange("p (c f) -> p c f", c=chunks),
                                 w[e].rearrange("(c p) f -> p c f", p=P)).then_inc(s_raw[e], 16)
                    at += n
            sp.wait_ge(s_const, 3)
            for h in range(B):
                for t in range(0, TILES, 3):
                    sp.dma_start(sorted_rows[h][t * P : (t + 3) * P, :].rearrange("(t p) d -> p t d", p=P),
                                 zeros.rearrange("p (t d) -> p t d", t=3)).then_inc(s_zero_fill, 16)
            sp.wait_ge(s_zero_fill, 16 * B * (TILES // 3))

        @block.gpsimd
        def _(pool):
            nc.gpsimd.memset(ident[:, :], 0.0).then_inc(s_const, 1)
            nc.gpsimd.memset(ones[:, :], 1.0).then_inc(s_const, 1)
            nc.gpsimd.memset(zeros, 0.0).then_inc(s_const, 1)
            nc.gpsimd.memset(neg_half[:, :], -0.5).then_inc(s_const, 1)
            pool.wait_ge(s_const, 4)
            nc.gpsimd.affine_select(out=ident[:, :], in_=ident[:, :], compare_op=ALU.not_equal, fill=1.0,
                                    base=0, pattern=[[-1, P]], channel_multiplier=1).then_inc(s_const, 1)
            nc.gpsimd.affine_select(out=before[:, :], in_=ones[:, :], compare_op=ALU.is_gt, fill=0.0,
                                    base=0, pattern=[[1, P]], channel_multiplier=-1).then_inc(s_const, 1)
            pool.wait_ge(s_const, 6)
            pool.wait_ge(s_amax_a, 1)
            nc.gpsimd.partition_all_reduce(amax_a[:, :], amax_a[:, :], P, ABSMAX).then_inc(s_all_a, 1)
            pool.wait_ge(s_amax_f, 1)
            nc.gpsimd.partition_all_reduce(amax_f[:, 0:3], amax_f[:, 0:3], P, ABSMAX).then_inc(s_all_f, 1)

            def split_group(e, g):
                n = NG * e + g
                raw = w_raw[:, n * GROUP : (n + 1) * GROUP]
                both = w_split[:, 2 * n * GROUP : 2 * (n + 1) * GROUP]
                by = scale_wn[:, g : g + 1] if g < 2 * DC else scale_f[:, 2:3]
                tmp = w_tmp[:, n % 2, :]
                if g == 0:
                    pool.wait_ge(s_raw[e], 48)
                nc.gpsimd.tensor_scalar(tmp, raw, by, 1.0, ALU.mult, ALU.mult).then_inc(s_wsplit, 1)
                pool.wait_ge(s_wsplit, 3 * n + 1)
                nc.gpsimd.tensor_scalar(both[:, 0:GROUP], tmp, 1.0, 1.0, ALU.mult, ALU.mult).then_inc(s_wsplit, 1)
                pool.wait_ge(s_wsplit, 3 * n + 2)
                nc.gpsimd.tensor_tensor(both[:, GROUP:], tmp, both[:, 0:GROUP], ALU.subtract).then_inc(s_wsplit, 1)
                pool.wait_ge(s_wsplit, 3 * n + 3)

            groups = [(e, g) for e in range(NE) for g in range(NG)]

            def rotate(n):
                for u in range(2):
                    pool.wait_ge(s_rot, 2 * n + u + 1)
                    if not (isinstance(n, int) and n == 0):
                        pool.wait_ge(s_tqk, n)
                    c = rot[:, u, 0, :].rearrange("p (m c k) -> p m c k", m=2, c=2)
                    s = rot[:, u, 1, :].rearrange("p (m c k) -> p m c k", m=2, c=2)
                    o = qk_tok[:, u, :].rearrange("p (m c k) -> p m c k", m=2, c=2)
                    nc.gpsimd.tensor_tensor(o[:, :, 0, :], c[:, :, 0, :], s[:, :, 0, :], ALU.subtract)
                    nc.gpsimd.tensor_tensor(o[:, :, 1, :], c[:, :, 1, :], s[:, :, 1, :], ALU.add).then_inc(s_qk, 1)

            def normalise(t):
                pool.wait_ge(s_yvar, t + 1)
                nc.gpsimd.tensor_tensor(y_rstd, y_var, neg_half[:, 0:1], ALU.pow).then_inc(s_yrstd, 1)
                pool.wait_ge(s_yrstd, t + 1)
                nc.gpsimd.tensor_tensor(y_shift, y_negmean, y_rstd, ALU.mult).then_inc(s_yshift, 1)
                pool.wait_ge(s_ynorm, t + 1)
                nc.gpsimd.tensor_tensor(x_sb[:, tile_of(t)], x_sb[:, tile_of(t)], y_norm, ALU.add).then_inc(s_x1, 1)

            pool.wait_ge(s_scale_f, 1)
            for b in range(B):
                pool.wait_ge(s_var_x, b + 1)
                nc.gpsimd.tensor_tensor(rstd_x, tmp_x[:, 3, :], neg_half[:, :], ALU.pow).then_inc(s_rstd_x, 1)
                n0 = b * PAIRS
                rotate(n0)
                with pool.Fori(1, PAIRS) as i:
                    rotate(n0 + i)
                if b == 0:
                    for e, g in groups:
                        split_group(e, g)
                t0 = b * NT
                with pool.Fori(0, NT) as i:
                    normalise(t0 + i)

        @block.scalar
        def _(act):
            act.wait_ge(s_scale_a, 1)
            act.wait_ge(s_wt, 2)
            for m in range(3):
                src = psum_t[m // 2][:, (m % 2) * D : (m % 2 + 1) * D].rearrange("p (c n) -> p c n", c=DC)
                nc.scalar.activation(wqkvT[:, :, 0, m * HD : (m + 1) * HD], src, ACT.Copy,
                                     scale=scale_a[:, m : m + 1]).then_inc(s_wt_hi, 1)
            nc.scalar.activation(woT[:, 0, :], psum_t[1][:, D : 2 * D], ACT.Copy,
                                 scale=scale_a[:, 3:4]).then_inc(s_wt_hi, 1)

            def x_hi(n):
                act.wait_ge(s_tx, n + 1)
                nc.scalar.activation(xT[:, 0, :, :, :].rearrange("p u c t -> p (u c t)"), psum_t[0][:, :],
                                     ACT.Copy).then_inc(s_xt_hi, 1)

            def v_hi(n, i):
                for u in range(2):
                    act.wait_ge(s_qkv, 2 * n + u + 1)
                    nc.scalar.activation(v_sb[:, bass.ds((2 * i + u) * 2 * HD, HD)],
                                         psum_s[:, u * 512 + 2 * HD : u * 512 + 3 * HD], ACT.Copy,
                                         scale=QKV_SCALE).then_inc(s_v_hi, 1)

            def qk_hi(n, i):
                act.wait_ge(s_tqk, n + 1)
                nc.scalar.activation(qkT[:, 0, :, bass.ds(i * 2 * P, 2 * P)],
                                     psum_t[1][:, :].rearrange("p (m t) -> p m t", m=2), ACT.Copy).then_inc(s_qk_hi, 1)

            def p_hi(t, g):
                act.wait_ge(s_tp, 4 * t + g + 1)
                nc.scalar.activation(pT[:, 0, g * 512 : (g + 1) * 512], psum_t[g % 2][:, :], ACT.Copy,
                                     scale=P_SCALE).then_inc(s_p_hi, 1)

            def step(t, new, turn, fin):
                if turn:
                    p_hi(t - 1, 0)
                    p_hi(t - 1, 1)
                if fin:
                    act.wait_ge(s_to, t - 1)
                    nc.scalar.activation(oT[:, 0, :], psum_y[:, 0:P], ACT.Copy).then_inc(s_o_hi, 1)
                if turn:
                    p_hi(t - 1, 2)
                    p_hi(t - 1, 3)
                if new:
                    act.wait_ge(s_negmax, t + 1)
                    for h in range(2):
                        if turn:
                            act.wait_ge(s_tp, 4 * (t - 1) + 2 * h + 2)
                        nc.scalar.activation(probs[:, h * S // 2 : (h + 1) * S // 2],
                                             psum_s[:, h * S // 2 : (h + 1) * S // 2], ACT.Exp, bias=neg_max,
                                             scale=alpha[:, 0:1], accum_out=row_sum[:, h : h + 1]).then_inc(s_exp, 1)
                if fin:
                    act.wait_ge(s_yshift, t - 1)
                    nc.scalar.activation(y_norm, psum_y[:, D : 2 * D], ACT.Identity, bias=y_shift,
                                         scale=y_rstd).then_inc(s_ynorm, 1)
                if turn:
                    act.wait_ge(s_pv, t)
                    act.wait_ge(s_rec, t)
                    nc.scalar.activation(o_part, psum_o[:, HD : 2 * HD], ACT.Copy, scale=row_rec).then_inc(s_o_part, 1)

            for b in range(B):
                n0 = b * PAIRS
                x_hi(n0)
                with act.Fori(0, PAIRS - 1) as i:
                    v_hi(n0 + i, i)
                    x_hi(n0 + i + 1)
                    qk_hi(n0 + i, i)
                v_hi(n0 + PAIRS - 1, PAIRS - 1)
                qk_hi(n0 + PAIRS - 1, PAIRS - 1)
                t0 = b * NT
                step(t0, True, False, False)
                step(t0 + 1, True, True, False)
                with act.Fori(2, NT) as i:
                    step(t0 + i, True, True, True)
                step(t0 + NT, False, True, True)
                step(t0 + NT + 1, False, False, True)

        @block.vector
        def _(dve):
            def link(ins):
                dve_steps[0] += 1
                ins.then_inc(s_dve, 1)
                dve.wait_ge(s_dve, dve_steps[0])

            def powers(amax, pow2, scale, signal):
                link(nc.vector.tensor_scalar(amax, amax, 2.0**-60, None, ALU.max))
                link(nc.vector.tensor_scalar(pow2.bitcast(I32), amax.bitcast(I32), EXP_BITS, None, ALU.bitwise_and))
                link(nc.vector.tensor_scalar(scale.bitcast(I32), pow2.bitcast(I32), -1.0,
                                             float((W_EXP + 2 * 127) << 23), ALU.mult, ALU.add))

            dve.wait_ge(s_attn_w, 64)
            nc.vector.tensor_reduce(amax_a[:, :], attn_raw, AX.X, ALU.max, apply_absolute_value=True).then_inc(s_amax_a, 1)
            dve.wait_ge(s_all_a, 1)
            powers(amax_a[:, :], pow_a[:, :], scale_a[:, :], None)
            link(nc.vector.tensor_tensor(alpha[:, :], pow_a[:, 0:1], pow_a[:, 1:2], ALU.mult))
            link(nc.vector.tensor_scalar(alpha[:, :], alpha[:, :], 2.0 ** (-2 * (W_EXP - 4)) / float(np.sqrt(HD)), None, ALU.mult))
            link(nc.vector.tensor_scalar(neg_alpha[:, :], alpha[:, :], -1.0, None, ALU.mult))
            link(nc.vector.tensor_tensor(attn_eps[:, :], scale_a[:, 2:3], scale_a[:, 3:4], ALU.mult))
            link(nc.vector.tensor_scalar(attn_eps[:, :], attn_eps[:, :], X_SCALE * QKV_SCALE, None, ALU.mult))
            link(nc.vector.tensor_tensor(attn_eps[:, :], attn_eps[:, :], attn_eps[:, :], ALU.mult))
            nc.vector.tensor_scalar(attn_eps[:, :], attn_eps[:, :], LN_EPS, None, ALU.mult).then_inc(s_scale_a, 1)
            dve.wait_ge(s_wt_hi, 4)
            for m in range(3):
                src = psum_t[m // 2][:, (m % 2) * D : (m % 2 + 1) * D].rearrange("p (c n) -> p c n", c=DC)
                at = slice(m * HD, (m + 1) * HD)
                nc.vector.scalar_tensor_tensor(wqkvT[:, :, 1, at], src, scale_a[:, m : m + 1], wqkvT[:, :, 0, at],
                                               ALU.mult, ALU.subtract).then_inc(s_wt_lo, 1)
            nc.vector.scalar_tensor_tensor(woT[:, 1, :], psum_t[1][:, D : 2 * D], scale_a[:, 3:4], woT[:, 0, :],
                                           ALU.mult, ALU.subtract).then_inc(s_wt_lo, 1)

            for e in range(NE):
                dve.wait_ge(s_raw[e], 48)
                src = w_raw[:, e * NG * GROUP : (e + 1) * NG * GROUP].rearrange("p (g n) -> p g n", g=NG)
                link(nc.vector.tensor_reduce(amax_g[:, e, :], src, AX.X, ALU.max, apply_absolute_value=True))
            dve.wait_ge(s_small, 32)
            link(nc.vector.tensor_reduce(amax_f[:, 0:NG], amax_g[:, :, :].rearrange("p e g -> p g e"), AX.X, ALU.max))
            for m in range(2):
                link(nc.vector.tensor_tensor(amax_f[:, m * DC : (m + 1) * DC], amax_f[:, m * DC : (m + 1) * DC],
                                             norm_c[:, :], ALU.mult))
            for m in range(3):
                link(nc.vector.tensor_reduce(amax_f[:, m : m + 1], amax_f[:, m * DC : (m + 1) * DC], AX.X, ALU.max,
                                             apply_absolute_value=True))
            nc.vector.tensor_scalar(amax_f[:, 6:7], amax_f[:, 0:1], 1.0, None, ALU.mult).then_inc(s_amax_f, 1)
            dve.wait_ge(s_all_f, 1)
            powers(amax_f[:, 0:3], pow_f[:, :], scale_f[:, :], None)
            for m in range(2):
                link(nc.vector.tensor_scalar(scale_wn[:, m * DC : (m + 1) * DC], norm_c[:, :], scale_f[:, m : m + 1],
                                             None, ALU.mult))
            link(nc.vector.tensor_scalar(silu_scale[:, :], pow_f[:, 0:1], 2.0**-W_EXP / X_SCALE, None, ALU.mult))
            link(nc.vector.tensor_scalar(gate_scale[:, :], scale_f[:, 0:1], 2.0**-21 / X_SCALE, None, ALU.mult))
            link(nc.vector.tensor_tensor(y_unscale[:, :], pow_f[:, 0:1], pow_f[:, 1:2], ALU.mult))
            link(nc.vector.tensor_tensor(y_unscale[:, :], y_unscale[:, :], pow_f[:, 2:3], ALU.mult))
            link(nc.vector.tensor_scalar(y_unscale[:, :], y_unscale[:, :], 2.0 ** (21 - 3 * W_EXP), None, ALU.mult))
            for c in range(DC):
                link(nc.vector.tensor_scalar(router_c[:, c, :], router_c[:, c, :], norm_c[:, c : c + 1], None, ALU.mult))
            nc.vector.tensor_scalar(amax_f[:, 7:8], amax_f[:, 0:1], 1.0, None, ALU.mult).then_inc(s_scale_f, 1)

            def x_norm(n, i):
                for u in range(2):
                    if not (isinstance(n, int) and n == 0):
                        dve.wait_ge(s_tx, n)
                    nc.vector.tensor_scalar(xn[:, u, :], x_sb[:, tile_of(2 * n + u)], mean_x[:, bass.ds(2 * i + u, 1)],
                                            rstd_x[:, bass.ds(2 * i + u, 1)], ALU.subtract, ALU.mult).then_inc(s_xn, 1)

            def x_lo(n):
                dve.wait_ge(s_xt_hi, n + 1)
                nc.vector.tensor_tensor(xT[:, 1, :, :, :].rearrange("p u c t -> p (u c t)"), psum_t[0][:, :],
                                        xT[:, 0, :, :, :].rearrange("p u c t -> p (u c t)"), ALU.subtract).then_inc(s_xt_lo, 1)

            def v_and_rotation(n, i):
                for u in range(2):
                    dve.wait_ge(s_v_hi, 2 * n + u + 1)
                    at = bass.ds((2 * i + u) * 2 * HD, HD)
                    lo = bass.ds((2 * i + u) * 2 * HD + HD, HD)
                    bank = psum_s[:, u * 512 : u * 512 + 3 * HD]
                    nc.vector.scalar_tensor_tensor(v_sb[:, lo], bank[:, 2 * HD :], QKV_SCALE, v_sb[:, at],
                                                   ALU.mult, ALU.subtract)
                    if not (isinstance(n, int) and n == 0):
                        dve.wait_ge(s_qk, 2 * n + u - 1)
                    pairs = bank[:, 0 : 2 * HD].rearrange("p (m k two) -> p m k two", m=2, two=2)
                    t = tab[:, bass.ds((2 * i + u) * 3 * HD // 2, 3 * HD // 2)].rearrange("p (c k) -> p c k", c=3)
                    shape = [P, 2, 2, HD // 2]
                    for odd in range(2):
                        ins = nc.vector.tensor_tensor(
                            rot[:, u, odd, :].rearrange("p (m c k) -> p m c k", m=2, c=2),
                            pairs[:, :, :, odd].unsqueeze(2).to_broadcast(shape),
                            t[:, odd : odd + 2, :].unsqueeze(1).to_broadcast(shape), ALU.mult)
                    ins.then_inc(s_rot, 1)

            def qk_lo(n, i):
                dve.wait_ge(s_qk_hi, n + 1)
                at = bass.ds(i * 2 * P, 2 * P)
                nc.vector.tensor_tensor(qkT[:, 1, :, at], psum_t[1][:, :].rearrange("p (m t) -> p m t", m=2),
                                        qkT[:, 0, :, at], ALU.subtract).then_inc(s_qk_lo, 1)

            def p_lo(t, g):
                dve.wait_ge(s_p_hi, 4 * t + g + 1)
                at = slice(g * 512, (g + 1) * 512)
                nc.vector.scalar_tensor_tensor(pT[:, 1, at], psum_t[g % 2][:, :], P_SCALE, pT[:, 0, at],
                                               ALU.mult, ALU.subtract).then_inc(s_p_lo, 1)

            def half_max(t, h):
                dve.wait_ge(s_scores, 2 * t + h + 1)
                nc.vector.tensor_reduce(row_max[:, h : h + 1], psum_s[:, h * S // 2 : (h + 1) * S // 2], AX.X,
                                        ALU.max).then_inc(s_max, 1)

            def step(t, new, turn, fin):
                if turn:
                    dve.wait_ge(s_exp, 2 * t)
                    nc.vector.tensor_scalar(row_sum[:, 0:1], row_sum[:, 0:1], row_sum[:, 1:2], P_SCALE,
                                            ALU.add, ALU.mult).then_inc(s_sum, 1)
                    dve.wait_ge(s_sum, t)
                    nc.vector.reciprocal(row_rec, row_sum[:, 0:1]).then_inc(s_rec, 1)
                    p_lo(t - 1, 0)
                    p_lo(t - 1, 1)
                if new:
                    half_max(t, 0)
                if fin:
                    dve.wait_ge(s_o_hi, t - 1)
                    nc.vector.tensor_tensor(oT[:, 1, :], psum_y[:, 0:P], oT[:, 0, :], ALU.subtract).then_inc(s_o_lo, 1)
                if new:
                    half_max(t, 1)
                    dve.wait_ge(s_max, 2 * t + 2)
                    nc.vector.scalar_tensor_tensor(neg_max, row_max[:, 0:1], row_max[:, 1:2], neg_alpha[:, 0:1],
                                                   ALU.max, ALU.mult).then_inc(s_negmax, 1)
                if turn:
                    p_lo(t - 1, 2)
                    p_lo(t - 1, 3)
                if fin:
                    dve.wait_ge(s_proj, t - 1)
                    nc.vector.bn_stats(y_stats, psum_y[:, D : 2 * D]).then_inc(s_ystat, 1)
                    dve.wait_ge(s_ystat, t - 1)
                    dve.sem_inc(s_held, 1)
                    nc.vector.bn_aggr(y_mv, y_stats).then_inc(s_ymv, 1)
                    dve.wait_ge(s_ymv, t - 1)
                    nc.vector.tensor_scalar(y_var, y_mv[:, 1:2], attn_eps[:, 0:1], None, ALU.add)
                    nc.vector.tensor_scalar(y_negmean, y_mv[:, 0:1], -1.0, None, ALU.mult).then_inc(s_yvar, 1)
                if turn:
                    dve.wait_ge(s_o_part, t)
                    if fin:
                        dve.wait_ge(s_to, t - 1)
                    nc.vector.scalar_tensor_tensor(o_tok, psum_o[:, 0:HD], row_rec, o_part, ALU.mult,
                                                   ALU.add).then_inc(s_o, 1)

            for b in range(B):
                for c in range(2 * b, 2 * b + 2):
                    dve.wait_ge(s_x[c], 16)
                with dve.Fori(0, NT) as i:
                    nc.vector.bn_stats(stats[:, bass.ds(i, 1), :].rearrange("p a k -> p (a k)"),
                                       x_sb[:, tile_of(b * NT + i)]).then_inc(s_dve, 1)
                dve_steps[0] += NT
                dve.wait_ge(s_dve, dve_steps[0])
                half_mean, half_m2 = (lambda k: stats[:, :, 3 * k + 1]), (lambda k: stats[:, :, 3 * k + 2])
                link(nc.vector.tensor_tensor(tmp_x[:, 0, :], half_mean(0), half_mean(1), ALU.subtract))
                link(nc.vector.tensor_tensor(tmp_x[:, 1, :], half_m2(0), half_m2(1), ALU.add))
                link(nc.vector.tensor_tensor(tmp_x[:, 2, :], tmp_x[:, 0, :], tmp_x[:, 0, :], ALU.mult))
                link(nc.vector.tensor_scalar(tmp_x[:, 1, :], tmp_x[:, 1, :], 1.0 / D, LN_EPS, ALU.mult, ALU.add))
                link(nc.vector.scalar_tensor_tensor(tmp_x[:, 3, :], tmp_x[:, 2, :], 0.25, tmp_x[:, 1, :], ALU.mult, ALU.add))
                link(nc.vector.tensor_tensor(mean_x, half_mean(0), half_mean(1), ALU.add))
                nc.vector.tensor_scalar(mean_x, mean_x, 0.5, None, ALU.mult).then_inc(s_var_x, 1)
                dve.wait_ge(s_rstd_x, b + 1)
                link(nc.vector.tensor_scalar(rstd_x, rstd_x, X_SCALE, None, ALU.mult))
                if b == 0:
                    dve.wait_ge(s_tab, 16)
                n0 = b * PAIRS
                x_norm(n0, 0)
                x_lo(n0)

                def pair(n, i, more):
                    if more:
                        x_norm(n + 1, i + 1)
                    v_and_rotation(n, i)
                    if more:
                        x_lo(n + 1)
                    qk_lo(n, i)

                pair(n0, 0, True)
                with dve.Fori(1, PAIRS - 1) as i:
                    pair(n0 + i, i, True)
                pair(n0 + PAIRS - 1, PAIRS - 1, False)
                t0 = b * NT
                step(t0, True, False, False)
                step(t0 + 1, True, True, False)
                with dve.Fori(2, NT) as i:
                    step(t0 + i, True, True, True)
                step(t0 + NT, False, True, True)
                step(t0 + NT + 1, False, False, True)

        @block.tensor
        def _(pe):
            pe.wait_ge(s_const, 5)
            pe.wait_ge(s_attn_w, 64)
            for m in range(4):
                for c in range(DC):
                    at = (m % 2) * D + c * P
                    last = nc.tensor.transpose(psum_t[m // 2][:, at : at + P], attn_raw[:, m, c * P : (c + 1) * P], ident[:, :])
                if m % 2:
                    last.then_inc(s_wt, 1)

            def turn_x(n):
                if isinstance(n, int) and n == 0:
                    pe.wait_ge(s_wt_lo, 4)
                else:
                    pe.wait_ge(s_xt_lo, n)
                for u in range(2):
                    pe.wait_ge(s_xn, 2 * n + u + 1)
                    for c in range(DC):
                        last = nc.tensor.transpose(psum_t[0][:, (u * DC + c) * P : (u * DC + c + 1) * P],
                                                   xn[:, u, c * P : (c + 1) * P], ident[:, :])
                last.then_inc(s_tx, 1)

            def qkv(n):
                pe.wait_ge(s_xt_lo, n + 1)
                for u in range(2):
                    if not (isinstance(n, int) and n == 0):
                        pe.wait_ge(s_rot, 2 * n + u - 1)
                    for k, (c, lx, lw) in enumerate([(c, a, w) for c in range(DC) for a, w in ((0, 0), (0, 1), (1, 0))]):
                        last = nc.tensor.matmul(psum_s[:, u * 512 : u * 512 + 3 * HD], xT[:, lx, u, c, :],
                                                wqkvT[:, c, lw, :], start=(k == 0), stop=(k == 3 * DC - 1))
                    last.then_inc(s_qkv, 1)

            def turn_qk(n):
                if not (isinstance(n, int) and n == 0):
                    pe.wait_ge(s_qk_lo, n)
                for u in range(2):
                    pe.wait_ge(s_qk, 2 * n + u + 1)
                    for m in range(2):
                        last = nc.tensor.transpose(psum_t[1][:, (2 * m + u) * P : (2 * m + u + 1) * P],
                                                   qk_tok[:, u, m * HD : (m + 1) * HD], ident[:, :])
                last.then_inc(s_tqk, 1)

            def turn_p(t, g):
                pe.wait_ge(s_exp, 2 * t + g // 2 + 1)
                for k in range(4):
                    kc = 4 * g + k
                    last = nc.tensor.transpose(psum_t[g % 2][:, k * P : (k + 1) * P], probs[:, kc * P : (kc + 1) * P], ident[:, :])
                last.then_inc(s_tp, 1)

            def scores(i, kb):
                for k, (lq, lk) in enumerate(((0, 0), (0, 1), (1, 0))):
                    last = nc.tensor.matmul(psum_s[:, kb * 512 : (kb + 1) * 512], qkT[:, lq, 0, bass.ds(i * P, P)],
                                            qkT[:, lk, 1, kb * 512 : (kb + 1) * 512], start=(k == 0), stop=(k == 2))
                return last

            def step(t, i, new, turn, fin):
                if turn:
                    for g in range(2):
                        if fin:
                            pe.wait_ge(s_p_lo, 4 * t - 6 + g + 1)
                        turn_p(t - 1, g)
                if new:
                    for h in range(2):
                        if turn:
                            pe.wait_ge(s_exp, 2 * t - 1 + h)
                        scores(i, 2 * h)
                        scores(i, 2 * h + 1).then_inc(s_scores, 1)
                if fin:
                    pe.wait_ge(s_o, t - 1)
                    if not (isinstance(t, int) and t == 2):
                        pe.wait_ge(s_ynorm, t - 2)
                    nc.tensor.transpose(psum_y[:, 0:P], o_tok, ident[:, :]).then_inc(s_to, 1)
                if turn:
                    for g in range(2, 4):
                        pe.wait_ge(s_p_lo, 4 * (t - 1) + g - 1)
                        turn_p(t - 1, g)
                if fin:
                    pe.wait_ge(s_o_lo, t - 1)
                    for k, (lo, lw) in enumerate(((0, 0), (0, 1), (1, 0))):
                        last = nc.tensor.matmul(psum_y[:, D : 2 * D], oT[:, lo, :], woT[:, lw, :], start=(k == 0), stop=(k == 2))
                    last.then_inc(s_proj, 1)
                if turn:
                    if fin:
                        pe.wait_ge(s_o, t - 1)
                    for kc in range(NT):
                        if kc % 4 == 0:
                            pe.wait_ge(s_p_lo, 4 * (t - 1) + kc // 4 + 1)
                        at = slice(kc * P, (kc + 1) * P)
                        nc.tensor.matmul(psum_o[:, 0 : 2 * HD], pT[:, 0, at], v_sb[:, kc * 2 * HD : (kc + 1) * 2 * HD],
                                         start=(kc == 0), stop=False, skip_group_check=True)
                        last = nc.tensor.matmul(psum_o[:, 0:HD], pT[:, 1, at], v_tiles[:, kc, 0, :],
                                                start=False, stop=(kc == NT - 1), skip_group_check=True)
                    last.then_inc(s_pv, 1)

            for b in range(B):
                n0 = b * PAIRS
                turn_x(n0)

                def pair(n, more):
                    qkv(n)
                    if more:
                        turn_x(n + 1)
                    turn_qk(n)

                pair(n0, True)
                with pe.Fori(1, PAIRS - 1) as i:
                    pair(n0 + i, True)
                pair(n0 + PAIRS - 1, False)
                t0 = b * NT
                pe.wait_ge(s_qk_lo, n0 + PAIRS)
                pe.wait_ge(s_rot, 2 * (n0 + PAIRS))
                step(t0, 0, True, False, False)
                step(t0 + 1, 1, True, True, False)
                with pe.Fori(2, NT) as i:
                    step(t0 + i, i, True, True, True)
                step(t0 + NT, None, False, True, True)
                step(t0 + NT + 1, None, False, False, True)

        used[0] = 0
        z_aug = take(B * NT * ZW)
        z_rows = z_aug.rearrange("p (t w) -> p t w", w=ZW)
        x_tile = take(ZW)
        x_row = take(D)
        e_xT = take(2 * D // 2).bitcast(F16).rearrange("p (l c t) -> p l c t", l=2, c=DC)
        silu_a = take(FF)
        h_row = take(FF)
        hT = take(2 * FF // 2).bitcast(F16).rearrange("p (l c t) -> p l c t", l=2, c=FC)
        y_row = take(D)
        zn = take(2 * D).rearrange("p (u d) -> p u d", u=2)
        znT = take(2 * D).rearrange("p (u c t) -> p u c t", u=2, c=DC)
        slots = 4
        gathered = take(slots * 2 * D).rearrange("p (g k d) -> p g k d", g=slots, k=2)
        squares = take(D)
        f_stats = take(NT * 6).rearrange("p (t k) -> p t k", t=NT)
        f_mean = take(NT)
        f_rstd = take(NT)
        f_tmp = take(4 * NT).rearrange("p (k t) -> p k t", k=4)
        sum_sq = take(NT)
        rms = take(2 * NT).rearrange("p (k t) -> p k t", k=2)
        r_logit = take(NT * NE)
        r_score = take(NT * NE)
        r_rest = take(NT * NE)
        r_pick = [take(NT * NE) for _ in range(2)]
        r_tmp = take(NT * NE)
        r_count = take(NT * NE)
        r_sum = take(NT * NE)
        tiny = take(4 * NT).rearrange("p (k t) -> p k t", k=4)
        best = take(2 * NT).rearrange("p (k t) -> p k t", k=2)
        gates = take(B * 2 * NT).rearrange("p (h k t) -> p h k t", h=B, k=2)
        rows_f = take(2 * NT).rearrange("p (k t) -> p k t", k=2)
        rows_of = take(B * 2 * NT).bitcast(U32).rearrange("p (h k t) -> p h k t", h=B, k=2)
        start_f = take(4 * NE).rearrange("p (k e) -> p k e", k=4)
        start_i = take(NE).bitcast(I32)
        rank_down = take(NE)
        rank_i = take(NE).bitcast(I32)
        tile_row = take(TILES)
        tile_row_i = take(TILES).bitcast(I32)
        tile_cmp = take(TILES * NE)
        expert_f = take(TILES)
        expert_of = take(B * TILES).bitcast(I32).rearrange("p (h t) -> p h t", h=B)
        zero_tile = take(NT)

        psum_a, psum_b = psum_s[:, 0:FF], psum_s[:, 512 : 512 + FF]
        psum_h, psum_x = psum_s[:, 1024:1536], psum_s[:, 1536 : 1536 + D]
        psum_e = psum_o[:, 0:D]
        psum_z, psum_l, psum_r = psum_t[0], psum_t[1], psum_y

        s_fconst = sem("routing_constants")
        s_pool = sem("pool_steps")
        s_fvar = sem("z_variance_ready")
        s_frstd = sem("z_rstd_ready")
        s_z = sem("z_ready")
        s_half = sem("z_first_expert_added")
        s_sq = sem("z_squared")
        s_ms = sem("mean_square_ready")
        s_rms = sem("rms_ready")
        s_zn = sem("zn_ready")
        s_tz = sem("zn_turned")
        s_znT = sem("znT_copied")
        s_logit = sem("logits_ready")
        s_shift = sem("shifted_logits_ready")
        s_expl = sem("exp_logits_ready")
        s_pick = sem("picks_ready")
        s_count = sem("counts_ready")
        s_rows = sem("rows_ready")
        s_eid = sem("tile_experts_ready")
        s_scat = [sem(f"rows_scattered{h}") for h in range(B)]
        s_ldx = sem("x_tile_loaded")
        s_xrow = sem("x_row_ready")
        s_te = sem("x_row_turned")
        s_ex_hi = sem("expert_xT_hi")
        s_ex_lo = sem("expert_xT_lo")
        s_a = sem("a_ready")
        s_b = sem("b_ready")
        s_silu = sem("silu_ready")
        s_h = sem("h_ready")
        s_th = sem("h_turned")
        s_h_hi = sem("hT_hi")
        s_h_lo = sem("hT_lo")
        s_e = sem("expert_out_ready")
        s_yrow = sem("y_row_ready")
        s_sty = [sem(f"y_row_stored{h}") for h in range(B)]
        s_gather = [sem(f"gathered{g}") for g in range(slots)]
        s_out_t = sem("out_normalised")
        s_out_r = sem("out_tile_ready")
        s_out = sem("out_stored")

        order = [(l, h) for l in range(LOOPS) for h in range(B)]

        def zrow(j):
            return bass.ds(j * ZW, D)

        def zfac(j):
            return bass.ds(j * ZW + D, 1)

        block_stack.close()
        block2 = ctx.enter_context(nc.Block())

        @block2.sync
        def _(sp):
            def load(h, n, s):
                if not (isinstance(s, int) and n + s == 0):
                    sp.wait_ge(s_xrow, n + s)
                sp.dma_start(x_tile, sorted_rows[h][bass.ds(s * P, P), :]).then_inc(s_ldx, 16)

            def store(h, n, s):
                sp.wait_ge(s_yrow, n + s + 1)
                sp.dma_start(expert_rows[h][bass.ds(s * P, P), :], y_row).then_inc(s_sty[h], 16)

            for k, (l, h) in enumerate(order):
                n = k * TILES
                sp.wait_ge(s_scat[h], 16 * 2 * NT * (l + 1))
                load(h, n, 0)
                load(h, n, 1)
                with sp.Fori(1, TILES - 1) as s:
                    load(h, n, s + 1)
                    store(h, n, s - 1)
                store(h, n, TILES - 2)
                store(h, n, TILES - 1)
            out_view = out.rearrange("b (t p) d -> p (b t) d", p=P)
            src = x_sb[:, :].rearrange("p (t d) -> p t d", d=D)
            for c in range(2 * B):
                t = c * NT // 2
                sp.wait_ge(s_out_r, t + NT // 2)
                sp.dma_start(out_view[:, t : t + NT // 2, :], src[:, t : t + NT // 2, :]).then_inc(s_out, 16)
            sp.wait_ge(s_out, 16 * 2 * B)

        @block2.gpsimd
        def _(pool):
            pool_steps = 0
            nc.gpsimd.iota(rank_i, pattern=[[-1, NE]], base=NE, channel_multiplier=0).then_inc(s_fconst, 1)
            nc.gpsimd.iota(tile_row_i, pattern=[[P, TILES]], base=0, channel_multiplier=0).then_inc(s_fconst, 1)
            nc.gpsimd.memset(zero_tile, 0.0).then_inc(s_fconst, 1)

            def layer_norm_root(k):
                pool.wait_ge(s_fvar, k)
                nc.gpsimd.tensor_tensor(f_rstd, f_tmp[:, 3, :], neg_half[:, :], ALU.pow).then_inc(s_frstd, 1)

            def rms_root(k):
                pool.wait_ge(s_ms, k)
                nc.gpsimd.tensor_tensor(rms[:, 1, :], rms[:, 0, :], neg_half[:, :], ALU.pow).then_inc(s_rms, 1)

            def scatter(k, h):
                pool.wait_ge(s_rows, k + 1)
                for c in range(2):
                    for j in range(NT):
                        nc.gpsimd.indirect_dma_start(
                            sorted_rows[h][:, :], bass.IndirectOffsetOnAxis(ap=rows_of[:, h, c, j : j + 1], axis=0),
                            z_rows[:, h * NT + j, :], None).then_inc(s_scat[h], 16)

            def gather(k, l, h):
                pool.wait_ge(s_sty[h], 16 * TILES * (l + 1))
                for j in range(NT):
                    use = k * NT + j
                    if use >= slots:
                        pool.wait_ge(s_z, B * NT + use - slots + 1)
                    for c in range(2):
                        nc.gpsimd.indirect_dma_start(
                            gathered[:, j % slots, c, :], None, expert_rows[h][:, :],
                            bass.IndirectOffsetOnAxis(ap=rows_of[:, h, c, j : j + 1], axis=0)).then_inc(s_gather[j % slots], 16)

            for h in range(B):
                layer_norm_root(h + 1)
                rms_root(h + 1)
                scatter(h, h)
            for h in range(B):
                gather(h, 0, h)
                rms_root(B + h + 1)
                scatter(B + h, h)
            for h in range(B):
                gather(B + h, 1, h)
                layer_norm_root(B + h + 1)

        @block2.scalar
        def _(act):
            def route(k, h):
                def square(j, first):
                    act.wait_ge(s_z, k * NT + j + 1)
                    if not first:
                        act.wait_ge(s_sq, k * NT + j)
                    nc.scalar.activation(squares, z_aug[:, zrow(h * NT + j)], ACT.Square,
                                         accum_out=sum_sq[:, bass.ds(j, 1)]).then_inc(s_sq, 1)

                square(0, k == 0)
                with act.Fori(1, NT) as j:
                    square(j, False)
                with act.Fori(0, PAIRS) as i:
                    act.wait_ge(s_tz, k * PAIRS + i + 1)
                    nc.scalar.activation(znT.rearrange("p u c t -> p (u c t)"), psum_z[:, :], ACT.Copy).then_inc(s_znT, 1)
                act.wait_ge(s_shift, k + 1)
                nc.scalar.activation(r_score, r_logit, ACT.Exp).then_inc(s_expl, 1)

            def experts(k):
                n = k * TILES

                def x_hi(s):
                    act.wait_ge(s_te, n + s + 1)
                    nc.scalar.activation(e_xT[:, 0, :, :].rearrange("p c t -> p (c t)"), psum_x, ACT.Copy).then_inc(s_ex_hi, 1)

                def h_hi(s):
                    act.wait_ge(s_th, n + s + 1)
                    nc.scalar.activation(hT[:, 0, :, :].rearrange("p c t -> p (c t)"), psum_h, ACT.Copy).then_inc(s_h_hi, 1)

                def silu(s, first):
                    act.wait_ge(s_a, n + s + 1)
                    if not first:
                        act.wait_ge(s_h, n + s)
                    nc.scalar.activation(silu_a, psum_a, ACT.Silu, scale=silu_scale[:, 0:1]).then_inc(s_silu, 1)

                def y_copy(s, first):
                    act.wait_ge(s_e, n + s + 1)
                    if not first:
                        act.wait_ge(s_sty[order[k][1]], 16 * (order[k][0] * TILES + s))
                    nc.scalar.activation(y_row, psum_e, ACT.Copy).then_inc(s_yrow, 1)

                x_hi(0)
                silu(0, k == 0)
                x_hi(1)
                if k:
                    act.wait_ge(s_sty[order[k - 1][1]], 16 * TILES * (order[k - 1][0] + 1))
                h_hi(0)
                silu(1, False)
                x_hi(2)
                y_copy(0, True)
                with act.Fori(2, TILES - 1) as s:
                    h_hi(s - 1)
                    silu(s, False)
                    x_hi(s + 1)
                    y_copy(s - 1, False)
                h_hi(TILES - 2)
                silu(TILES - 1, False)
                y_copy(TILES - 2, False)
                h_hi(TILES - 1)
                y_copy(TILES - 1, False)

            for l in range(LOOPS):
                for h in range(B):
                    route(l * B + h, h)
                for h in range(B):
                    experts(l * B + h)

        @block2.vector
        def _(dve):
            def link(ins):
                dve_steps[0] += 1
                ins.then_inc(s_dve, 1)
                dve.wait_ge(s_dve, dve_steps[0])

            def tok_exp(t):
                return t.rearrange("p (t e) -> p t e", e=NE)

            def per_tile(t):
                return t.unsqueeze(2).to_broadcast([P, NT, NE])

            def per_expert(t):
                return t.unsqueeze(1).to_broadcast([P, NT, NE])

            def norm_stats(k, at):
                with dve.Fori(0, NT) as j:
                    nc.vector.bn_stats(f_stats[:, bass.ds(j, 1), :].rearrange("p a k -> p (a k)"), at(j)).then_inc(s_dve, 1)
                dve_steps[0] += NT
                dve.wait_ge(s_dve, dve_steps[0])
                half_mean, half_m2 = (lambda q: f_stats[:, :, 3 * q + 1]), (lambda q: f_stats[:, :, 3 * q + 2])
                link(nc.vector.tensor_tensor(f_tmp[:, 0, :], half_mean(0), half_mean(1), ALU.subtract))
                link(nc.vector.tensor_tensor(f_tmp[:, 1, :], half_m2(0), half_m2(1), ALU.add))
                link(nc.vector.tensor_tensor(f_tmp[:, 2, :], f_tmp[:, 0, :], f_tmp[:, 0, :], ALU.mult))
                link(nc.vector.tensor_scalar(f_tmp[:, 1, :], f_tmp[:, 1, :], 1.0 / D, LN_EPS, ALU.mult, ALU.add))
                link(nc.vector.scalar_tensor_tensor(f_tmp[:, 3, :], f_tmp[:, 2, :], 0.25, f_tmp[:, 1, :], ALU.mult, ALU.add))
                link(nc.vector.tensor_tensor(f_mean, half_mean(0), half_mean(1), ALU.add))
                nc.vector.tensor_scalar(f_mean, f_mean, 0.5, None, ALU.mult).then_inc(s_fvar, 1)
                dve.wait_ge(s_frstd, k)

            def combine(k, h):
                with dve.Fori(0, NT // slots) as i:
                    for g in range(slots):
                        j = i * slots + g
                        dve.wait_ge(s_gather[g], 32 * (k * NT // slots + i + 1))
                        nc.vector.scalar_tensor_tensor(z_aug[:, zrow(h * NT + j)], gathered[:, g, 0, :],
                                                       gates[:, h, 0, bass.ds(j, 1)], z_aug[:, zrow(h * NT + j)],
                                                       ALU.mult, ALU.add).then_inc(s_half, 1)
                        dve.wait_ge(s_half, k * NT + j + 1)
                        nc.vector.scalar_tensor_tensor(z_aug[:, zrow(h * NT + j)], gathered[:, g, 1, :],
                                                       gates[:, h, 1, bass.ds(j, 1)], z_aug[:, zrow(h * NT + j)],
                                                       ALU.mult, ALU.add).then_inc(s_z, 1)

            def route(k, l, h):
                dve.wait_ge(s_sq, (k + 1) * NT)
                nc.vector.tensor_scalar(rms[:, 0, :], sum_sq, 1.0 / D, RMS_EPS, ALU.mult, ALU.add).then_inc(s_ms, 1)
                dve.wait_ge(s_rms, k + 1)
                if l:
                    dve.wait_ge(s_scat[h], 16 * 2 * NT * l)
                factor = z_rows[:, h * NT : (h + 1) * NT, D]
                link(nc.vector.tensor_scalar(factor, rms[:, 1, :], X_SCALE, None, ALU.mult))

                def zn_pair(i, first):
                    if not first:
                        dve.wait_ge(s_tz, k * PAIRS + i)
                    for u in range(2):
                        j = h * NT + 2 * i + u
                        nc.vector.tensor_scalar(zn[:, u, :], z_aug[:, zrow(j)], z_aug[:, zfac(j)], None,
                                                ALU.mult).then_inc(s_zn, 1)

                zn_pair(0, k == 0)
                with dve.Fori(1, PAIRS) as i:
                    zn_pair(i, False)
                dve.wait_ge(s_logit, (k + 1) * PAIRS)
                logit, score, rest, tmp = tok_exp(r_logit), tok_exp(r_score), tok_exp(r_rest), tok_exp(r_tmp)
                link(nc.vector.tensor_scalar(r_logit, psum_l[:, 0 : NT * NE], 1.0 / X_SCALE, None, ALU.mult))
                link(nc.vector.tensor_reduce(tiny[:, 0, :], logit, AX.X, ALU.max))
                nc.vector.tensor_tensor(logit, logit, per_tile(tiny[:, 0, :]), ALU.subtract).then_inc(s_shift, 1)
                dve.wait_ge(s_expl, k + 1)
                link(nc.vector.tensor_reduce(tiny[:, 1, :], score, AX.X, ALU.add))
                link(nc.vector.reciprocal(tiny[:, 2, :], tiny[:, 1, :]))
                link(nc.vector.tensor_tensor(score, score, per_tile(tiny[:, 2, :]), ALU.mult))
                src = score
                for c in range(2):
                    pick = tok_exp(r_pick[c])
                    link(nc.vector.tensor_reduce(best[:, c, :], src, AX.X, ALU.max))
                    link(nc.vector.tensor_tensor(tmp, src, per_tile(best[:, c, :]), ALU.is_ge))
                    link(nc.vector.tensor_tensor(tmp, tmp, per_expert(rank_down), ALU.mult))
                    link(nc.vector.tensor_reduce(tiny[:, 3, :], tmp, AX.X, ALU.max))
                    link(nc.vector.tensor_tensor(pick, per_expert(rank_down), per_tile(tiny[:, 3, :]), ALU.is_equal))
                    if c == 0:
                        link(nc.vector.scalar_tensor_tensor(rest, pick, -2.0, score, ALU.mult, ALU.add))
                        src = rest
                nc.vector.tensor_tensor(r_count, r_pick[0], r_pick[1], ALU.add).then_inc(s_pick, 1)
                link(nc.vector.tensor_tensor(tiny[:, 0, :], best[:, 0, :], best[:, 1, :], ALU.add))
                link(nc.vector.tensor_scalar(tiny[:, 0, :], tiny[:, 0, :], GATE_EPS, None, ALU.add))
                link(nc.vector.reciprocal(tiny[:, 1, :], tiny[:, 0, :]))
                for c in range(2):
                    link(nc.vector.tensor_tensor(tiny[:, 2, :], best[:, c, :], tiny[:, 1, :], ALU.mult))
                    link(nc.vector.tensor_scalar(gates[:, h, c, :], tiny[:, 2, :], y_unscale[:, 0:1], None, ALU.mult))
                dve.wait_ge(s_count, k + 1)
                link(nc.vector.tensor_copy(r_tmp, psum_r[:, NT * NE : 2 * NT * NE]))
                up_to = tok_exp(r_sum)
                for e in range(NE):
                    ins = nc.vector.tensor_tensor_scan(up_to[:, :, e], tmp[:, :, e], zero_tile, 0.0, ALU.add, ALU.add)
                link(ins)
                total, padded, upper, start = (start_f[:, q, :] for q in range(4))
                link(nc.vector.tensor_scalar(start_i, up_to[:, NT - 1, :], float(P - 1), None, ALU.add))
                link(nc.vector.tensor_scalar(start_i, start_i, -P, None, ALU.bitwise_and))
                link(nc.vector.tensor_copy(padded, start_i))
                link(nc.vector.tensor_tensor_scan(upper, padded, zero_tile[:, 0:NE], 0.0, ALU.add, ALU.add))
                link(nc.vector.tensor_tensor(start, upper, padded, ALU.subtract))
                link(nc.vector.tensor_tensor(r_sum, r_sum, r_tmp, ALU.subtract))
                link(nc.vector.tensor_tensor(r_sum, r_sum, psum_r[:, 0 : NT * NE], ALU.add))
                link(nc.vector.tensor_tensor(up_to, up_to, per_expert(start), ALU.add))
                for c in range(2):
                    link(nc.vector.tensor_tensor(r_tmp, r_pick[c], r_sum, ALU.mult))
                    link(nc.vector.tensor_reduce(rows_f[:, c, :], tmp, AX.X, ALU.add))
                nc.vector.tensor_copy(rows_of[:, h, :, :], rows_f).then_inc(s_rows, 1)
                shape = [P, TILES, NE]
                cmp = tile_cmp.rearrange("p (t e) -> p t e", e=NE)
                link(nc.vector.tensor_tensor(cmp, tile_row.unsqueeze(2).to_broadcast(shape),
                                             start.unsqueeze(1).to_broadcast(shape), ALU.is_ge))
                link(nc.vector.tensor_reduce(expert_f, cmp, AX.X, ALU.add))
                nc.vector.tensor_scalar(expert_of[:, h, :], expert_f, -1.0, None, ALU.add).then_inc(s_eid, 1)

            def experts(k):
                n = k * TILES

                def x_rows(s, first):
                    dve.wait_ge(s_ldx, 16 * (n + s + 1))
                    if not first:
                        dve.wait_ge(s_te, n + s)
                    nc.vector.tensor_scalar(x_row, x_tile[:, 0:D], x_tile[:, D : D + 1], None, ALU.mult).then_inc(s_xrow, 1)

                def x_lo(s):
                    dve.wait_ge(s_ex_hi, n + s + 1)
                    nc.vector.tensor_tensor(e_xT[:, 1, :, :].rearrange("p c t -> p (c t)"), psum_x,
                                            e_xT[:, 0, :, :].rearrange("p c t -> p (c t)"), ALU.subtract).then_inc(s_ex_lo, 1)

                def h_lo(s):
                    dve.wait_ge(s_h_hi, n + s + 1)
                    nc.vector.tensor_tensor(hT[:, 1, :, :].rearrange("p c t -> p (c t)"), psum_h,
                                            hT[:, 0, :, :].rearrange("p c t -> p (c t)"), ALU.subtract).then_inc(s_h_lo, 1)

                def gate(s, first):
                    dve.wait_ge(s_b, n + s + 1)
                    dve.wait_ge(s_silu, n + s + 1)
                    if not first:
                        dve.wait_ge(s_th, n + s)
                    nc.vector.scalar_tensor_tensor(h_row, psum_b, gate_scale[:, 0:1], silu_a, ALU.mult,
                                                   ALU.mult).then_inc(s_h, 1)

                x_rows(0, k == 0)
                x_lo(0)
                x_rows(1, False)
                gate(0, k == 0)
                x_lo(1)

                def tile(s, more):
                    if more:
                        x_rows(s + 1, False)
                    h_lo(s - 1)
                    gate(s, False)
                    if more:
                        x_lo(s + 1)

                with dve.Fori(1, TILES - 1) as s:
                    tile(s, True)
                tile(TILES - 1, False)
                h_lo(TILES - 1)

            dve.wait_ge(s_fconst, 3)
            link(nc.vector.tensor_copy(rank_down, rank_i))
            link(nc.vector.tensor_copy(tile_row, tile_row_i))
            for h in range(B):
                norm_stats(h + 1, lambda j: x_sb[:, tile_of(h * NT + j)])
                with dve.Fori(0, NT) as j:
                    nc.vector.tensor_scalar(z_aug[:, zrow(h * NT + j)], x_sb[:, tile_of(h * NT + j)],
                                            f_mean[:, bass.ds(j, 1)], f_rstd[:, bass.ds(j, 1)], ALU.subtract,
                                            ALU.mult).then_inc(s_z, 1)
                if h == 0:
                    link(nc.vector.memset(z_rows[:, :, D:ZW], 0.0))
                route(h, 0, h)
            for h in range(B):
                experts(h)
            for h in range(B):
                combine(h, h)
                route(B + h, 1, h)
            for h in range(B):
                experts(B + h)
            for h in range(B):
                combine(B + h, h)
                dve.wait_ge(s_z, (2 * B + h + 1) * NT)
                norm_stats(B + h + 1, lambda j: z_aug[:, zrow(h * NT + j)])
                with dve.Fori(0, NT) as j:
                    nc.vector.tensor_scalar(z_aug[:, zrow(h * NT + j)], z_aug[:, zrow(h * NT + j)],
                                            f_mean[:, bass.ds(j, 1)], f_rstd[:, bass.ds(j, 1)], ALU.subtract,
                                            ALU.mult).then_inc(s_out_t, 1)
                    dve.wait_ge(s_out_t, h * NT + j + 1)
                    nc.vector.tensor_tensor(x_sb[:, tile_of(h * NT + j)], x_sb[:, tile_of(h * NT + j)],
                                            z_aug[:, zrow(h * NT + j)], ALU.add).then_inc(s_out_r, 1)

        @block2.tensor
        def _(pe):
            def route(k, h):
                def turn(i, first):
                    if not first:
                        pe.wait_ge(s_znT, k * PAIRS + i)
                    for u in range(2):
                        pe.wait_ge(s_zn, k * NT + 2 * i + u + 1)
                        for c in range(DC):
                            last = nc.tensor.transpose(psum_z[:, (u * DC + c) * P : (u * DC + c + 1) * P],
                                                       zn[:, u, c * P : (c + 1) * P], ident[:, :])
                    last.then_inc(s_tz, 1)

                def logits(i):
                    pe.wait_ge(s_znT, k * PAIRS + i + 1)
                    for u in range(2):
                        for c in range(DC):
                            last = nc.tensor.matmul(psum_l[:, bass.ds((2 * i + u) * NE, NE)], znT[:, u, c, :],
                                                    router_c[:, c, :], start=(c == 0), stop=(c == DC - 1))
                    last.then_inc(s_logit, 1)

                if k:
                    pe.wait_ge(s_pick, k)
                turn(0, k == 0)
                logits(0)
                with pe.Fori(1, PAIRS) as i:
                    turn(i, False)
                    logits(i)
                pe.wait_ge(s_pick, k + 1)
                if k:
                    pe.wait_ge(s_rows, k)
                nc.tensor.matmul(psum_r[:, 0 : NT * NE], before[:, :], r_count, start=True, stop=True)
                nc.tensor.matmul(psum_r[:, NT * NE : 2 * NT * NE], ones[:, :], r_count, start=True, stop=True).then_inc(s_count, 1)

            def experts(k, h):
                n = k * TILES

                def turn_x(s):
                    pe.wait_ge(s_xrow, n + s + 1)
                    if not (isinstance(s, int) and n + s == 0):
                        pe.wait_ge(s_ex_lo, n + s)
                    for c in range(DC):
                        last = nc.tensor.transpose(psum_x[:, c * P : (c + 1) * P], x_row[:, c * P : (c + 1) * P], ident[:, :])
                    last.then_inc(s_te, 1)

                def inner(s, first):
                    e = pe.value_load(expert_of[0:1, h, bass.ds(s, 1)], min_val=0, max_val=NE - 1)
                    pe.wait_ge(s_ex_lo, n + s + 1)
                    if not first:
                        pe.wait_ge(s_h, n + s)
                    for m, (bank, signal) in enumerate(((psum_a, s_a), (psum_b, s_b))):
                        for q, (c, lx, lw) in enumerate([(c, a, w) for c in range(DC) for a, w in ((0, 0), (0, 1), (1, 0))]):
                            at = ((m * DC + c) * 2 + lw) * GROUP
                            last = nc.tensor.matmul(bank, e_xT[:, lx, c, :], w_split[:, bass.ds(e * EW + at, FF)],
                                                    start=(q == 0), stop=(q == 3 * DC - 1))
                        last.then_inc(signal, 1)
                    return e

                def turn_h(s, first):
                    pe.wait_ge(s_h, n + s + 1)
                    if not first:
                        pe.wait_ge(s_h_lo, n + s)
                    for c in range(FC):
                        last = nc.tensor.transpose(psum_h[:, c * P : (c + 1) * P], h_row[:, c * P : (c + 1) * P], ident[:, :])
                    last.then_inc(s_th, 1)

                def outer(s, first):
                    e = pe.value_load(expert_of[0:1, h, bass.ds(s, 1)], min_val=0, max_val=NE - 1)
                    pe.wait_ge(s_h_lo, n + s + 1)
                    if not first:
                        pe.wait_ge(s_yrow, n + s)
                    for q, (c, lh, lw) in enumerate([(c, a, w) for c in range(FC) for a, w in ((0, 0), (0, 1), (1, 0))]):
                        per = GROUP // D
                        at = ((2 * DC + c // per) * 2 + lw) * GROUP + c % per * D
                        last = nc.tensor.matmul(psum_e, hT[:, lh, c, :], w_split[:, bass.ds(e * EW + at, D)],
                                                start=(q == 0), stop=(q == 3 * FC - 1))
                    last.then_inc(s_e, 1)

                pe.wait_ge(s_eid, k + 1)
                turn_x(0)
                inner(0, k == 0)
                turn_x(1)

                def tile(s, more):
                    turn_h(s - 1, isinstance(s, int) and n + s == 1)
                    inner(s, False)
                    if more:
                        turn_x(s + 1)
                    outer(s - 1, isinstance(s, int) and n + s == 1)

                tile(1, True)
                with pe.Fori(2, TILES - 1) as s:
                    tile(s, True)
                tile(TILES - 1, False)
                turn_h(TILES - 1, False)
                outer(TILES - 1, False)

            for l in range(LOOPS):
                for h in range(B):
                    route(l * B + h, h)
                for h in range(B):
                    experts(l * B + h, h)


_INS = ["L0_attn_x", "L0_attn_wq", "L0_attn_wk", "L0_attn_wv", "L0_attn_wo", "L0_ffn_norm_w", "L0_ffn_router_w",
        "L0_ffn_w1", "L0_ffn_w3", "L0_ffn_w2"]


def kernel(**inputs):
    import concourse.bacc as _bacc
    from concourse.bass_utils import run_bass_kernel_spmd as _run

    nc = _bacc.Bacc("TRN2", target_bir_lowering=False, num_devices=1)
    arrays, args = {}, []
    named = [(name, np.ascontiguousarray(inputs[name])) for name in _INS] + [("rope", rope_table())]
    for name, a in named:
        arrays[f"in_{name}"] = a
        args.append(nc.dram_tensor(f"in_{name}", a.shape, mybir.dt.from_np(a.dtype), kind="ExternalInput").ap())
    args.append(nc.dram_tensor("out_0", (B, S, D), F32, kind="ExternalOutput").ap())
    args.append([nc.dram_tensor(f"sorted_rows{h}", (ROWS, ZW), F32, kind="Internal").ap() for h in range(B)])
    args.append([nc.dram_tensor(f"expert_rows{h}", (ROWS, D), F32, kind="Internal").ap() for h in range(B)])
    sandwich_kernel(nc, *args)
    r = _run(nc, [arrays], core_ids=[0])
    return r.results[0]["out_0"]
```

```python
from contextlib import ExitStack

import concourse.bass as bass
import numpy as np
from concourse import mybir

ALU = mybir.AluOpType
ACT = mybir.ActivationFunctionType
AX = mybir.AxisListType
F32 = mybir.dt.float32
F16 = mybir.dt.float16
I32 = mybir.dt.int32
U32 = mybir.dt.uint32
ABSMAX = bass.bass_isa.ReduceOp.absmax

P = 128
B, S, D, HD = 2, 2048, 256, 128
NE, FF, LOOPS = 8, 512, 2
DC, FC = D // P, FF // P
NT = S // P
PAIRS = NT // 2
KB = S // 512
TILES = 2 * S // P + NE - 1
ROWS = TILES * P
UNROLL = 3
ZW = D + 4
GROUP = 512
NG = (2 * DC * FF + FC * D) // GROUP
EW = NG * 2 * GROUP

LN_EPS, RMS_EPS, GATE_EPS = 1e-5, 1e-6, 1e-9
W_EXP = 9
X_SCALE = 2.0**11
QKV_SCALE = 2.0**-15
P_SCALE = 2.0**14
ARENA = 19700
EXP_BITS = 0x7F800000
ROPE_BASE = 10000.0


def rope_table():
    inv = np.float32(1.0) / np.float32(ROPE_BASE) ** (np.arange(0, HD, 2, dtype=np.float32) / np.float32(HD))
    ang = np.arange(S - 1, dtype=np.float32)[:, None] * inv[None, :]
    cos = np.concatenate([np.ones((1, HD // 2), np.float32), np.cos(ang)])
    sin = np.concatenate([np.zeros((1, HD // 2), np.float32), np.sin(ang)])
    return (np.stack([cos, sin, cos], axis=1) * np.float32(QKV_SCALE)).astype(np.float32)


def sandwich_kernel(nc, x, wq, wk, wv, wo, norm_w, router_w, w1, w3, w2, rope, out, sorted_rows, expert_rows):
    with ExitStack() as ctx:

        def sb(name, shape, dt=F32):
            return ctx.enter_context(nc.sbuf_tensor(name, shape, dt))

        def sem(name):
            return ctx.enter_context(nc.semaphore(name))

        w_raw = sb("w_raw", [P, NE * NG * GROUP])
        w_split = w_raw[:, :].bitcast(F16)
        x_sb = sb("x_sb", [P, B * NT * D])
        ident = sb("ident", [P, P])
        before = sb("before", [P, P])
        ones = sb("ones", [P, P])
        neg_half = sb("neg_half", [P, NT])
        norm_c = sb("norm_c", [P, DC])
        router_c = sb("router_c", [P, DC, NE])
        amax_a = sb("amax_a", [P, 4])
        pow_a = sb("pow_a", [P, 4])
        scale_a = sb("scale_a", [P, 4])
        amax_g = sb("amax_g", [P, NE, NG])
        amax_f = sb("amax_f", [P, 8])
        pow_f = sb("pow_f", [P, 3])
        scale_f = sb("scale_f", [P, 3])
        scale_wn = sb("scale_wn", [P, 2 * DC])
        alpha = sb("alpha", [P, 1])
        neg_alpha = sb("neg_alpha", [P, 1])
        attn_eps = sb("attn_eps", [P, 1])
        silu_scale = sb("silu_scale", [P, 1])
        gate_scale = sb("gate_scale", [P, 1])
        y_unscale = sb("y_unscale", [P, 1])

        arena = sb("arena", [P, ARENA])
        used = [0]

        def take(words):
            a = arena[:, used[0] : used[0] + words]
            used[0] += words
            assert used[0] <= ARENA, used[0]
            return a

        qkT = take(2 * 2 * S // 2).bitcast(F16).rearrange("p (l m s) -> p l m s", l=2, m=2)
        v_sb = take(NT * 2 * HD // 2).bitcast(F16)
        v_tiles = v_sb.rearrange("p (t l h) -> p t l h", t=NT, l=2)
        probs = take(S)
        pT = take(2 * S // 2).bitcast(F16).rearrange("p (l s) -> p l s", l=2)
        tab = take(NT * 3 * HD // 2)
        rot = take(2 * 2 * 2 * HD).rearrange("p (u m n) -> p u m n", u=2, m=2)
        qk_tok = take(2 * 2 * HD).rearrange("p (u n) -> p u n", u=2)
        xn = take(2 * D).rearrange("p (u d) -> p u d", u=2)
        xT = take(2 * 2 * D // 2).bitcast(F16).rearrange("p (l u c t) -> p l u c t", l=2, u=2, c=DC)
        o_tok = take(HD)
        o_part = take(HD)
        oT = take(2 * P // 2).bitcast(F16).rearrange("p (l t) -> p l t", l=2)
        y_norm = take(D)
        w_tmp = take(2 * GROUP).rearrange("p (u n) -> p u n", u=2)
        zeros = take(3 * ZW)
        attn_raw = probs[:, 0 : 4 * D].rearrange("p (m n) -> p m n", m=4)
        wqkvT = take(DC * 2 * 3 * HD // 2).bitcast(F16).rearrange("p (c l n) -> p c l n", c=DC, l=2)
        woT = take(2 * D // 2).bitcast(F16).rearrange("p (l n) -> p l n", l=2)
        stats = take(NT * 6).rearrange("p (t k) -> p t k", t=NT)
        mean_x = take(NT)
        rstd_x = take(NT)
        tmp_x = take(4 * NT).rearrange("p (k t) -> p k t", k=4)
        row_max = take(2)
        neg_max = take(1)
        row_sum = take(2)
        row_rec = take(1)
        y_stats = take(6)
        y_mv = take(2)
        y_var = take(1)
        y_negmean = take(1)
        y_rstd = take(1)
        y_shift = take(1)

        psum_s = ctx.enter_context(nc.psum_tensor("psum_s", [P, S], F32))
        psum_t = [ctx.enter_context(nc.psum_tensor(f"psum_t{i}", [P, 512], F32)) for i in range(2)]
        psum_o = ctx.enter_context(nc.psum_tensor("psum_o", [P, 512], F32))
        psum_y = ctx.enter_context(nc.psum_tensor("psum_y", [P, 512], F32))

        s_x = [sem(f"x_loaded{i}") for i in range(4)]
        s_attn_w = sem("attn_weights_loaded")
        s_small = sem("small_inputs_loaded")
        s_tab = sem("rope_loaded")
        s_raw = [sem(f"expert_loaded{e}") for e in range(NE)]
        s_zero_fill = sem("sorted_rows_zeroed")
        s_const = sem("constants_ready")
        s_amax_a = sem("attn_amax_parts")
        s_all_a = sem("attn_amax_ready")
        s_scale_a = sem("attn_scales_ready")
        s_wt = sem("attn_weights_turned")
        s_wt_hi = sem("attn_weights_hi")
        s_wt_lo = sem("attn_weights_lo")
        s_amax_f = sem("expert_amax_parts")
        s_all_f = sem("expert_amax_ready")
        s_scale_f = sem("expert_scales_ready")
        s_wsplit = sem("expert_weights_steps")
        s_dve = sem("vector_steps")
        s_var_x = sem("ln_variance_ready")
        s_rstd_x = sem("ln_rstd_ready")
        s_xn = sem("xn_ready")
        s_tx = sem("xn_turned")
        s_xt_hi = sem("xT_hi")
        s_xt_lo = sem("xT_lo")
        s_qkv = sem("qkv_ready")
        s_v_hi = sem("v_hi")
        s_rot = sem("qkv_bank_read")
        s_qk = sem("qk_rotated")
        s_tqk = sem("qk_turned")
        s_qk_hi = sem("qkT_hi")
        s_qk_lo = sem("qkT_lo")
        s_scores = sem("scores_ready")
        s_max = sem("row_max_parts")
        s_negmax = sem("neg_max_ready")
        s_exp = sem("probs_ready")
        s_tp = sem("probs_turned")
        s_p_hi = sem("pT_hi")
        s_p_lo = sem("pT_lo")
        s_pv = sem("weighted_values_ready")
        s_sum = sem("row_sum_ready")
        s_rec = sem("row_rec_ready")
        s_o_part = sem("o_part_ready")
        s_o = sem("o_ready")
        s_to = sem("o_turned")
        s_o_hi = sem("oT_hi")
        s_o_lo = sem("oT_lo")
        s_proj = sem("projection_ready")
        s_ystat = sem("y_stats_ready")
        s_ymv = sem("y_mean_var_ready")
        s_held = sem("waits_held")
        s_yvar = sem("y_var_ready")
        s_yrstd = sem("y_rstd_ready")
        s_yshift = sem("y_shift_ready")
        s_ynorm = sem("y_norm_ready")
        s_x1 = sem("x1_ready")

        dve_steps = [0]

        def tile_of(j):
            return bass.ds(j * D, D)

        block_stack = ctx.enter_context(ExitStack())
        block = block_stack.enter_context(nc.Block())


        @block.sync
        def _(sp):
            x_view = x.rearrange("b (t p) d -> p (b t) d", p=P)
            x_dst = x_sb[:, :].rearrange("p (t d) -> p t d", d=D)
            q = B * NT // 4
            sp.dma_start(x_dst[:, 0:q, :], x_view[:, 0:q, :]).then_inc(s_x[0], 16)
            for m, w in enumerate((wq, wk, wv)):
                sp.dma_start(attn_raw[:, m, :], w).then_inc(s_attn_w, 16)
            sp.dma_start(attn_raw[:, 3, :].rearrange("p (c h) -> p c h", c=DC),
                         wo.rearrange("(c p) h -> p c h", p=P)).then_inc(s_attn_w, 16)
            for c in range(1, 4):
                sp.dma_start(x_dst[:, c * q : (c + 1) * q, :], x_view[:, c * q : (c + 1) * q, :]).then_inc(s_x[c], 16)
                if c == 1:
                    sp.dma_start(tab.rearrange("p (t k) -> p t k", t=NT),
                                 rope.rearrange("(t p) c k -> p t (c k)", p=P)).then_inc(s_tab, 16)
                    with nc.allow_non_contiguous_dma(reason="256 values"):
                        sp.dma_start(norm_c[:, :], norm_w.rearrange("(c p) -> p c", p=P)).then_inc(s_small, 16)
                    sp.dma_start(router_c[:, :, :], router_w.rearrange("(c p) e -> p c e", p=P)).then_inc(s_small, 16)
            for e in range(NE):
                at = e * NG * GROUP
                for w, chunks, width in ((w1, DC, FF), (w3, DC, FF), (w2, FC, D)):
                    n = chunks * width
                    sp.dma_start(w_raw[:, at : at + n].rearrange("p (c f) -> p c f", c=chunks),
                                 w[e].rearrange("(c p) f -> p c f", p=P)).then_inc(s_raw[e], 16)
                    at += n
            sp.wait_ge(s_const, 3)
            for h in range(B):
                for t in range(0, TILES, 3):
                    sp.dma_start(sorted_rows[h][t * P : (t + 3) * P, :].rearrange("(t p) d -> p t d", p=P),
                                 zeros.rearrange("p (t d) -> p t d", t=3)).then_inc(s_zero_fill, 16)
            sp.wait_ge(s_zero_fill, 16 * B * (TILES // 3))

        @block.gpsimd
        def _(pool):
            nc.gpsimd.memset(ident[:, :], 0.0).then_inc(s_const, 1)
            nc.gpsimd.memset(ones[:, :], 1.0).then_inc(s_const, 1)
            nc.gpsimd.memset(zeros, 0.0).then_inc(s_const, 1)
            nc.gpsimd.memset(neg_half[:, :], -0.5).then_inc(s_const, 1)
            pool.wait_ge(s_const, 4)
            nc.gpsimd.affine_select(out=ident[:, :], in_=ident[:, :], compare_op=ALU.not_equal, fill=1.0,
                                    base=0, pattern=[[-1, P]], channel_multiplier=1).then_inc(s_const, 1)
            nc.gpsimd.affine_select(out=before[:, :], in_=ones[:, :], compare_op=ALU.is_gt, fill=0.0,
                                    base=0, pattern=[[1, P]], channel_multiplier=-1).then_inc(s_const, 1)
            pool.wait_ge(s_const, 6)
            pool.wait_ge(s_amax_a, 1)
            nc.gpsimd.partition_all_reduce(amax_a[:, :], amax_a[:, :], P, ABSMAX).then_inc(s_all_a, 1)
            pool.wait_ge(s_amax_f, 1)
            nc.gpsimd.partition_all_reduce(amax_f[:, 0:3], amax_f[:, 0:3], P, ABSMAX).then_inc(s_all_f, 1)

            def split_group(e, g):
                n = NG * e + g
                raw = w_raw[:, n * GROUP : (n + 1) * GROUP]
                both = w_split[:, 2 * n * GROUP : 2 * (n + 1) * GROUP]
                by = scale_wn[:, g : g + 1] if g < 2 * DC else scale_f[:, 2:3]
                tmp = w_tmp[:, n % 2, :]
                if g == 0:
                    pool.wait_ge(s_raw[e], 48)
                nc.gpsimd.tensor_scalar(tmp, raw, by, 1.0, ALU.mult, ALU.mult).then_inc(s_wsplit, 1)
                pool.wait_ge(s_wsplit, 3 * n + 1)
                nc.gpsimd.tensor_scalar(both[:, 0:GROUP], tmp, 1.0, 1.0, ALU.mult, ALU.mult).then_inc(s_wsplit, 1)
                pool.wait_ge(s_wsplit, 3 * n + 2)
                nc.gpsimd.tensor_tensor(both[:, GROUP:], tmp, both[:, 0:GROUP], ALU.subtract).then_inc(s_wsplit, 1)
                pool.wait_ge(s_wsplit, 3 * n + 3)

            groups = [(e, g) for e in range(NE) for g in range(NG)]

            def rotate(n):
                for u in range(2):
                    pool.wait_ge(s_rot, 2 * n + u + 1)
                    if not (isinstance(n, int) and n == 0):
                        pool.wait_ge(s_tqk, n)
                    c = rot[:, u, 0, :].rearrange("p (m c k) -> p m c k", m=2, c=2)
                    s = rot[:, u, 1, :].rearrange("p (m c k) -> p m c k", m=2, c=2)
                    o = qk_tok[:, u, :].rearrange("p (m c k) -> p m c k", m=2, c=2)
                    nc.gpsimd.tensor_tensor(o[:, :, 0, :], c[:, :, 0, :], s[:, :, 0, :], ALU.subtract)
                    nc.gpsimd.tensor_tensor(o[:, :, 1, :], c[:, :, 1, :], s[:, :, 1, :], ALU.add).then_inc(s_qk, 1)

            def normalise(t):
                pool.wait_ge(s_yvar, t + 1)
                nc.gpsimd.tensor_tensor(y_rstd, y_var, neg_half[:, 0:1], ALU.pow).then_inc(s_yrstd, 1)
                pool.wait_ge(s_yrstd, t + 1)
                nc.gpsimd.tensor_tensor(y_shift, y_negmean, y_rstd, ALU.mult).then_inc(s_yshift, 1)
                pool.wait_ge(s_ynorm, t + 1)
                nc.gpsimd.tensor_tensor(x_sb[:, tile_of(t)], x_sb[:, tile_of(t)], y_norm, ALU.add).then_inc(s_x1, 1)

            pool.wait_ge(s_scale_f, 1)
            for b in range(B):
                pool.wait_ge(s_var_x, b + 1)
                nc.gpsimd.tensor_tensor(rstd_x, tmp_x[:, 3, :], neg_half[:, :], ALU.pow).then_inc(s_rstd_x, 1)
                n0 = b * PAIRS
                rotate(n0)
                with pool.Fori(1, PAIRS) as i:
                    rotate(n0 + i)
                if b == 0:
                    for e, g in groups:
                        split_group(e, g)
                t0 = b * NT
                with pool.Fori(0, NT) as i:
                    normalise(t0 + i)

        @block.scalar
        def _(act):
            act.wait_ge(s_scale_a, 1)
            act.wait_ge(s_wt, 2)
            for m in range(3):
                src = psum_t[m // 2][:, (m % 2) * D : (m % 2 + 1) * D].rearrange("p (c n) -> p c n", c=DC)
                nc.scalar.activation(wqkvT[:, :, 0, m * HD : (m + 1) * HD], src, ACT.Copy,
                                     scale=scale_a[:, m : m + 1]).then_inc(s_wt_hi, 1)
            nc.scalar.activation(woT[:, 0, :], psum_t[1][:, D : 2 * D], ACT.Copy,
                                 scale=scale_a[:, 3:4]).then_inc(s_wt_hi, 1)

            def x_hi(n):
                act.wait_ge(s_tx, n + 1)
                nc.scalar.activation(xT[:, 0, :, :, :].rearrange("p u c t -> p (u c t)"), psum_t[0][:, :],
                                     ACT.Copy).then_inc(s_xt_hi, 1)

            def v_hi(n, i):
                for u in range(2):
                    act.wait_ge(s_qkv, 2 * n + u + 1)
                    nc.scalar.activation(v_sb[:, bass.ds((2 * i + u) * 2 * HD, HD)],
                                         psum_s[:, u * 512 + 2 * HD : u * 512 + 3 * HD], ACT.Copy,
                                         scale=QKV_SCALE).then_inc(s_v_hi, 1)

            def qk_hi(n, i):
                act.wait_ge(s_tqk, n + 1)
                nc.scalar.activation(qkT[:, 0, :, bass.ds(i * 2 * P, 2 * P)],
                                     psum_t[1][:, :].rearrange("p (m t) -> p m t", m=2), ACT.Copy).then_inc(s_qk_hi, 1)

            def p_hi(t, g):
                act.wait_ge(s_tp, 4 * t + g + 1)
                nc.scalar.activation(pT[:, 0, g * 512 : (g + 1) * 512], psum_t[g % 2][:, :], ACT.Copy,
                                     scale=P_SCALE).then_inc(s_p_hi, 1)

            def step(t, new, turn, fin):
                if turn:
                    p_hi(t - 1, 0)
                    p_hi(t - 1, 1)
                if fin:
                    act.wait_ge(s_to, t - 1)
                    nc.scalar.activation(oT[:, 0, :], psum_y[:, 0:P], ACT.Copy).then_inc(s_o_hi, 1)
                if turn:
                    p_hi(t - 1, 2)
                    p_hi(t - 1, 3)
                if new:
                    act.wait_ge(s_negmax, t + 1)
                    for h in range(2):
                        if turn:
                            act.wait_ge(s_tp, 4 * (t - 1) + 2 * h + 2)
                        nc.scalar.activation(probs[:, h * S // 2 : (h + 1) * S // 2],
                                             psum_s[:, h * S // 2 : (h + 1) * S // 2], ACT.Exp, bias=neg_max,
                                             scale=alpha[:, 0:1], accum_out=row_sum[:, h : h + 1]).then_inc(s_exp, 1)
                if fin:
                    act.wait_ge(s_yshift, t - 1)
                    nc.scalar.activation(y_norm, psum_y[:, D : 2 * D], ACT.Identity, bias=y_shift,
                                         scale=y_rstd).then_inc(s_ynorm, 1)
                if turn:
                    act.wait_ge(s_pv, t)
                    act.wait_ge(s_rec, t)
                    nc.scalar.activation(o_part, psum_o[:, HD : 2 * HD], ACT.Copy, scale=row_rec).then_inc(s_o_part, 1)

            for b in range(B):
                n0 = b * PAIRS
                x_hi(n0)
                with act.Fori(0, PAIRS - 1) as i:
                    v_hi(n0 + i, i)
                    x_hi(n0 + i + 1)
                    qk_hi(n0 + i, i)
                v_hi(n0 + PAIRS - 1, PAIRS - 1)
                qk_hi(n0 + PAIRS - 1, PAIRS - 1)
                t0 = b * NT
                step(t0, True, False, False)
                step(t0 + 1, True, True, False)
                with act.Fori(2, NT) as i:
                    step(t0 + i, True, True, True)
                step(t0 + NT, False, True, True)
                step(t0 + NT + 1, False, False, True)

        @block.vector
        def _(dve):
            def link(ins):
                dve_steps[0] += 1
                ins.then_inc(s_dve, 1)
                dve.wait_ge(s_dve, dve_steps[0])

            def powers(amax, pow2, scale, signal):
                link(nc.vector.tensor_scalar(amax, amax, 2.0**-60, None, ALU.max))
                link(nc.vector.tensor_scalar(pow2.bitcast(I32), amax.bitcast(I32), EXP_BITS, None, ALU.bitwise_and))
                link(nc.vector.tensor_scalar(scale.bitcast(I32), pow2.bitcast(I32), -1.0,
                                             float((W_EXP + 2 * 127) << 23), ALU.mult, ALU.add))

            dve.wait_ge(s_attn_w, 64)
            nc.vector.tensor_reduce(amax_a[:, :], attn_raw, AX.X, ALU.max, apply_absolute_value=True).then_inc(s_amax_a, 1)
            dve.wait_ge(s_all_a, 1)
            powers(amax_a[:, :], pow_a[:, :], scale_a[:, :], None)
            link(nc.vector.tensor_tensor(alpha[:, :], pow_a[:, 0:1], pow_a[:, 1:2], ALU.mult))
            link(nc.vector.tensor_scalar(alpha[:, :], alpha[:, :], 2.0 ** (-2 * (W_EXP - 4)) / float(np.sqrt(HD)), None, ALU.mult))
            link(nc.vector.tensor_scalar(neg_alpha[:, :], alpha[:, :], -1.0, None, ALU.mult))
            link(nc.vector.tensor_tensor(attn_eps[:, :], scale_a[:, 2:3], scale_a[:, 3:4], ALU.mult))
            link(nc.vector.tensor_scalar(attn_eps[:, :], attn_eps[:, :], X_SCALE * QKV_SCALE, None, ALU.mult))
            link(nc.vector.tensor_tensor(attn_eps[:, :], attn_eps[:, :], attn_eps[:, :], ALU.mult))
            nc.vector.tensor_scalar(attn_eps[:, :], attn_eps[:, :], LN_EPS, None, ALU.mult).then_inc(s_scale_a, 1)
            dve.wait_ge(s_wt_hi, 4)
            for m in range(3):
                src = psum_t[m // 2][:, (m % 2) * D : (m % 2 + 1) * D].rearrange("p (c n) -> p c n", c=DC)
                at = slice(m * HD, (m + 1) * HD)
                nc.vector.scalar_tensor_tensor(wqkvT[:, :, 1, at], src, scale_a[:, m : m + 1], wqkvT[:, :, 0, at],
                                               ALU.mult, ALU.subtract).then_inc(s_wt_lo, 1)
            nc.vector.scalar_tensor_tensor(woT[:, 1, :], psum_t[1][:, D : 2 * D], scale_a[:, 3:4], woT[:, 0, :],
                                           ALU.mult, ALU.subtract).then_inc(s_wt_lo, 1)

            for e in range(NE):
                dve.wait_ge(s_raw[e], 48)
                src = w_raw[:, e * NG * GROUP : (e + 1) * NG * GROUP].rearrange("p (g n) -> p g n", g=NG)
                link(nc.vector.tensor_reduce(amax_g[:, e, :], src, AX.X, ALU.max, apply_absolute_value=True))
            dve.wait_ge(s_small, 32)
            link(nc.vector.tensor_reduce(amax_f[:, 0:NG], amax_g[:, :, :].rearrange("p e g -> p g e"), AX.X, ALU.max))
            for m in range(2):
                link(nc.vector.tensor_tensor(amax_f[:, m * DC : (m + 1) * DC], amax_f[:, m * DC : (m + 1) * DC],
                                             norm_c[:, :], ALU.mult))
            for m in range(3):
                link(nc.vector.tensor_reduce(amax_f[:, m : m + 1], amax_f[:, m * DC : (m + 1) * DC], AX.X, ALU.max,
                                             apply_absolute_value=True))
            nc.vector.tensor_scalar(amax_f[:, 6:7], amax_f[:, 0:1], 1.0, None, ALU.mult).then_inc(s_amax_f, 1)
            dve.wait_ge(s_all_f, 1)
            powers(amax_f[:, 0:3], pow_f[:, :], scale_f[:, :], None)
            for m in range(2):
                link(nc.vector.tensor_scalar(scale_wn[:, m * DC : (m + 1) * DC], norm_c[:, :], scale_f[:, m : m + 1],
                                             None, ALU.mult))
            link(nc.vector.tensor_scalar(silu_scale[:, :], pow_f[:, 0:1], 2.0**-W_EXP / X_SCALE, None, ALU.mult))
            link(nc.vector.tensor_scalar(gate_scale[:, :], scale_f[:, 0:1], 2.0**-21 / X_SCALE, None, ALU.mult))
            link(nc.vector.tensor_tensor(y_unscale[:, :], pow_f[:, 0:1], pow_f[:, 1:2], ALU.mult))
            link(nc.vector.tensor_tensor(y_unscale[:, :], y_unscale[:, :], pow_f[:, 2:3], ALU.mult))
            link(nc.vector.tensor_scalar(y_unscale[:, :], y_unscale[:, :], 2.0 ** (21 - 3 * W_EXP), None, ALU.mult))
            for c in range(DC):
                link(nc.vector.tensor_scalar(router_c[:, c, :], router_c[:, c, :], norm_c[:, c : c + 1], None, ALU.mult))
            nc.vector.tensor_scalar(amax_f[:, 7:8], amax_f[:, 0:1], 1.0, None, ALU.mult).then_inc(s_scale_f, 1)

            def x_norm(n, i):
                for u in range(2):
                    if not (isinstance(n, int) and n == 0):
                        dve.wait_ge(s_tx, n)
                    nc.vector.tensor_scalar(xn[:, u, :], x_sb[:, tile_of(2 * n + u)], mean_x[:, bass.ds(2 * i + u, 1)],
                                            rstd_x[:, bass.ds(2 * i + u, 1)], ALU.subtract, ALU.mult).then_inc(s_xn, 1)

            def x_lo(n):
                dve.wait_ge(s_xt_hi, n + 1)
                nc.vector.tensor_tensor(xT[:, 1, :, :, :].rearrange("p u c t -> p (u c t)"), psum_t[0][:, :],
                                        xT[:, 0, :, :, :].rearrange("p u c t -> p (u c t)"), ALU.subtract).then_inc(s_xt_lo, 1)

            def v_and_rotation(n, i):
                for u in range(2):
                    dve.wait_ge(s_v_hi, 2 * n + u + 1)
                    at = bass.ds((2 * i + u) * 2 * HD, HD)
                    lo = bass.ds((2 * i + u) * 2 * HD + HD, HD)
                    bank = psum_s[:, u * 512 : u * 512 + 3 * HD]
                    nc.vector.scalar_tensor_tensor(v_sb[:, lo], bank[:, 2 * HD :], QKV_SCALE, v_sb[:, at],
                                                   ALU.mult, ALU.subtract)
                    if not (isinstance(n, int) and n == 0):
                        dve.wait_ge(s_qk, 2 * n + u - 1)
                    pairs = bank[:, 0 : 2 * HD].rearrange("p (m k two) -> p m k two", m=2, two=2)
                    t = tab[:, bass.ds((2 * i + u) * 3 * HD // 2, 3 * HD // 2)].rearrange("p (c k) -> p c k", c=3)
                    shape = [P, 2, 2, HD // 2]
                    for odd in range(2):
                        ins = nc.vector.tensor_tensor(
                            rot[:, u, odd, :].rearrange("p (m c k) -> p m c k", m=2, c=2),
                            pairs[:, :, :, odd].unsqueeze(2).to_broadcast(shape),
                            t[:, odd : odd + 2, :].unsqueeze(1).to_broadcast(shape), ALU.mult)
                    ins.then_inc(s_rot, 1)

            def qk_lo(n, i):
                dve.wait_ge(s_qk_hi, n + 1)
                at = bass.ds(i * 2 * P, 2 * P)
                nc.vector.tensor_tensor(qkT[:, 1, :, at], psum_t[1][:, :].rearrange("p (m t) -> p m t", m=2),
                                        qkT[:, 0, :, at], ALU.subtract).then_inc(s_qk_lo, 1)

            def p_lo(t, g):
                dve.wait_ge(s_p_hi, 4 * t + g + 1)
                at = slice(g * 512, (g + 1) * 512)
                nc.vector.scalar_tensor_tensor(pT[:, 1, at], psum_t[g % 2][:, :], P_SCALE, pT[:, 0, at],
                                               ALU.mult, ALU.subtract).then_inc(s_p_lo, 1)

            def half_max(t, h):
                dve.wait_ge(s_scores, 2 * t + h + 1)
                nc.vector.tensor_reduce(row_max[:, h : h + 1], psum_s[:, h * S // 2 : (h + 1) * S // 2], AX.X,
                                        ALU.max).then_inc(s_max, 1)

            def step(t, new, turn, fin):
                if turn:
                    dve.wait_ge(s_exp, 2 * t)
                    nc.vector.tensor_scalar(row_sum[:, 0:1], row_sum[:, 0:1], row_sum[:, 1:2], P_SCALE,
                                            ALU.add, ALU.mult).then_inc(s_sum, 1)
                    dve.wait_ge(s_sum, t)
                    nc.vector.reciprocal(row_rec, row_sum[:, 0:1]).then_inc(s_rec, 1)
                    p_lo(t - 1, 0)
                    p_lo(t - 1, 1)
                if new:
                    half_max(t, 0)
                if fin:
                    dve.wait_ge(s_o_hi, t - 1)
                    nc.vector.tensor_tensor(oT[:, 1, :], psum_y[:, 0:P], oT[:, 0, :], ALU.subtract).then_inc(s_o_lo, 1)
                if new:
                    half_max(t, 1)
                    dve.wait_ge(s_max, 2 * t + 2)
                    nc.vector.scalar_tensor_tensor(neg_max, row_max[:, 0:1], row_max[:, 1:2], neg_alpha[:, 0:1],
                                                   ALU.max, ALU.mult).then_inc(s_negmax, 1)
                if turn:
                    p_lo(t - 1, 2)
                    p_lo(t - 1, 3)
                if fin:
                    dve.wait_ge(s_proj, t - 1)
                    nc.vector.bn_stats(y_stats, psum_y[:, D : 2 * D]).then_inc(s_ystat, 1)
                    dve.wait_ge(s_ystat, t - 1)
                    dve.sem_inc(s_held, 1)
                    nc.vector.bn_aggr(y_mv, y_stats).then_inc(s_ymv, 1)
                    dve.wait_ge(s_ymv, t - 1)
                    nc.vector.tensor_scalar(y_var, y_mv[:, 1:2], attn_eps[:, 0:1], None, ALU.add)
                    nc.vector.tensor_scalar(y_negmean, y_mv[:, 0:1], -1.0, None, ALU.mult).then_inc(s_yvar, 1)
                if turn:
                    dve.wait_ge(s_o_part, t)
                    if fin:
                        dve.wait_ge(s_to, t - 1)
                    nc.vector.scalar_tensor_tensor(o_tok, psum_o[:, 0:HD], row_rec, o_part, ALU.mult,
                                                   ALU.add).then_inc(s_o, 1)

            for b in range(B):
                for c in range(2 * b, 2 * b + 2):
                    dve.wait_ge(s_x[c], 16)
                with dve.Fori(0, NT) as i:
                    nc.vector.bn_stats(stats[:, bass.ds(i, 1), :].rearrange("p a k -> p (a k)"),
                                       x_sb[:, tile_of(b * NT + i)]).then_inc(s_dve, 1)
                dve_steps[0] += NT
                dve.wait_ge(s_dve, dve_steps[0])
                half_mean, half_m2 = (lambda k: stats[:, :, 3 * k + 1]), (lambda k: stats[:, :, 3 * k + 2])
                link(nc.vector.tensor_tensor(tmp_x[:, 0, :], half_mean(0), half_mean(1), ALU.subtract))
                link(nc.vector.tensor_tensor(tmp_x[:, 1, :], half_m2(0), half_m2(1), ALU.add))
                link(nc.vector.tensor_tensor(tmp_x[:, 2, :], tmp_x[:, 0, :], tmp_x[:, 0, :], ALU.mult))
                link(nc.vector.tensor_scalar(tmp_x[:, 1, :], tmp_x[:, 1, :], 1.0 / D, LN_EPS, ALU.mult, ALU.add))
                link(nc.vector.scalar_tensor_tensor(tmp_x[:, 3, :], tmp_x[:, 2, :], 0.25, tmp_x[:, 1, :], ALU.mult, ALU.add))
                link(nc.vector.tensor_tensor(mean_x, half_mean(0), half_mean(1), ALU.add))
                nc.vector.tensor_scalar(mean_x, mean_x, 0.5, None, ALU.mult).then_inc(s_var_x, 1)
                dve.wait_ge(s_rstd_x, b + 1)
                link(nc.vector.tensor_scalar(rstd_x, rstd_x, X_SCALE, None, ALU.mult))
                if b == 0:
                    dve.wait_ge(s_tab, 16)
                n0 = b * PAIRS
                x_norm(n0, 0)
                x_lo(n0)

                def pair(n, i, more):
                    if more:
                        x_norm(n + 1, i + 1)
                    v_and_rotation(n, i)
                    if more:
                        x_lo(n + 1)
                    qk_lo(n, i)

                pair(n0, 0, True)
                with dve.Fori(1, PAIRS - 1) as i:
                    pair(n0 + i, i, True)
                pair(n0 + PAIRS - 1, PAIRS - 1, False)
                t0 = b * NT
                step(t0, True, False, False)
                step(t0 + 1, True, True, False)
                with dve.Fori(2, NT) as i:
                    step(t0 + i, True, True, True)
                step(t0 + NT, False, True, True)
                step(t0 + NT + 1, False, False, True)

        @block.tensor
        def _(pe):
            pe.wait_ge(s_const, 5)
            pe.wait_ge(s_attn_w, 64)
            for m in range(4):
                for c in range(DC):
                    at = (m % 2) * D + c * P
                    last = nc.tensor.transpose(psum_t[m // 2][:, at : at + P], attn_raw[:, m, c * P : (c + 1) * P], ident[:, :])
                if m % 2:
                    last.then_inc(s_wt, 1)

            def turn_x(n):
                if isinstance(n, int) and n == 0:
                    pe.wait_ge(s_wt_lo, 4)
                else:
                    pe.wait_ge(s_xt_lo, n)
                for u in range(2):
                    pe.wait_ge(s_xn, 2 * n + u + 1)
                    for c in range(DC):
                        last = nc.tensor.transpose(psum_t[0][:, (u * DC + c) * P : (u * DC + c + 1) * P],
                                                   xn[:, u, c * P : (c + 1) * P], ident[:, :])
                last.then_inc(s_tx, 1)

            def qkv(n):
                pe.wait_ge(s_xt_lo, n + 1)
                for u in range(2):
                    if not (isinstance(n, int) and n == 0):
                        pe.wait_ge(s_rot, 2 * n + u - 1)
                    for k, (c, lx, lw) in enumerate([(c, a, w) for c in range(DC) for a, w in ((0, 0), (0, 1), (1, 0))]):
                        last = nc.tensor.matmul(psum_s[:, u * 512 : u * 512 + 3 * HD], xT[:, lx, u, c, :],
                                                wqkvT[:, c, lw, :], start=(k == 0), stop=(k == 3 * DC - 1))
                    last.then_inc(s_qkv, 1)

            def turn_qk(n):
                if not (isinstance(n, int) and n == 0):
                    pe.wait_ge(s_qk_lo, n)
                for u in range(2):
                    pe.wait_ge(s_qk, 2 * n + u + 1)
                    for m in range(2):
                        last = nc.tensor.transpose(psum_t[1][:, (2 * m + u) * P : (2 * m + u + 1) * P],
                                                   qk_tok[:, u, m * HD : (m + 1) * HD], ident[:, :])
                last.then_inc(s_tqk, 1)

            def turn_p(t, g):
                pe.wait_ge(s_exp, 2 * t + g // 2 + 1)
                for k in range(4):
                    kc = 4 * g + k
                    last = nc.tensor.transpose(psum_t[g % 2][:, k * P : (k + 1) * P], probs[:, kc * P : (kc + 1) * P], ident[:, :])
                last.then_inc(s_tp, 1)

            def scores(i, kb):
                for k, (lq, lk) in enumerate(((0, 0), (0, 1), (1, 0))):
                    last = nc.tensor.matmul(psum_s[:, kb * 512 : (kb + 1) * 512], qkT[:, lq, 0, bass.ds(i * P, P)],
                                            qkT[:, lk, 1, kb * 512 : (kb + 1) * 512], start=(k == 0), stop=(k == 2))
                return last

            def step(t, i, new, turn, fin):
                if turn:
                    for g in range(2):
                        if fin:
                            pe.wait_ge(s_p_lo, 4 * t - 6 + g + 1)
                        turn_p(t - 1, g)
                if new:
                    for h in range(2):
                        if turn:
                            pe.wait_ge(s_exp, 2 * t - 1 + h)
                        scores(i, 2 * h)
                        scores(i, 2 * h + 1).then_inc(s_scores, 1)
                if fin:
                    pe.wait_ge(s_o, t - 1)
                    if not (isinstance(t, int) and t == 2):
                        pe.wait_ge(s_ynorm, t - 2)
                    nc.tensor.transpose(psum_y[:, 0:P], o_tok, ident[:, :]).then_inc(s_to, 1)
                if turn:
                    for g in range(2, 4):
                        pe.wait_ge(s_p_lo, 4 * (t - 1) + g - 1)
                        turn_p(t - 1, g)
                if fin:
                    pe.wait_ge(s_o_lo, t - 1)
                    for k, (lo, lw) in enumerate(((0, 0), (0, 1), (1, 0))):
                        last = nc.tensor.matmul(psum_y[:, D : 2 * D], oT[:, lo, :], woT[:, lw, :], start=(k == 0), stop=(k == 2))
                    last.then_inc(s_proj, 1)
                if turn:
                    if fin:
                        pe.wait_ge(s_o, t - 1)
                    for kc in range(NT):
                        if kc % 4 == 0:
                            pe.wait_ge(s_p_lo, 4 * (t - 1) + kc // 4 + 1)
                        at = slice(kc * P, (kc + 1) * P)
                        nc.tensor.matmul(psum_o[:, 0 : 2 * HD], pT[:, 0, at], v_sb[:, kc * 2 * HD : (kc + 1) * 2 * HD],
                                         start=(kc == 0), stop=False, skip_group_check=True)
                        last = nc.tensor.matmul(psum_o[:, 0:HD], pT[:, 1, at], v_tiles[:, kc, 0, :],
                                                start=False, stop=(kc == NT - 1), skip_group_check=True)
                    last.then_inc(s_pv, 1)

            for b in range(B):
                n0 = b * PAIRS
                turn_x(n0)

                def pair(n, more):
                    qkv(n)
                    if more:
                        turn_x(n + 1)
                    turn_qk(n)

                pair(n0, True)
                with pe.Fori(1, PAIRS - 1) as i:
                    pair(n0 + i, True)
                pair(n0 + PAIRS - 1, False)
                t0 = b * NT
                pe.wait_ge(s_qk_lo, n0 + PAIRS)
                pe.wait_ge(s_rot, 2 * (n0 + PAIRS))
                step(t0, 0, True, False, False)
                step(t0 + 1, 1, True, True, False)
                with pe.Fori(2, NT) as i:
                    step(t0 + i, i, True, True, True)
                step(t0 + NT, None, False, True, True)
                step(t0 + NT + 1, None, False, False, True)

        used[0] = 0
        z_aug = take(B * NT * ZW)
        slots = 4
        z_rows = z_aug.rearrange("p (t w) -> p t w", w=ZW)
        x_tile = take(UNROLL * ZW).rearrange("p (u w) -> p u w", u=UNROLL)
        x_row = take(D)
        e_xT = take(2 * D // 2).bitcast(F16).rearrange("p (l c t) -> p l c t", l=2, c=DC)
        silu_a = take(FF)
        h_row = take(FF)
        hT = take(2 * FF // 2).bitcast(F16).rearrange("p (l c t) -> p l c t", l=2, c=FC)
        y_row = take(UNROLL * D).rearrange("p (u d) -> p u d", u=UNROLL)
        z_turn = take(slots * D).rearrange("p (g d) -> p g d", g=slots)
        zT = take(2 * D).rearrange("p (u c t) -> p u c t", u=2, c=DC)
        gathered = take(slots * 2 * D).rearrange("p (g k d) -> p g k d", g=slots, k=2)
        squares = take(D)
        f_stats = take(NT * 6).rearrange("p (t k) -> p t k", t=NT)
        f_mean = take(NT)
        f_rstd = take(NT)
        f_tmp = take(4 * NT).rearrange("p (k t) -> p k t", k=4)
        sum_sq = take(NT)
        rms = take(2 * NT).rearrange("p (k t) -> p k t", k=2)
        r_logit = take(NT * NE)
        r_score = take(NT * NE)
        r_rest = take(NT * NE)
        r_pick = [take(NT * NE) for _ in range(2)]
        r_tmp = take(NT * NE)
        r_count = take(NT * NE)
        r_sum = take(NT * NE)
        tiny = take(4 * NT).rearrange("p (k t) -> p k t", k=4)
        best = take(2 * NT).rearrange("p (k t) -> p k t", k=2)
        gates = take(B * 2 * NT).rearrange("p (h k t) -> p h k t", h=B, k=2)
        rows_f = take(2 * NT).rearrange("p (k t) -> p k t", k=2)
        rows_of = take(B * 2 * NT).bitcast(U32).rearrange("p (h k t) -> p h k t", h=B, k=2)
        start_f = take(4 * NE).rearrange("p (k e) -> p k e", k=4)
        start_i = take(NE).bitcast(I32)
        rank_down = take(NE)
        rank_i = take(NE).bitcast(I32)
        tile_row = take(TILES)
        tile_row_i = take(TILES).bitcast(I32)
        tile_cmp = take(TILES * NE)
        expert_f = take(TILES)
        expert_of = take(B * TILES).bitcast(I32).rearrange("p (h t) -> p h t", h=B)
        zero_tile = take(NT)

        psum_a, psum_b = psum_s[:, 0:FF], psum_s[:, 512 : 512 + FF]
        psum_h, psum_x = psum_s[:, 1024:1536], psum_s[:, 1536 : 1536 + D]
        psum_e = psum_o[:, 0:D]
        psum_z, psum_l, psum_r = psum_t[0], psum_t[1], psum_y

        s_fconst = sem("routing_constants")
        s_pool = sem("pool_steps")
        s_fvar = sem("z_variance_ready")
        s_frstd = sem("z_rstd_ready")
        s_z = sem("z_ready")
        s_half = sem("z_first_expert_added")
        s_sq = sem("z_squared")
        s_ms = sem("mean_square_ready")
        s_rms = sem("rms_ready")
        s_zn = sem("z_copied")
        s_tz = sem("z_turned")
        s_znT = sem("zT_copied")
        s_fstat = sem("final_statistics")
        s_logit = sem("logits_ready")
        s_shift = sem("shifted_logits_ready")
        s_expl = sem("exp_logits_ready")
        s_pick = sem("picks_ready")
        s_count = sem("counts_ready")
        s_rows = sem("rows_ready")
        s_eid = sem("tile_experts_ready")
        s_scat = [sem(f"rows_scattered{h}") for h in range(B)]
        s_ldx = [sem(f"x_tile_loaded{u}") for u in range(UNROLL)]
        s_xrow = sem("x_row_ready")
        s_te = sem("x_row_turned")
        s_ex_hi = sem("expert_xT_hi")
        s_ex_lo = sem("expert_xT_lo")
        s_a = sem("a_ready")
        s_b = sem("b_ready")
        s_silu = sem("silu_ready")
        s_h = sem("h_ready")
        s_th = sem("h_turned")
        s_h_hi = sem("hT_hi")
        s_h_lo = sem("hT_lo")
        s_e = sem("expert_out_ready")
        s_yrow = sem("y_row_ready")
        s_sty = [sem(f"y_row_stored{u}") for u in range(UNROLL)]
        s_gather = [sem(f"gathered{g}") for g in range(slots)]
        s_out_t = sem("out_normalised")
        s_out_r = sem("out_tile_ready")
        s_out = sem("out_stored")

        order = [(l, h) for l in range(LOOPS) for h in range(B)]

        def zrow(j):
            return bass.ds(j * ZW, D)

        def zfac(j):
            return bass.ds(j * ZW + D, 1)


        GROUPS = TILES // UNROLL
        assert GROUPS * UNROLL == TILES
        QUADS = NT // slots

        def expert_pass(eng, k, group, quad, stage, last):
            group(0, None, True, False)
            if k == 0:
                group(1, None, False, False)
                with eng.Fori(2, GROUPS - 1) as i:
                    group(i, None, False, False)
            else:
                with eng.Fori(1, 1 + QUADS) as i:
                    group(i, lambda u, when: quad(k, i - 1, u, when), False, False)
                for g in range(2):
                    group(1 + QUADS + g, lambda u, when: stage(k, UNROLL * g + u, when), False, False)
                if k < 3:
                    with eng.Fori(3 + QUADS, GROUPS - 1) as i:
                        group(i, None, False, False)
                else:
                    with eng.Fori(3 + QUADS, 3 + 2 * QUADS) as i:
                        group(i, lambda u, when: last(i - 3 - QUADS, u, when), False, False)
                    for i in range(3 + 2 * QUADS, GROUPS - 1):
                        group(i, None, False, False)
            group(GROUPS - 1, None, False, True)

        block_stack.close()
        block2 = ctx.enter_context(nc.Block())

        @block2.sync
        def _(sp):
            def load(k, i, u):
                s = k * TILES + i * UNROLL + u
                if not (isinstance(s, int) and s < UNROLL):
                    sp.wait_ge(s_xrow, s - UNROLL + 1)
                rows = bass.ds((i * UNROLL + u) * P, P)
                sp.dma_start(x_tile[:, u, :], sorted_rows[order[k][1]][rows, :]).then_inc(s_ldx[u], 16)

            def store(k, i, u):
                sp.wait_ge(s_yrow, k * TILES + i * UNROLL + u + 1)
                rows = bass.ds((i * UNROLL + u) * P, P)
                sp.dma_start(expert_rows[order[k][1]][rows, :], y_row[:, u, :]).then_inc(s_sty[u], 16)

            def all_scattered(k):
                sp.wait_ge(s_scat[order[k][1]], 16 * 2 * NT * (order[k][0] + 1))

            all_scattered(0)
            for u in range(UNROLL):
                load(0, 0, u)
            for k in range(len(order)):
                with sp.Fori(0, GROUPS - 1) as i:
                    for u in range(UNROLL):
                        load(k, i + 1, u)
                        store(k, i, u)
                if k + 1 < len(order):
                    all_scattered(k + 1)
                for u in range(UNROLL):
                    if k + 1 < len(order):
                        load(k + 1, 0, u)
                    store(k, GROUPS - 1, u)
            out_view = out.rearrange("b (t p) d -> p (b t) d", p=P)
            src = x_sb[:, :].rearrange("p (t d) -> p t d", d=D)
            for c in range(2 * B):
                t = c * NT // 2
                sp.wait_ge(s_out_r, t + NT // 2)
                sp.dma_start(out_view[:, t : t + NT // 2, :], src[:, t : t + NT // 2, :]).then_inc(s_out, 16)
            sp.wait_ge(s_out, 16 * 2 * B)

        @block2.gpsimd
        def _(pool):
            nc.gpsimd.iota(rank_i, pattern=[[-1, NE]], base=NE, channel_multiplier=0).then_inc(s_fconst, 1)
            nc.gpsimd.iota(tile_row_i, pattern=[[P, TILES]], base=0, channel_multiplier=0).then_inc(s_fconst, 1)
            nc.gpsimd.memset(zero_tile, 0.0).then_inc(s_fconst, 1)

            def layer_norm_root(k):
                pool.wait_ge(s_fvar, k)
                nc.gpsimd.tensor_tensor(f_rstd, f_tmp[:, 3, :], neg_half[:, :], ALU.pow).then_inc(s_frstd, 1)

            def rms_root(r):
                pool.wait_ge(s_ms, r + 1)
                nc.gpsimd.tensor_tensor(rms[:, 1, :], rms[:, 0, :], neg_half[:, :], ALU.pow).then_inc(s_rms, 1)

            def scatter(r, h):
                pool.wait_ge(s_rows, r + 1)
                for c in range(2):
                    for j in range(NT):
                        nc.gpsimd.indirect_dma_start(
                            sorted_rows[h][:, :], bass.IndirectOffsetOnAxis(ap=rows_of[:, h, c, j : j + 1], axis=0),
                            z_rows[:, h * NT + j, :], None).then_inc(s_scat[h], 16)

            def gather(k):
                h = order[k][1]
                for u in range(UNROLL):
                    pool.wait_ge(s_sty[u], 16 * GROUPS * (k + 1))
                for j in range(NT):
                    use = k * NT + j
                    if use >= slots:
                        pool.wait_ge(s_z, B * NT + use - slots + 1)
                    for c in range(2):
                        nc.gpsimd.indirect_dma_start(
                            gathered[:, j % slots, c, :], None, expert_rows[h][:, :],
                            bass.IndirectOffsetOnAxis(ap=rows_of[:, h, c, j : j + 1], axis=0)).then_inc(s_gather[j % slots], 16)

            for h in range(B):
                layer_norm_root(h + 1)
                rms_root(h)
                scatter(h, h)
            for h in range(B):
                gather(h)
                rms_root(B + h)
                scatter(B + h, h)
            for h in range(B):
                gather(B + h)
                layer_norm_root(B + h + 1)

        @block2.scalar
        def _(act):
            def square(r, j, first=False):
                act.wait_ge(s_z, r * NT + j + 1)
                if not first:
                    act.wait_ge(s_sq, r * NT + j)
                nc.scalar.activation(squares, z_aug[:, zrow(r % B * NT + j)], ACT.Square,
                                     accum_out=sum_sq[:, bass.ds(j, 1)]).then_inc(s_sq, 1)

            def copy_zT(r, p):
                act.wait_ge(s_tz, r * PAIRS + p + 1)
                nc.scalar.activation(zT.rearrange("p u c t -> p (u c t)"), psum_z[:, :], ACT.Copy).then_inc(s_znT, 1)

            def exps(r):
                act.wait_ge(s_shift, r + 1)
                nc.scalar.activation(r_score, r_logit, ACT.Exp).then_inc(s_expl, 1)

            def route(r):
                square(r, 0, r == 0)
                for j in range(1, slots):
                    square(r, j)
                copy_zT(r, 0)
                copy_zT(r, 1)
                with act.Fori(1, QUADS) as q:
                    for g in range(slots):
                        square(r, q * slots + g)
                    copy_zT(r, 2 * q)
                    copy_zT(r, 2 * q + 1)
                exps(r)

            def quad(k, q, u, when):
                if k < 3 and u and when == "mid":
                    r = B + k - 1
                    for g in range(2):
                        square(r, q * slots + 2 * (u - 1) + g)
                    copy_zT(r, 2 * q + u - 1)

            def stage(k, step, when):
                if k < 3 and step == 2 and when == "mid":
                    exps(B + k - 1)

            def last(q, u, when):
                pass

            def experts(k):
                def x_hi(s):
                    act.wait_ge(s_te, s + 1)
                    nc.scalar.activation(e_xT[:, 0, :, :].rearrange("p c t -> p (c t)"), psum_x, ACT.Copy).then_inc(s_ex_hi, 1)

                def h_hi(s):
                    act.wait_ge(s_th, s + 1)
                    nc.scalar.activation(hT[:, 0, :, :].rearrange("p c t -> p (c t)"), psum_h, ACT.Copy).then_inc(s_h_hi, 1)

                def silu(s):
                    act.wait_ge(s_a, s + 1)
                    nc.scalar.activation(silu_a, psum_a, ACT.Silu, scale=silu_scale[:, 0:1]).then_inc(s_silu, 1)

                def y_copy(i, u):
                    act.wait_ge(s_e, (k * GROUPS + i) * UNROLL + u + 1)
                    if not (k == 0 and isinstance(i, int) and i == 0):
                        act.wait_ge(s_sty[u], 16 * (k * GROUPS + i))
                    nc.scalar.activation(y_row[:, u, :], psum_e, ACT.Copy).then_inc(s_yrow, 1)

                def group(i, join, first, final):
                    for u in range(UNROLL):
                        s = (k * GROUPS + i) * UNROLL + u
                        begin = first and u == 0
                        if begin:
                            x_hi(s)
                        else:
                            h_hi(s - 1)
                        silu(s)
                        if not (final and u == UNROLL - 1):
                            x_hi(s + 1)
                        if join:
                            join(u, "mid")
                        if not begin:
                            y_copy(*((i, u - 1) if u else (i - 1, UNROLL - 1)))
                    if final:
                        h_hi(s)
                        y_copy(i, UNROLL - 1)

                expert_pass(act, k, group, quad, stage, last)

            for h in range(B):
                route(h)
            for k in range(len(order)):
                experts(k)

        @block2.vector
        def _(dve):
            def link(ins):
                dve_steps[0] += 1
                ins.then_inc(s_dve, 1)
                dve.wait_ge(s_dve, dve_steps[0])

            def tok_exp(t):
                return t.rearrange("p (t e) -> p t e", e=NE)

            def per_tile(t):
                return t.unsqueeze(2).to_broadcast([P, NT, NE])

            def per_expert(t):
                return t.unsqueeze(1).to_broadcast([P, NT, NE])

            def norm_root():
                half_mean, half_m2 = (lambda q: f_stats[:, :, 3 * q + 1]), (lambda q: f_stats[:, :, 3 * q + 2])
                link(nc.vector.tensor_tensor(f_tmp[:, 0, :], half_mean(0), half_mean(1), ALU.subtract))
                link(nc.vector.tensor_tensor(f_tmp[:, 1, :], half_m2(0), half_m2(1), ALU.add))
                link(nc.vector.tensor_tensor(f_tmp[:, 2, :], f_tmp[:, 0, :], f_tmp[:, 0, :], ALU.mult))
                link(nc.vector.tensor_scalar(f_tmp[:, 1, :], f_tmp[:, 1, :], 1.0 / D, LN_EPS, ALU.mult, ALU.add))
                link(nc.vector.scalar_tensor_tensor(f_tmp[:, 3, :], f_tmp[:, 2, :], 0.25, f_tmp[:, 1, :], ALU.mult, ALU.add))
                link(nc.vector.tensor_tensor(f_mean, half_mean(0), half_mean(1), ALU.add))
                nc.vector.tensor_scalar(f_mean, f_mean, 0.5, None, ALU.mult).then_inc(s_fvar, 1)

            def to_turn(r, q, g, first=False):
                j = q * slots + g
                dve.wait_ge(s_z, r * NT + j + 1)
                if not first:
                    dve.wait_ge(s_tz, r * PAIRS + 2 * q + g // 2 - 1)
                nc.vector.tensor_scalar(z_turn[:, g, :], z_aug[:, zrow(r % B * NT + j)], 1.0, None, ALU.mult).then_inc(s_zn, 1)

            def combine(k, q, gs):
                h = order[k][1]
                for g in gs:
                    j = q * slots + g
                    dve.wait_ge(s_gather[g], 32 * (k * QUADS + q + 1))
                    nc.vector.scalar_tensor_tensor(z_aug[:, zrow(h * NT + j)], gathered[:, g, 0, :],
                                                   gates[:, h, 0, bass.ds(j, 1)], z_aug[:, zrow(h * NT + j)],
                                                   ALU.mult, ALU.add).then_inc(s_half, 1)
                for g in gs:
                    j = q * slots + g
                    dve.wait_ge(s_half, k * NT + j + 1)
                    nc.vector.scalar_tensor_tensor(z_aug[:, zrow(h * NT + j)], gathered[:, g, 1, :],
                                                   gates[:, h, 1, bass.ds(j, 1)], z_aug[:, zrow(h * NT + j)],
                                                   ALU.mult, ALU.add).then_inc(s_z, 1)

            def final_stats(k, q, gs):
                h = order[k][1]
                for g in gs:
                    j = q * slots + g
                    dve.wait_ge(s_z, (B + k) * NT + j + 1)
                    dve.sem_inc(s_held, 1)
                    nc.vector.bn_stats(f_stats[:, bass.ds(j, 1), :].rearrange("p a k -> p (a k)"),
                                       z_aug[:, zrow(h * NT + j)]).then_inc(s_fstat, 1)

            def finish(k, q, gs):
                h = order[k][1]
                for g in gs:
                    j = q * slots + g
                    nc.vector.tensor_scalar(z_aug[:, zrow(h * NT + j)], z_aug[:, zrow(h * NT + j)],
                                            f_mean[:, bass.ds(j, 1)], f_rstd[:, bass.ds(j, 1)], ALU.subtract,
                                            ALU.mult).then_inc(s_out_t, 1)
                for g in gs:
                    j = q * slots + g
                    dve.wait_ge(s_out_t, h * NT + j + 1)
                    nc.vector.tensor_tensor(x_sb[:, tile_of(h * NT + j)], x_sb[:, tile_of(h * NT + j)],
                                            z_aug[:, zrow(h * NT + j)], ALU.add).then_inc(s_out_r, 1)

            def mean_square(r):
                dve.wait_ge(s_sq, (r + 1) * NT)
                nc.vector.tensor_scalar(rms[:, 0, :], sum_sq, 1.0 / D, RMS_EPS, ALU.mult, ALU.add).then_inc(s_ms, 1)

            def shifted_logits(r):
                h = r % B
                dve.wait_ge(s_rms, r + 1)
                link(nc.vector.tensor_scalar(z_rows[:, h * NT : (h + 1) * NT, D], rms[:, 1, :], X_SCALE, None, ALU.mult))
                dve.wait_ge(s_logit, (r + 1) * PAIRS)
                logit = tok_exp(r_logit)
                link(nc.vector.tensor_tensor(logit, tok_exp(psum_l[:, 0 : NT * NE]), per_tile(rms[:, 1, :]), ALU.mult))
                link(nc.vector.tensor_reduce(tiny[:, 0, :], logit, AX.X, ALU.max))
                nc.vector.tensor_tensor(logit, logit, per_tile(tiny[:, 0, :]), ALU.subtract).then_inc(s_shift, 1)

            def picks(r):
                score, rest, tmp = tok_exp(r_score), tok_exp(r_rest), tok_exp(r_tmp)
                dve.wait_ge(s_expl, r + 1)
                link(nc.vector.tensor_reduce(tiny[:, 1, :], score, AX.X, ALU.add))
                link(nc.vector.reciprocal(tiny[:, 2, :], tiny[:, 1, :]))
                link(nc.vector.tensor_tensor(score, score, per_tile(tiny[:, 2, :]), ALU.mult))
                src = score
                for c in range(2):
                    pick = tok_exp(r_pick[c])
                    link(nc.vector.tensor_reduce(best[:, c, :], src, AX.X, ALU.max))
                    link(nc.vector.tensor_tensor(tmp, src, per_tile(best[:, c, :]), ALU.is_ge))
                    link(nc.vector.tensor_tensor(tmp, tmp, per_expert(rank_down), ALU.mult))
                    link(nc.vector.tensor_reduce(tiny[:, 3, :], tmp, AX.X, ALU.max))
                    link(nc.vector.tensor_tensor(pick, per_expert(rank_down), per_tile(tiny[:, 3, :]), ALU.is_equal))
                    if c == 0:
                        link(nc.vector.scalar_tensor_tensor(rest, pick, -2.0, score, ALU.mult, ALU.add))
                        src = rest
                nc.vector.tensor_tensor(r_count, r_pick[0], r_pick[1], ALU.add).then_inc(s_pick, 1)

            def gate_values(r):
                h = r % B
                link(nc.vector.tensor_tensor(tiny[:, 0, :], best[:, 0, :], best[:, 1, :], ALU.add))
                link(nc.vector.tensor_scalar(tiny[:, 0, :], tiny[:, 0, :], GATE_EPS, None, ALU.add))
                link(nc.vector.reciprocal(tiny[:, 1, :], tiny[:, 0, :]))
                for c in range(2):
                    link(nc.vector.tensor_tensor(tiny[:, 2, :], best[:, c, :], tiny[:, 1, :], ALU.mult))
                    link(nc.vector.tensor_scalar(gates[:, h, c, :], tiny[:, 2, :], y_unscale[:, 0:1], None, ALU.mult))

            def rows(r):
                h = r % B
                dve.wait_ge(s_count, r + 1)
                link(nc.vector.tensor_copy(r_tmp, psum_r[:, NT * NE : 2 * NT * NE]))
                tmp, up_to = tok_exp(r_tmp), tok_exp(r_sum)
                for e in range(NE):
                    ins = nc.vector.tensor_tensor_scan(up_to[:, :, e], tmp[:, :, e], zero_tile, 0.0, ALU.add, ALU.add)
                link(ins)
                total, padded, upper, start = (start_f[:, q, :] for q in range(4))
                link(nc.vector.tensor_scalar(start_i, up_to[:, NT - 1, :], float(P - 1), None, ALU.add))
                link(nc.vector.tensor_scalar(start_i, start_i, -P, None, ALU.bitwise_and))
                link(nc.vector.tensor_copy(padded, start_i))
                link(nc.vector.tensor_tensor_scan(upper, padded, zero_tile[:, 0:NE], 0.0, ALU.add, ALU.add))
                link(nc.vector.tensor_tensor(start, upper, padded, ALU.subtract))
                link(nc.vector.tensor_tensor(r_sum, r_sum, r_tmp, ALU.subtract))
                link(nc.vector.tensor_tensor(r_sum, r_sum, psum_r[:, 0 : NT * NE], ALU.add))
                link(nc.vector.tensor_tensor(up_to, up_to, per_expert(start), ALU.add))
                for c in range(2):
                    link(nc.vector.tensor_tensor(r_tmp, r_pick[c], r_sum, ALU.mult))
                    link(nc.vector.tensor_reduce(rows_f[:, c, :], tmp, AX.X, ALU.add))
                nc.vector.tensor_copy(rows_of[:, h, :, :], rows_f).then_inc(s_rows, 1)
                shape = [P, TILES, NE]
                cmp = tile_cmp.rearrange("p (t e) -> p t e", e=NE)
                link(nc.vector.tensor_tensor(cmp, tile_row.unsqueeze(2).to_broadcast(shape),
                                             start.unsqueeze(1).to_broadcast(shape), ALU.is_ge))
                link(nc.vector.tensor_reduce(expert_f, cmp, AX.X, ALU.add))
                nc.vector.tensor_scalar(expert_of[:, h, :], expert_f, -1.0, None, ALU.add).then_inc(s_eid, 1)

            def first_z(h):
                with dve.Fori(0, NT) as j:
                    nc.vector.bn_stats(f_stats[:, bass.ds(j, 1), :].rearrange("p a k -> p (a k)"),
                                       x_sb[:, tile_of(h * NT + j)]).then_inc(s_fstat, 1)
                dve.wait_ge(s_fstat, (h + 1) * NT)
                norm_root()
                dve.wait_ge(s_frstd, h + 1)

                def z_quad(q, first):
                    for g in range(slots):
                        j = q * slots + g
                        nc.vector.tensor_scalar(z_aug[:, zrow(h * NT + j)], x_sb[:, tile_of(h * NT + j)],
                                                f_mean[:, bass.ds(j, 1)], f_rstd[:, bass.ds(j, 1)], ALU.subtract,
                                                ALU.mult).then_inc(s_z, 1)
                    for g in range(slots):
                        to_turn(h, q, g, first)

                z_quad(0, h == 0)
                with dve.Fori(1, QUADS) as q:
                    z_quad(q, False)

            def quad(k, q, u, when):
                if u < 2:
                    gs = (2 * u, 2 * u + 1)
                    combine(k - 1, q, gs)
                    if k < 3:
                        for g in gs:
                            to_turn(B + k - 1, q, g)
                    else:
                        final_stats(k - 1, q, gs)

            def stage(k, step, when):
                if k < 3:
                    if step in (0, 1, 3, 4, 5):
                        (mean_square, shifted_logits, None, picks, gate_values, rows)[step](B + k - 1)
                elif step == 0:
                    dve.wait_ge(s_fstat, (B + 1) * NT)
                    norm_root()
                elif step == 2:
                    dve.wait_ge(s_frstd, B + 1)

            def last(q, u, when):
                if u < 2:
                    finish(len(order) - B, q, (2 * u, 2 * u + 1))

            def experts(k):
                def x_rows(i, u):
                    s = (k * GROUPS + i) * UNROLL + u
                    dve.wait_ge(s_ldx[u], 16 * (k * GROUPS + i + 1))
                    if not (isinstance(s, int) and s == 0):
                        dve.wait_ge(s_te, s)
                    nc.vector.tensor_scalar(x_row, x_tile[:, u, 0:D], x_tile[:, u, D : D + 1], None, ALU.mult).then_inc(s_xrow, 1)

                def x_lo(s):
                    dve.wait_ge(s_ex_hi, s + 1)
                    nc.vector.tensor_tensor(e_xT[:, 1, :, :].rearrange("p c t -> p (c t)"), psum_x,
                                            e_xT[:, 0, :, :].rearrange("p c t -> p (c t)"), ALU.subtract).then_inc(s_ex_lo, 1)

                def h_lo(s):
                    dve.wait_ge(s_h_hi, s + 1)
                    nc.vector.tensor_tensor(hT[:, 1, :, :].rearrange("p c t -> p (c t)"), psum_h,
                                            hT[:, 0, :, :].rearrange("p c t -> p (c t)"), ALU.subtract).then_inc(s_h_lo, 1)

                def gate(s):
                    dve.wait_ge(s_b, s + 1)
                    dve.wait_ge(s_silu, s + 1)
                    nc.vector.scalar_tensor_tensor(h_row, psum_b, gate_scale[:, 0:1], silu_a, ALU.mult,
                                                   ALU.mult).then_inc(s_h, 1)

                def group(i, join, first, final):
                    for u in range(UNROLL):
                        s = (k * GROUPS + i) * UNROLL + u
                        begin = first and u == 0
                        more = not (final and u == UNROLL - 1)
                        if begin:
                            x_rows(i, 0)
                            x_lo(s)
                        if more:
                            x_rows(*((i, u + 1) if u + 1 < UNROLL else (i + 1, 0)))
                        if not begin:
                            h_lo(s - 1)
                        gate(s)
                        if more:
                            x_lo(s + 1)
                        if join:
                            join(u, "end")
                    if final:
                        h_lo(s)

                expert_pass(dve, k, group, quad, stage, last)

            dve.wait_ge(s_fconst, 3)
            link(nc.vector.tensor_copy(rank_down, rank_i))
            link(nc.vector.tensor_copy(tile_row, tile_row_i))
            link(nc.vector.memset(z_rows[:, :, D:ZW], 0.0))
            for h in range(B):
                first_z(h)
                for step in (mean_square, shifted_logits, picks, gate_values, rows):
                    step(h)
            for k in range(len(order)):
                experts(k)
            k = len(order) - 1
            with dve.Fori(0, QUADS) as q:
                combine(k, q, range(slots))
                final_stats(k, q, range(slots))
            dve.wait_ge(s_fstat, (B + 2) * NT)
            norm_root()
            dve.wait_ge(s_frstd, B + 2)
            with dve.Fori(0, QUADS) as q:
                finish(k, q, range(slots))

        @block2.tensor
        def _(pe):
            def turn(r, q, half, first=False):
                p = r * PAIRS + 2 * q + half
                if not first:
                    pe.wait_ge(s_znT, p)
                pe.wait_ge(s_zn, 2 * p + 2)
                for v in range(2):
                    for c in range(DC):
                        last = nc.tensor.transpose(psum_z[:, (v * DC + c) * P : (v * DC + c + 1) * P],
                                                   z_turn[:, 2 * half + v, c * P : (c + 1) * P], ident[:, :])
                last.then_inc(s_tz, 1)

            def logits(r, q, half):
                p = 2 * q + half
                pe.wait_ge(s_znT, r * PAIRS + p + 1)
                for v in range(2):
                    for c in range(DC):
                        last = nc.tensor.matmul(psum_l[:, bass.ds((2 * p + v) * NE, NE)], zT[:, v, c, :],
                                                router_c[:, c, :], start=(c == 0), stop=(c == DC - 1))
                last.then_inc(s_logit, 1)

            def counts(r):
                pe.wait_ge(s_pick, r + 1)
                if r:
                    pe.wait_ge(s_rows, r)
                nc.tensor.matmul(psum_r[:, 0 : NT * NE], before[:, :], r_count, start=True, stop=True)
                nc.tensor.matmul(psum_r[:, NT * NE : 2 * NT * NE], ones[:, :], r_count, start=True, stop=True).then_inc(s_count, 1)

            def route(r):
                if r:
                    pe.wait_ge(s_pick, r)
                for half in range(2):
                    turn(r, 0, half, r == 0 and half == 0)
                    logits(r, 0, half)
                with pe.Fori(1, QUADS) as q:
                    for half in range(2):
                        turn(r, q, half)
                        logits(r, q, half)
                counts(r)

            def quad(k, q, u, when):
                if k < 3:
                    r = B + k - 1
                    if when == "mid":
                        if u == 2:
                            logits(r, q, 0)
                        if u:
                            turn(r, q, u - 1)
                    elif u == 2:
                        logits(r, q, 1)

            def stage(k, step, when):
                if k < 3 and step == 4 and when == "mid":
                    counts(B + k - 1)

            def last(q, u, when):
                pass

            def experts(k):
                h = order[k][1]

                def expert(s):
                    return pe.value_load(expert_of[0:1, h, bass.ds(s, 1)], min_val=0, max_val=NE - 1)

                def turn_x(n):
                    pe.wait_ge(s_xrow, n + 1)
                    for c in range(DC):
                        last = nc.tensor.transpose(psum_x[:, c * P : (c + 1) * P], x_row[:, c * P : (c + 1) * P], ident[:, :])
                    last.then_inc(s_te, 1)

                def inner(n, e):
                    pe.wait_ge(s_ex_lo, n + 1)
                    for m, (bank, signal) in enumerate(((psum_a, s_a), (psum_b, s_b))):
                        for q, (c, lx, lw) in enumerate([(c, a, w) for c in range(DC) for a, w in ((0, 0), (1, 0), (0, 1))]):
                            at = ((m * DC + c) * 2 + lw) * GROUP
                            last = nc.tensor.matmul(bank, e_xT[:, lx, c, :], w_split[:, bass.ds(e * EW + at, FF)],
                                                    start=(q == 0), stop=(q == 3 * DC - 1))
                        last.then_inc(signal, 1)

                def turn_h(n):
                    pe.wait_ge(s_h, n + 1)
                    for c in range(FC):
                        last = nc.tensor.transpose(psum_h[:, c * P : (c + 1) * P], h_row[:, c * P : (c + 1) * P], ident[:, :])
                    last.then_inc(s_th, 1)

                def outer(n, e):
                    pe.wait_ge(s_h_lo, n + 1)
                    if not (isinstance(n, int) and n == 0):
                        pe.wait_ge(s_yrow, n)
                    for q, (c, lh, lw) in enumerate([(c, a, w) for c in range(FC) for a, w in ((0, 0), (1, 0), (0, 1))]):
                        per = GROUP // D
                        at = ((2 * DC + c // per) * 2 + lw) * GROUP + c % per * D
                        last = nc.tensor.matmul(psum_e, hT[:, lh, c, :], w_split[:, bass.ds(e * EW + at, D)],
                                                start=(q == 0), stop=(q == 3 * FC - 1))
                    last.then_inc(s_e, 1)

                def group(i, join, first, final):
                    if first:
                        pe.wait_ge(s_eid, k + 1)
                    before_e = None if first else expert(i * UNROLL - 1)
                    for u in range(UNROLL):
                        n = (k * GROUPS + i) * UNROLL + u
                        e = expert(i * UNROLL + u)
                        begin = first and u == 0
                        if begin:
                            turn_x(n)
                        else:
                            turn_h(n - 1)
                        inner(n, e)
                        if not (final and u == UNROLL - 1):
                            turn_x(n + 1)
                        if join:
                            join(u, "mid")
                        if not begin:
                            outer(n - 1, before_e)
                        if join:
                            join(u, "end")
                        before_e = e
                    if final:
                        turn_h(n)
                        outer(n, before_e)

                expert_pass(pe, k, group, quad, stage, last)

            for h in range(B):
                route(h)
            for k in range(len(order)):
                experts(k)


_INS = ["L0_attn_x", "L0_attn_wq", "L0_attn_wk", "L0_attn_wv", "L0_attn_wo", "L0_ffn_norm_w", "L0_ffn_router_w",
        "L0_ffn_w1", "L0_ffn_w3", "L0_ffn_w2"]


def kernel(**inputs):
    import concourse.bacc as _bacc
    from concourse.bass_utils import run_bass_kernel_spmd as _run

    nc = _bacc.Bacc("TRN2", target_bir_lowering=False, num_devices=1)
    arrays, args = {}, []
    named = [(name, np.ascontiguousarray(inputs[name])) for name in _INS] + [("rope", rope_table())]
    for name, a in named:
        arrays[f"in_{name}"] = a
        args.append(nc.dram_tensor(f"in_{name}", a.shape, mybir.dt.from_np(a.dtype), kind="ExternalInput").ap())
    args.append(nc.dram_tensor("out_0", (B, S, D), F32, kind="ExternalOutput").ap())
    args.append([nc.dram_tensor(f"sorted_rows{h}", (ROWS, ZW), F32, kind="Internal").ap() for h in range(B)])
    args.append([nc.dram_tensor(f"expert_rows{h}", (ROWS, D), F32, kind="Internal").ap() for h in range(B)])
    sandwich_kernel(nc, *args)
    r = _run(nc, [arrays], core_ids=[0])
    return r.results[0]["out_0"]
```

```python
from contextlib import ExitStack

import concourse.bass as bass
import numpy as np
from concourse import mybir

ALU = mybir.AluOpType
ACT = mybir.ActivationFunctionType
AX = mybir.AxisListType
F32 = mybir.dt.float32
F16 = mybir.dt.float16
I32 = mybir.dt.int32
U32 = mybir.dt.uint32
ABSMAX = bass.bass_isa.ReduceOp.absmax

P = 128
B, S, D, HD = 2, 2048, 256, 128
NE, FF, LOOPS = 8, 512, 2
DC, FC = D // P, FF // P
NT = S // P
PAIRS = NT // 2
KB = S // 512
TILES = 2 * S // P + NE - 1
ROWS = TILES * P
UNROLL = 3
ZW = D + 2
GROUP = 512
NG = (2 * DC * FF + FC * D) // GROUP
SPLITS = 2
EW = NG * 2 * GROUP

LN_EPS, RMS_EPS, GATE_EPS = 1e-5, 1e-6, 1e-9
W_EXP = 9
X_SCALE = 2.0**11
QKV_SCALE = 2.0**-15
P_SCALE = 2.0**14
ARENA = 17960
EXP_BITS = 0x7F800000
ROPE_BASE = 10000.0


def rope_table():
    inv = np.float32(1.0) / np.float32(ROPE_BASE) ** (np.arange(0, HD, 2, dtype=np.float32) / np.float32(HD))
    ang = np.arange(S - 1, dtype=np.float32)[:, None] * inv[None, :]
    cos = np.concatenate([np.ones((1, HD // 2), np.float32), np.cos(ang)])
    sin = np.concatenate([np.zeros((1, HD // 2), np.float32), np.sin(ang)])
    return (np.stack([cos, sin, cos], axis=1) * np.float32(QKV_SCALE)).astype(np.float32)


def sandwich_kernel(nc, x, wq, wk, wv, wo, norm_w, router_w, w1, w3, w2, rope, out, sorted_rows, expert_rows, token_rows):
    with ExitStack() as ctx:

        def sb(name, shape, dt=F32):
            return ctx.enter_context(nc.sbuf_tensor(name, shape, dt))

        def sem(name):
            return ctx.enter_context(nc.semaphore(name))

        w_all = sb("w_all", [P, (NE * NG + SPLITS) * GROUP])
        w_raw = w_all[:, SPLITS * GROUP :]
        w_split = w_all[:, :].bitcast(F16)
        zeros = w_all[:, 0 : 3 * ZW]
        x_sb = sb("x_sb", [P, B * NT * ZW])
        x_rows = x_sb[:, :].rearrange("p (t w) -> p t w", w=ZW)
        ident = sb("ident", [P, P])
        before = sb("before", [P, P])
        ones = sb("ones", [P, P])
        neg_half = sb("neg_half", [P, NT])
        norm_c = sb("norm_c", [P, DC])
        router_c = sb("router_c", [P, DC, NE])
        amax_a = sb("amax_a", [P, 4])
        pow_a = sb("pow_a", [P, 4])
        scale_a = sb("scale_a", [P, 4])
        amax_g = sb("amax_g", [P, NE * NG])
        amax_f = sb("amax_f", [P, 8])
        pow_f = sb("pow_f", [P, 3])
        scale_f = sb("scale_f", [P, 3])
        scale_g = sb("scale_g", [P, NE, NG])
        alpha = sb("alpha", [P, 1])
        neg_alpha = sb("neg_alpha", [P, 1])
        attn_eps = sb("attn_eps", [P, 1])
        silu_scale = sb("silu_scale", [P, 1])
        gate_scale = sb("gate_scale", [P, 1])
        y_unscale = sb("y_unscale", [P, 1])
        f_stats = sb("f_stats", [P, NT, 6])
        f_tmp = sb("f_tmp", [P, 4, NT])
        first_var = sb("first_var", [P, B, NT])
        f_mean = sb("f_mean", [P, B, NT])
        f_var = sb("f_var", [P, B, NT])
        f_rstd = sb("f_rstd", [P, B, NT])
        mean_sq = sb("mean_sq", [P, B, NT])
        rms = sb("rms", [P, B, NT])

        gates_sb = sb("gates", [P, B * 2 * NT])
        rows_sb = sb("rows_of", [P, B * 2 * NT], U32)
        expert_sb = sb("expert_of", [P, B * TILES], I32)
        gates = gates_sb[:, :].rearrange("p (h k t) -> p h k t", h=B, k=2)
        rows_of = rows_sb[:, :].rearrange("p (h k t) -> p h k t", h=B, k=2)
        expert_of = expert_sb[:, :].rearrange("p (h t) -> p h t", h=B)
        rank_sb = sb("rank_down", [P, NE])
        tile_row_sb = sb("tile_row", [P, TILES])
        zero_sb = sb("zero_tile", [P, NT])
        rank_down, tile_row, zero_tile = rank_sb[:, :], tile_row_sb[:, :], zero_sb[:, :]

        arena = sb("arena", [P, ARENA])
        used = [0]

        def take(words):
            a = arena[:, used[0] : used[0] + words]
            used[0] += words
            assert used[0] <= ARENA, used[0]
            return a

        slots = 4
        z_turn = take(slots * D).rearrange("p (g d) -> p g d", g=slots)
        zT = take(2 * 2 * D).rearrange("p (half u c t) -> p half u c t", half=2, u=2, c=DC)
        r_logit = take(NT * NE)
        r_score = take(NT * NE)
        r_rest = take(NT * NE)
        r_pick = [take(NT * NE) for _ in range(2)]
        r_tmp = take(NT * NE)
        r_count = take(NT * NE)
        r_sum = take(NT * NE)
        tiny = take(4 * NT).rearrange("p (k t) -> p k t", k=4)
        best = take(2 * NT).rearrange("p (k t) -> p k t", k=2)
        rows_f = take(2 * NT).rearrange("p (k t) -> p k t", k=2)
        start_f = take(4 * NE).rearrange("p (k e) -> p k e", k=4)
        start_i = take(NE).bitcast(I32)
        tile_cmp = take(TILES * NE)
        expert_f = take(TILES)
        routing_words = used[0]
        assert routing_words <= 2 * S, "fits under probs and pT"

        used[0] = 0
        probs = take(S)
        pT = take(2 * S // 2).bitcast(F16).rearrange("p (l s) -> p l s", l=2)
        qkT = take(2 * 2 * S // 2).bitcast(F16).rearrange("p (l m s) -> p l m s", l=2, m=2)
        v_sb = take(NT * 2 * HD // 2).bitcast(F16)
        v_tiles = v_sb.rearrange("p (t l h) -> p t l h", t=NT, l=2)
        tab = take(NT * 3 * HD // 2)
        shared = take(2 * 2 * 2 * HD)
        rot = shared.rearrange("p (u m n) -> p u m n", u=2, m=2)
        o_tok, o_part = shared[:, 0:HD], shared[:, HD : 2 * HD]
        oT = shared[:, 2 * HD : 2 * HD + P].bitcast(F16).rearrange("p (l t) -> p l t", l=2)
        y_norm = shared[:, 2 * HD + P : 2 * HD + P + D]
        qk_tok = take(2 * 2 * HD).rearrange("p (u n) -> p u n", u=2)
        xn = take(2 * D).rearrange("p (u d) -> p u d", u=2)
        xT = take(2 * 2 * D // 2).bitcast(F16).rearrange("p (l u c t) -> p l u c t", l=2, u=2, c=DC)
        w_tmp = take(GROUP)
        attn_raw = probs[:, 0 : 4 * D].rearrange("p (m n) -> p m n", m=4)
        wqkvT = take(DC * 2 * 3 * HD // 2).bitcast(F16).rearrange("p (c l n) -> p c l n", c=DC, l=2)
        woT = take(2 * D // 2).bitcast(F16).rearrange("p (l n) -> p l n", l=2)
        stats = take(NT * 6).rearrange("p (t k) -> p t k", t=NT)
        mean_x = take(NT)
        rstd_x = take(NT)
        shift_x = take(NT)
        tmp_x = take(4 * NT).rearrange("p (k t) -> p k t", k=4)
        row_max = take(2)
        neg_max = take(1)
        row_sum = take(2)
        row_rec = take(1)
        y_stats = take(6)
        y_mv = take(2)
        y_var = take(1)
        y_negmean = take(1)
        y_rstd = take(1)
        y_shift = take(1)

        psum_s = ctx.enter_context(nc.psum_tensor("psum_s", [P, S], F32))
        psum_t = [ctx.enter_context(nc.psum_tensor(f"psum_t{i}", [P, 512], F32)) for i in range(2)]
        psum_o = ctx.enter_context(nc.psum_tensor("psum_o", [P, 512], F32))
        psum_y = ctx.enter_context(nc.psum_tensor("psum_y", [P, 512], F32))

        C = NT * NE
        psum_z = (psum_o[:, :], psum_t[0][:, :])
        psum_l = (psum_y[:, 0:C], psum_t[1][:, 0:C])
        psum_r = (psum_y[:, C : 3 * C], psum_y[:, 0 : 2 * C])

        s_x = [sem(f"x_loaded{i}") for i in range(4)]
        s_attn_w = sem("attn_weights_loaded")
        s_small = sem("small_inputs_loaded")
        s_tab = sem("rope_loaded")
        s_raw = [sem(f"expert_loaded{e}") for e in range(NE)]
        s_zero_fill = sem("sorted_rows_zeroed")
        s_const = sem("constants_ready")
        s_amax_a = sem("attn_amax_parts")
        s_all_a = sem("attn_amax_ready")
        s_scale_a = sem("attn_scales_ready")
        s_wt = sem("attn_weights_turned")
        s_wt_hi = sem("attn_weights_hi")
        s_wt_lo = sem("attn_weights_lo")
        s_amax_f = sem("expert_amax_parts")
        s_all_f = sem("expert_amax_ready")
        s_scale_f = sem("expert_scales_ready")
        s_amax_g = sem("group_amax_ready")
        s_w_hi = sem("expert_weights_hi")
        s_w_tmp = sem("expert_weights_scaled")
        s_w_lo = sem("expert_weights_lo_by_pool")
        s_w_lo_v = sem("expert_weights_lo_by_vector")
        s_dve = sem("vector_steps")
        s_var_x = sem("ln_variance_ready")
        s_rstd_x = sem("ln_rstd_ready")
        s_shift_x = sem("ln_shift_ready")
        s_xn = sem("xn_ready")
        s_tx = sem("xn_turned")
        s_xt_hi = sem("xT_hi")
        s_xt_lo = sem("xT_lo")
        s_qkv = sem("qkv_ready")
        s_v_hi = sem("v_hi")
        s_rot = sem("qkv_bank_read")
        s_qk = sem("qk_rotated")
        s_tqk = sem("qk_turned")
        s_qk_hi = sem("qkT_hi")
        s_qk_lo = sem("qkT_lo")
        s_scores = sem("scores_ready")
        s_max = sem("row_max_parts")
        s_negmax = sem("neg_max_ready")
        s_exp = sem("probs_ready")
        s_tp = sem("probs_turned")
        s_p_hi = sem("pT_hi")
        s_p_lo = sem("pT_lo")
        s_pv = sem("weighted_values_ready")
        s_sum = sem("row_sum_ready")
        s_rec = sem("row_rec_ready")
        s_o_part = sem("o_part_ready")
        s_o = sem("o_ready")
        s_to = sem("o_turned")
        s_o_hi = sem("oT_hi")
        s_o_lo = sem("oT_lo")
        s_proj = sem("projection_ready")
        s_ystat = sem("y_stats_ready")
        s_ymv = sem("y_mean_var_ready")
        s_held = sem("waits_held")
        s_yvar = sem("y_var_ready")
        s_yrstd = sem("y_rstd_ready")
        s_yshift = sem("y_shift_ready")
        s_ynorm = sem("y_norm_ready")
        s_x1 = sem("x1_ready")
        s_fstat = sem("z_statistics")
        s_fvar = sem("z_variance_ready")
        s_frstd = sem("z_rstd_ready")
        s_ms = sem("mean_square_ready")
        s_rms = sem("rms_ready")
        s_fconst = sem("routing_constants")
        s_zn = sem("z_copied")
        s_tz = sem("z_turned")
        s_znT = sem("zT_copied")
        s_logit = sem("logits_ready")
        s_shift = sem("shifted_logits_ready")
        s_expl = sem("exp_logits_ready")
        s_pick = sem("picks_ready")
        s_count = sem("counts_ready")
        s_rows = sem("rows_ready")
        s_eid = sem("tile_experts_ready")
        s_scat = [sem(f"rows_scattered{h}") for h in range(B)]

        FILLS = 16 * B * (TILES // 3)
        QUADS = NT // slots
        dve_steps = [0]

        def tile_of(j):
            return bass.ds(j * ZW, D)


        def layer_norm_root(pool, n, h, tiles):
            pool.wait_ge(s_fvar, n)
            nc.gpsimd.tensor_tensor(f_rstd[:, h, tiles], f_var[:, h, tiles], neg_half[:, tiles], ALU.pow).then_inc(s_frstd, 1)

        def rms_root(pool, r):
            pool.wait_ge(s_ms, r + 1)
            nc.gpsimd.tensor_tensor(rms[:, r % B, :], mean_sq[:, r % B, :], neg_half[:, :], ALU.pow).then_inc(s_rms, 1)

        def variance(link, h, tiles, half=0.5):
            half_mean, half_m2 = (lambda q: f_stats[:, tiles, 3 * q + 1]), (lambda q: f_stats[:, tiles, 3 * q + 2])
            diff, m2, square = (f_tmp[:, q, tiles] for q in range(3))
            mean, var, var_eps = f_mean[:, h, tiles], first_var[:, h, tiles], f_var[:, h, tiles]
            nc.vector.tensor_tensor(diff, half_mean(0), half_mean(1), ALU.subtract)
            nc.vector.tensor_tensor(m2, half_m2(0), half_m2(1), ALU.add)
            link(nc.vector.tensor_tensor(mean, half_mean(0), half_mean(1), ALU.add))
            nc.vector.tensor_tensor(square, diff, diff, ALU.mult)
            nc.vector.tensor_scalar(var, m2, 1.0 / D, None, ALU.mult)
            nc.vector.tensor_scalar(var_eps, m2, 1.0 / D, LN_EPS, ALU.mult, ALU.add)
            link(nc.vector.tensor_scalar(mean, mean, half, None, ALU.mult))
            nc.vector.scalar_tensor_tensor(var, square, 0.25, var, ALU.mult, ALU.add)
            nc.vector.scalar_tensor_tensor(var_eps, square, 0.25, var_eps, ALU.mult, ALU.add).then_inc(s_fvar, 1)

        def first_stats(dve, h, j):
            dve.wait_ge(s_x1, h * NT + j + 1)
            dve.sem_inc(s_held, 1)
            nc.vector.bn_stats(f_stats[:, bass.ds(j, 1), :].rearrange("p a k -> p (a k)"),
                               x_sb[:, tile_of(h * NT + j)]).then_inc(s_fstat, 1)

        def first_mean_square(dve, link, h):
            dve.wait_ge(s_frstd, h + 1)
            link(nc.vector.tensor_tensor(mean_sq[:, h, :], first_var[:, h, :], f_rstd[:, h, :], ALU.mult))
            link(nc.vector.tensor_tensor(mean_sq[:, h, :], mean_sq[:, h, :], f_rstd[:, h, :], ALU.mult))
            nc.vector.tensor_scalar(mean_sq[:, h, :], mean_sq[:, h, :], RMS_EPS, None, ALU.add).then_inc(s_ms, 1)

        order = [(l, h) for l in range(LOOPS) for h in range(B)]
        END = len(order) - 1


        def tok_exp(t):
            return t.rearrange("p (t e) -> p t e", e=NE)

        def per_tile(t):
            return t.unsqueeze(2).to_broadcast([P, NT, NE])

        def per_expert(t):
            return t.unsqueeze(1).to_broadcast([P, NT, NE])

        def shifted_logits(dve, link, r, dispatched):
            h = r % B
            dve.wait_ge(s_rms, r + 1)
            link(nc.vector.tensor_scalar(dispatched[:, :, D], rms[:, h, :], X_SCALE, None, ALU.mult))
            if r == 0:
                link(nc.vector.tensor_tensor(dispatched[:, :, D], dispatched[:, :, D], f_rstd[:, h, :], ALU.mult))
                link(nc.vector.tensor_copy(dispatched[:, :, D + 1], f_mean[:, h, :]))
            dve.wait_ge(s_logit, (r + 1) * PAIRS)
            logit = tok_exp(r_logit)
            link(nc.vector.tensor_tensor(logit, tok_exp(psum_l[r > 0]), per_tile(rms[:, h, :]), ALU.mult))
            link(nc.vector.tensor_reduce(tiny[:, 0, :], logit, AX.X, ALU.max))
            nc.vector.tensor_tensor(logit, logit, per_tile(tiny[:, 0, :]), ALU.subtract).then_inc(s_shift, 1)

        def softmax(dve, link, r):
            score = tok_exp(r_score)
            dve.wait_ge(s_expl, r + 1)
            link(nc.vector.tensor_reduce(tiny[:, 1, :], score, AX.X, ALU.add))
            link(nc.vector.reciprocal(tiny[:, 2, :], tiny[:, 1, :]))
            link(nc.vector.tensor_tensor(score, score, per_tile(tiny[:, 2, :]), ALU.mult))

        def pick_best(dve, link, r, c):
            score, rest, tmp, pick = tok_exp(r_score), tok_exp(r_rest), tok_exp(r_tmp), tok_exp(r_pick[c])
            src = rest if c else score
            link(nc.vector.tensor_reduce(best[:, c, :], src, AX.X, ALU.max))
            link(nc.vector.tensor_tensor(tmp, src, per_tile(best[:, c, :]), ALU.is_ge))
            link(nc.vector.tensor_tensor(tmp, tmp, per_expert(rank_down), ALU.mult))
            link(nc.vector.tensor_reduce(tiny[:, 3, :], tmp, AX.X, ALU.max))
            link(nc.vector.tensor_tensor(pick, per_expert(rank_down), per_tile(tiny[:, 3, :]), ALU.is_equal))
            if c == 0:
                link(nc.vector.scalar_tensor_tensor(rest, pick, -2.0, score, ALU.mult, ALU.add))
            else:
                nc.vector.tensor_tensor(r_count, r_pick[0], r_pick[1], ALU.add).then_inc(s_pick, 1)

        def gate_values(dve, link, r):
            h = r % B
            link(nc.vector.tensor_tensor(tiny[:, 0, :], best[:, 0, :], best[:, 1, :], ALU.add))
            link(nc.vector.tensor_scalar(tiny[:, 0, :], tiny[:, 0, :], GATE_EPS, None, ALU.add))
            link(nc.vector.reciprocal(tiny[:, 1, :], tiny[:, 0, :]))
            for c in range(2):
                ins = nc.vector.tensor_tensor(tiny[:, 2 + c, :], best[:, c, :], tiny[:, 1, :], ALU.mult)
            link(ins)
            for c in range(2):
                ins = nc.vector.tensor_scalar(gates[:, h, c, :], tiny[:, 2 + c, :], y_unscale[:, 0:1], None, ALU.mult)
            link(ins)


        def tiles_before(dve, link, r):
            dve.wait_ge(s_count, r + 1)
            link(nc.vector.tensor_copy(r_tmp, psum_r[r > 0][:, C : 2 * C]))
            tmp, up_to = tok_exp(r_tmp), tok_exp(r_sum)
            for e in range(NE):
                ins = nc.vector.tensor_tensor_scan(up_to[:, :, e], tmp[:, :, e], zero_tile, 0.0, ALU.add, ALU.add)
            link(ins)

        def expert_starts(dve, link, r):
            total, padded, upper, start = (start_f[:, q, :] for q in range(4))
            link(nc.vector.tensor_copy(total, tok_exp(r_sum)[:, NT - 1, :]))
            link(nc.vector.tensor_scalar(start_i, total, float(P - 1), None, ALU.add))
            link(nc.vector.tensor_scalar(start_i, start_i, -P, None, ALU.bitwise_and))
            link(nc.vector.tensor_copy(padded, start_i))
            link(nc.vector.tensor_tensor_scan(upper, padded, zero_tile[:, 0:NE], 0.0, ALU.add, ALU.add))
            link(nc.vector.tensor_tensor(start, upper, padded, ALU.subtract))

        def expert_rows_of_tiles(dve, link, r):
            link(nc.vector.tensor_tensor(r_sum, r_sum, r_tmp, ALU.subtract))
            link(nc.vector.tensor_tensor(r_sum, r_sum, psum_r[r > 0][:, 0:C], ALU.add))
            link(nc.vector.tensor_tensor(tok_exp(r_sum), tok_exp(r_sum), per_expert(start_f[:, 3, :]), ALU.add))

        def rows_of_tokens(dve, link, r):
            picked = (r_tmp, r_rest)
            for c in range(2):
                ins = nc.vector.tensor_tensor(picked[c], r_pick[c], r_sum, ALU.mult)
            link(ins)
            for c in range(2):
                ins = nc.vector.tensor_reduce(rows_f[:, c, :], tok_exp(picked[c]), AX.X, ALU.add)
            link(ins)
            nc.vector.tensor_copy(rows_of[:, r % B, :, :], rows_f).then_inc(s_rows, 1)

        def experts_of_tiles(dve, link, r):
            total, upper, start = (start_f[:, q, :] for q in (0, 2, 3))
            shape = [P, TILES, NE]
            cmp = tile_cmp.rearrange("p (t e) -> p t e", e=NE)
            link(nc.vector.tensor_tensor(cmp, tile_row.unsqueeze(2).to_broadcast(shape),
                                         start.unsqueeze(1).to_broadcast(shape), ALU.is_ge))
            link(nc.vector.tensor_reduce(expert_f, cmp, AX.X, ALU.add))
            nc.vector.tensor_scalar(expert_of[:, r % B, :], expert_f, -1.0, None, ALU.add).then_inc(s_eid, 1)
            if r == END:
                dve.wait_ge(s_eid, r + 1)
                tile_end = expert_f
                link(nc.vector.tensor_tensor(upper, start, total, ALU.add))
                link(nc.vector.tensor_tensor(cmp, cmp, upper.unsqueeze(1).to_broadcast(shape), ALU.mult))
                link(nc.vector.tensor_reduce(tile_end, cmp, AX.X, ALU.max))
                link(nc.vector.tensor_tensor(spare_dest, cell_row, tile_end, ALU.is_ge))
                link(nc.vector.tensor_tensor(spare_dest, spare_dest, spare_row, ALU.mult))

        place = (tiles_before, expert_starts, expert_rows_of_tiles, rows_of_tokens, experts_of_tiles)

        def turn(pe, r, p, half):
            if r or not isinstance(p, int):
                pe.wait_ge(s_znT, r * PAIRS + p)
            pe.wait_ge(s_zn, 2 * (r * PAIRS + p) + 2)
            for v in range(2):
                for c in range(DC):
                    last = nc.tensor.transpose(psum_z[r > 0][:, (v * DC + c) * P : (v * DC + c + 1) * P],
                                               z_turn[:, 2 * half + v, c * P : (c + 1) * P], ident[:, :])
            last.then_inc(s_tz, 1)

        def logits(pe, r, p, half):
            pe.wait_ge(s_znT, r * PAIRS + p + 1)
            for v in range(2):
                for c in range(DC):
                    last = nc.tensor.matmul(psum_l[r > 0][:, bass.ds((2 * p + v) * NE, NE)], zT[:, half, v, c, :],
                                            router_c[:, c, :], start=(c == 0), stop=(c == DC - 1))
            last.then_inc(s_logit, 1)

        def counts(pe, r):
            pe.wait_ge(s_pick, r + 1)
            if r:
                pe.wait_ge(s_rows, r)
            nc.tensor.matmul(psum_r[r > 0][:, 0:C], before[:, :], r_count, start=True, stop=True)
            nc.tensor.matmul(psum_r[r > 0][:, C : 2 * C], ones[:, :], r_count, start=True, stop=True).then_inc(s_count, 1)

        def copy_zT(act, r, p, half):
            act.wait_ge(s_tz, r * PAIRS + p + 1)
            nc.scalar.activation(zT[:, half, :, :, :].rearrange("p u c t -> p (u c t)"), psum_z[r > 0],
                                 ACT.Copy).then_inc(s_znT, 1)

        def exps(act, r):
            act.wait_ge(s_shift, r + 1)
            nc.scalar.activation(r_score, r_logit, ACT.Exp).then_inc(s_expl, 1)

        block_stack = ctx.enter_context(ExitStack())
        block = block_stack.enter_context(nc.Block())


        @block.sync
        def _(sp):
            x_view = x.rearrange("b (t p) d -> p (b t) d", p=P)
            x_dst = x_rows[:, :, 0:D]
            q = B * NT // 4

            def load_x(c):
                sp.dma_start(x_dst[:, c * q : (c + 1) * q, :], x_view[:, c * q : (c + 1) * q, :]).then_inc(s_x[c], 16)

            load_x(0)
            for m, w in enumerate((wq, wk, wv)):
                sp.dma_start(attn_raw[:, m, :], w).then_inc(s_attn_w, 16)
            sp.dma_start(attn_raw[:, 3, :].rearrange("p (c h) -> p c h", c=DC),
                         wo.rearrange("(c p) h -> p c h", p=P)).then_inc(s_attn_w, 16)
            load_x(1)
            sp.dma_start(tab.rearrange("p (t k) -> p t k", t=NT),
                         rope.rearrange("(t p) c k -> p t (c k)", p=P)).then_inc(s_tab, 16)
            load_x(2)
            load_x(3)
            with nc.allow_non_contiguous_dma(reason="256 values"):
                sp.dma_start(norm_c[:, :], norm_w.rearrange("(c p) -> p c", p=P)).then_inc(s_small, 16)
            sp.dma_start(router_c[:, :, :], router_w.rearrange("(c p) e -> p c e", p=P)).then_inc(s_small, 16)
            for e in range(NE):
                at = e * NG * GROUP
                for w, chunks, width in ((w1, DC, FF), (w3, DC, FF), (w2, FC, D)):
                    n = chunks * width
                    sp.dma_start(w_raw[:, at : at + n].rearrange("p (c f) -> p c f", c=chunks),
                                 w[e].rearrange("(c p) f -> p c f", p=P)).then_inc(s_raw[e], 16)
                    at += n
            sp.wait_ge(s_const, 3)
            for h in range(B):
                for t in range(0, TILES, 3):
                    sp.dma_start(sorted_rows[h][t * P : (t + 3) * P, :].rearrange("(t p) d -> p t d", p=P),
                                 zeros.rearrange("p (t d) -> p t d", t=3)).then_inc(s_zero_fill, 16)
            sp.wait_ge(s_zero_fill, FILLS)

        @block.gpsimd
        def _(pool):
            nc.gpsimd.memset(ident[:, :], 0.0).then_inc(s_const, 1)
            nc.gpsimd.memset(ones[:, :], 1.0).then_inc(s_const, 1)
            nc.gpsimd.memset(zeros, 0.0).then_inc(s_const, 1)
            nc.gpsimd.memset(neg_half[:, :], -0.5).then_inc(s_const, 1)
            nc.gpsimd.iota(rank_down.bitcast(I32), pattern=[[-1, NE]], base=NE, channel_multiplier=0).then_inc(s_fconst, 1)
            nc.gpsimd.iota(tile_row.bitcast(I32), pattern=[[P, TILES]], base=0, channel_multiplier=0).then_inc(s_fconst, 1)
            nc.gpsimd.memset(zero_tile, 0.0).then_inc(s_fconst, 1)
            pool.wait_ge(s_const, 4)
            nc.gpsimd.affine_select(out=ident[:, :], in_=ident[:, :], compare_op=ALU.not_equal, fill=1.0,
                                    base=0, pattern=[[-1, P]], channel_multiplier=1).then_inc(s_const, 1)
            nc.gpsimd.affine_select(out=before[:, :], in_=ones[:, :], compare_op=ALU.is_gt, fill=0.0,
                                    base=0, pattern=[[1, P]], channel_multiplier=-1).then_inc(s_const, 1)
            pool.wait_ge(s_const, 6)
            pool.wait_ge(s_amax_a, 1)
            nc.gpsimd.partition_all_reduce(amax_a[:, :], amax_a[:, :], P, ABSMAX).then_inc(s_all_a, 1)
            def rotate(n):
                for u in range(2):
                    pool.wait_ge(s_rot, 2 * n + u + 1)
                    if not (isinstance(n, int) and n == 0):
                        pool.wait_ge(s_tqk, n)
                    c = rot[:, u, 0, :].rearrange("p (m c k) -> p m c k", m=2, c=2)
                    s = rot[:, u, 1, :].rearrange("p (m c k) -> p m c k", m=2, c=2)
                    o = qk_tok[:, u, :].rearrange("p (m c k) -> p m c k", m=2, c=2)
                    nc.gpsimd.tensor_tensor(o[:, :, 0, :], c[:, :, 0, :], s[:, :, 0, :], ALU.subtract)
                    nc.gpsimd.tensor_tensor(o[:, :, 1, :], c[:, :, 1, :], s[:, :, 1, :], ALU.add).then_inc(s_qk, 1)

            def split(group, done):
                if not (isinstance(done, int) and done == 0):
                    pool.wait_ge(s_w_lo, done)
                raw = w_raw[:, bass.ds(group * GROUP, GROUP)]
                scale = scale_g[:, :, :].rearrange("p e g -> p (e g)")[:, bass.ds(group, 1)]
                nc.gpsimd.tensor_tensor(w_tmp, raw, scale.to_broadcast([P, GROUP]), ALU.mult).then_inc(s_w_tmp, 1)
                pool.wait_ge(s_w_tmp, done + 1)
                pool.wait_ge(s_w_hi, group + 1)
                nc.gpsimd.tensor_tensor(w_split[:, bass.ds(group * 2 * GROUP + GROUP, GROUP)], w_tmp,
                                        w_split[:, bass.ds(group * 2 * GROUP, GROUP)], ALU.subtract).then_inc(s_w_lo, 1)

            def normalise(t, splits):
                pool.wait_ge(s_yvar, t + 1)
                nc.gpsimd.tensor_tensor(y_rstd, y_var, neg_half[:, 0:1], ALU.pow).then_inc(s_yrstd, 1)
                pool.wait_ge(s_yrstd, t + 1)
                nc.gpsimd.tensor_tensor(y_shift, y_negmean, y_rstd, ALU.mult).then_inc(s_yshift, 1)
                if splits is not None:
                    split(splits, splits - PAIRS)
                pool.wait_ge(s_ynorm, t + 1)
                nc.gpsimd.tensor_tensor(x_sb[:, tile_of(t)], x_sb[:, tile_of(t)], y_norm, ALU.add).then_inc(s_x1, 1)
                if splits is not None:
                    split(splits + 1, splits + 1 - PAIRS)

            def row_root(b):
                pool.wait_ge(s_var_x, b + 1)
                nc.gpsimd.tensor_tensor(rstd_x, tmp_x[:, 3, :], neg_half[:, :], ALU.pow).then_inc(s_rstd_x, 1)

            def scatter_first(count):
                for _ in range(count):
                    c, j = divmod(scattered[0], NT)
                    nc.gpsimd.indirect_dma_start(
                        sorted_rows[0][:, :], bass.IndirectOffsetOnAxis(ap=rows_of[:, 0, c, j : j + 1], axis=0),
                        x_rows[:, j, :], None).then_inc(s_scat[0], 16)
                    scattered[0] += 1

            scattered = [0]
            row_root(0)
            for b in range(B):
                n0 = b * PAIRS
                if b:
                    pool.wait_ge(s_scale_f, 1)
                rotate(n0)
                if b:
                    split(0, 0)
                    rms_root(pool, 0)
                with pool.Fori(1, PAIRS) as i:
                    rotate(n0 + i)
                    if b:
                        split(SPLITS * i, i)
                t0 = b * NT
                if b == 0:
                    with pool.Fori(0, NT - 2) as i:
                        normalise(t0 + i, None)
                else:
                    pool.wait_ge(s_rows, 1)
                    pool.wait_ge(s_zero_fill, FILLS)
                    scatter_first(NT + 2)
                    for pair in range(PAIRS - 1):
                        with pool.Fori(2 * pair, 2 * pair + 2) as i:
                            normalise(t0 + i, SPLITS * (PAIRS + i))
                        scatter_first(2)
                normalise(t0 + NT - 2, None)
                if b == 0:
                    pool.wait_ge(s_amax_f, 1)
                    nc.gpsimd.partition_all_reduce(amax_f[:, 0:3], amax_f[:, 0:3], P, ABSMAX).then_inc(s_all_f, 1)
                normalise(t0 + NT - 1, None)
                if b == 0:
                    row_root(1)
                    layer_norm_root(pool, 1, 0, slice(0, NT))

        @block.scalar
        def _(act):
            act.wait_ge(s_scale_a, 1)
            act.wait_ge(s_wt, 2)
            for m in range(3):
                src = psum_t[m // 2][:, (m % 2) * D : (m % 2 + 1) * D].rearrange("p (c n) -> p c n", c=DC)
                nc.scalar.activation(wqkvT[:, :, 0, m * HD : (m + 1) * HD], src, ACT.Copy,
                                     scale=scale_a[:, m : m + 1]).then_inc(s_wt_hi, 1)
            nc.scalar.activation(woT[:, 0, :], psum_t[1][:, D : 2 * D], ACT.Copy,
                                 scale=scale_a[:, 3:4]).then_inc(s_wt_hi, 1)

            def x_norm(n, i):
                for u in range(2):
                    if not (isinstance(n, int) and n == 0):
                        act.wait_ge(s_tx, n)
                    nc.scalar.activation(xn[:, u, :], x_sb[:, tile_of(2 * n + u)], ACT.Identity,
                                         bias=shift_x[:, bass.ds(2 * i + u, 1)],
                                         scale=rstd_x[:, bass.ds(2 * i + u, 1)]).then_inc(s_xn, 1)

            def x_hi(n):
                act.wait_ge(s_tx, n + 1)
                nc.scalar.activation(xT[:, 0, :, :, :].rearrange("p u c t -> p (u c t)"), psum_t[0][:, :],
                                     ACT.Copy).then_inc(s_xt_hi, 1)

            def v_hi(n, i):
                for u in range(2):
                    act.wait_ge(s_qkv, 2 * n + u + 1)
                    nc.scalar.activation(v_sb[:, bass.ds((2 * i + u) * 2 * HD, HD)],
                                         psum_s[:, u * 512 + 2 * HD : u * 512 + 3 * HD], ACT.Copy,
                                         scale=QKV_SCALE).then_inc(s_v_hi, 1)

            def qk_hi(n, i):
                act.wait_ge(s_tqk, n + 1)
                nc.scalar.activation(qkT[:, 0, :, bass.ds(i * 2 * P, 2 * P)],
                                     psum_t[1][:, :].rearrange("p (m t) -> p m t", m=2), ACT.Copy).then_inc(s_qk_hi, 1)

            def p_hi(t, g):
                act.wait_ge(s_tp, 4 * t + g + 1)
                nc.scalar.activation(pT[:, 0, g * 512 : (g + 1) * 512], psum_t[g % 2][:, :], ACT.Copy,
                                     scale=P_SCALE).then_inc(s_p_hi, 1)

            def split_hi(group):
                nc.scalar.activation(w_split[:, bass.ds(group * 2 * GROUP, GROUP)], w_raw[:, bass.ds(group * GROUP, GROUP)],
                                     ACT.Copy, scale=scale_g[:, :, :].rearrange("p e g -> p (e g)")[:, bass.ds(group, 1)]
                                     ).then_inc(s_w_hi, 1)

            def split_pair(i):
                if not (isinstance(i, int) and i == 0):
                    act.wait_ge(s_w_lo, i)
                    act.wait_ge(s_w_lo_v, i)
                for g in range(SPLITS):
                    split_hi(SPLITS * i + g)

            def step(t, i, new, turn, fin, norm, split):
                if turn:
                    p_hi(t - 1, 0)
                    p_hi(t - 1, 1)
                if fin:
                    act.wait_ge(s_pv, t - 1)
                    act.wait_ge(s_rec, t - 1)
                    nc.scalar.activation(o_part, psum_o[:, HD : 2 * HD], ACT.Copy, scale=row_rec).then_inc(s_o_part, 1)
                if norm:
                    act.wait_ge(s_yshift, t - 2)
                    nc.scalar.activation(y_norm, psum_y[:, D : 2 * D], ACT.Identity, bias=y_shift,
                                         scale=y_rstd).then_inc(s_ynorm, 1)
                if split:
                    if isinstance(i, int) and i > NT:
                        act.wait_ge(s_w_lo, PAIRS + SPLITS * (NT - 2))
                        act.wait_ge(s_w_lo_v, PAIRS + SPLITS * (i - NT - 1))
                    else:
                        act.wait_ge(s_w_lo, PAIRS + SPLITS * (i - 3))
                    split_hi(SPLITS * (PAIRS + i - 3))
                if fin:
                    act.wait_ge(s_to, t - 1)
                    nc.scalar.activation(oT[:, 0, :], psum_y[:, 0:P], ACT.Copy).then_inc(s_o_hi, 1)
                if split:
                    split_hi(SPLITS * (PAIRS + i - 3) + 1)
                if turn:
                    p_hi(t - 1, 2)
                    p_hi(t - 1, 3)
                if new:
                    act.wait_ge(s_negmax, t + 1)
                    for h in range(2):
                        if turn:
                            act.wait_ge(s_tp, 4 * (t - 1) + 2 * h + 2)
                        nc.scalar.activation(probs[:, h * S // 2 : (h + 1) * S // 2],
                                             psum_s[:, h * S // 2 : (h + 1) * S // 2], ACT.Exp, bias=neg_max,
                                             scale=alpha[:, 0:1], accum_out=row_sum[:, h : h + 1]).then_inc(s_exp, 1)

            for b in range(B):
                last = b == B - 1
                n0 = b * PAIRS
                if b == 0:
                    act.wait_ge(s_shift_x, 1)
                    x_norm(n0, 0)
                    x_hi(n0)
                x_norm(n0 + 1, 1)
                v_hi(n0, 0)
                x_hi(n0 + 1)
                if last:
                    act.wait_ge(s_scale_f, 1)
                    act.wait_ge(s_zero_fill, FILLS)
                    split_pair(0)
                with act.Fori(1, PAIRS - 1) as i:
                    x_norm(n0 + i + 1, i + 1)
                    v_hi(n0 + i, i)
                    x_hi(n0 + i + 1)
                    qk_hi(n0 + i - 1, i - 1)
                    if last:
                        copy_zT(act, 0, i - 1, 0)
                        split_pair(i)
                v_hi(n0 + PAIRS - 1, PAIRS - 1)
                qk_hi(n0 + PAIRS - 2, PAIRS - 2)
                if last:
                    copy_zT(act, 0, PAIRS - 2, 0)
                    split_pair(PAIRS - 1)
                qk_hi(n0 + PAIRS - 1, PAIRS - 1)
                if last:
                    copy_zT(act, 0, PAIRS - 1, 0)
                if last:
                    exps(act, 0)
                t0 = b * NT
                if last:
                    act.wait_ge(s_w_lo_v, PAIRS)
                step(t0, 0, True, False, False, False, False)
                if last:
                    act.wait_ge(s_eid, 1)
                step(t0 + 1, 1, True, True, False, False, False)
                step(t0 + 2, 2, True, True, True, False, False)
                with act.Fori(3, NT) as i:
                    step(t0 + i, i, True, True, True, True, last)
                step(t0 + NT, NT, False, True, True, True, last)
                step(t0 + NT + 1, NT + 1, False, False, True, True, last)
                step(t0 + NT + 2, NT + 2, False, False, False, True, last)
                if not last:
                    act.wait_ge(s_shift_x, b + 2)
                    x_norm(n0 + PAIRS, 0)
                    x_hi(n0 + PAIRS)

        @block.vector
        def _(dve):
            def link(ins):
                dve_steps[0] += 1
                ins.then_inc(s_dve, 1)
                dve.wait_ge(s_dve, dve_steps[0])

            def powers(amax, pow2, scale, signal):
                link(nc.vector.tensor_scalar(amax, amax, 2.0**-60, None, ALU.max))
                link(nc.vector.tensor_scalar(pow2.bitcast(I32), amax.bitcast(I32), EXP_BITS, None, ALU.bitwise_and))
                link(nc.vector.tensor_scalar(scale.bitcast(I32), pow2.bitcast(I32), -1.0,
                                             float((W_EXP + 2 * 127) << 23), ALU.mult, ALU.add))

            def half_stats(b, c):
                dve.wait_ge(s_x[2 * b + c], 16)
                with dve.Fori(0, 2) as q:
                    for g in range(NT // 4):
                        i = c * (NT // 2) + q * (NT // 4) + g
                        nc.vector.bn_stats(stats[:, bass.ds(i, 1), :].rearrange("p a k -> p (a k)"),
                                           x_sb[:, tile_of(b * NT + i)]).then_inc(s_dve, 1)
                dve_steps[0] += NT // 2
                dve.wait_ge(s_dve, dve_steps[0])

            def row_stats(b):
                half_stats(b, 0)
                half_stats(b, 1)

            def row_variance():
                half_mean, half_m2 = (lambda k: stats[:, :, 3 * k + 1]), (lambda k: stats[:, :, 3 * k + 2])
                nc.vector.tensor_tensor(tmp_x[:, 0, :], half_mean(0), half_mean(1), ALU.subtract)
                nc.vector.tensor_tensor(tmp_x[:, 1, :], half_m2(0), half_m2(1), ALU.add)
                link(nc.vector.tensor_tensor(mean_x, half_mean(0), half_mean(1), ALU.add))
                nc.vector.tensor_tensor(tmp_x[:, 2, :], tmp_x[:, 0, :], tmp_x[:, 0, :], ALU.mult)
                nc.vector.tensor_scalar(tmp_x[:, 1, :], tmp_x[:, 1, :], 1.0 / D, LN_EPS, ALU.mult, ALU.add)
                link(nc.vector.tensor_scalar(mean_x, mean_x, 0.5, None, ALU.mult))
                nc.vector.scalar_tensor_tensor(tmp_x[:, 3, :], tmp_x[:, 2, :], 0.25, tmp_x[:, 1, :], ALU.mult,
                                               ALU.add).then_inc(s_var_x, 1)

            half_stats(0, 0)
            dve.wait_ge(s_attn_w, 64)
            nc.vector.tensor_reduce(amax_a[:, :], attn_raw, AX.X, ALU.max, apply_absolute_value=True).then_inc(s_amax_a, 1)
            half_stats(0, 1)
            row_variance()
            dve.wait_ge(s_all_a, 1)
            powers(amax_a[:, :], pow_a[:, :], scale_a[:, :], None)
            link(nc.vector.tensor_tensor(alpha[:, :], pow_a[:, 0:1], pow_a[:, 1:2], ALU.mult))
            link(nc.vector.tensor_scalar(alpha[:, :], alpha[:, :], 2.0 ** (-2 * (W_EXP - 4)) / float(np.sqrt(HD)), None, ALU.mult))
            link(nc.vector.tensor_scalar(neg_alpha[:, :], alpha[:, :], -1.0, None, ALU.mult))
            link(nc.vector.tensor_tensor(attn_eps[:, :], scale_a[:, 2:3], scale_a[:, 3:4], ALU.mult))
            link(nc.vector.tensor_scalar(attn_eps[:, :], attn_eps[:, :], X_SCALE * QKV_SCALE, None, ALU.mult))
            link(nc.vector.tensor_tensor(attn_eps[:, :], attn_eps[:, :], attn_eps[:, :], ALU.mult))
            nc.vector.tensor_scalar(attn_eps[:, :], attn_eps[:, :], LN_EPS, None, ALU.mult).then_inc(s_scale_a, 1)
            dve.wait_ge(s_wt_hi, 4)
            for m in range(3):
                src = psum_t[m // 2][:, (m % 2) * D : (m % 2 + 1) * D].rearrange("p (c n) -> p c n", c=DC)
                at = slice(m * HD, (m + 1) * HD)
                nc.vector.scalar_tensor_tensor(wqkvT[:, :, 1, at], src, scale_a[:, m : m + 1], wqkvT[:, :, 0, at],
                                               ALU.mult, ALU.subtract).then_inc(s_wt_lo, 1)
            nc.vector.scalar_tensor_tensor(woT[:, 1, :], psum_t[1][:, D : 2 * D], scale_a[:, 3:4], woT[:, 0, :],
                                           ALU.mult, ALU.subtract).then_inc(s_wt_lo, 1)

            def group_amax(t):
                n = NE * NG // NT
                src = w_raw[:, bass.ds(t * n * GROUP, n * GROUP)].rearrange("p (g k) -> p g k", g=n)
                nc.vector.tensor_reduce(amax_g[:, bass.ds(t * n, n)], src, AX.X, ALU.max,
                                        apply_absolute_value=True).then_inc(s_amax_g, 1)

            def expert_amax():
                dve.wait_ge(s_amax_g, NT)
                dve.wait_ge(s_small, 32)
                link(nc.vector.tensor_reduce(amax_f[:, 0:NG], amax_g[:, :].rearrange("p (e g) -> p g e", g=NG), AX.X, ALU.max))
                for m in range(2):
                    ins = nc.vector.tensor_tensor(amax_f[:, m * DC : (m + 1) * DC], amax_f[:, m * DC : (m + 1) * DC],
                                                  norm_c[:, :], ALU.mult)
                link(ins)
                for m in range(3):
                    link(nc.vector.tensor_reduce(amax_f[:, m : m + 1], amax_f[:, m * DC : (m + 1) * DC], AX.X, ALU.max,
                                                 apply_absolute_value=True))
                nc.vector.tensor_scalar(amax_f[:, 6:7], amax_f[:, 0:1], 1.0, None, ALU.mult).then_inc(s_amax_f, 1)

            def expert_scales():
                dve.wait_ge(s_all_f, 1)
                powers(amax_f[:, 0:3], pow_f[:, :], scale_f[:, :], None)
                for m in range(2):
                    nc.vector.tensor_scalar(scale_g[:, 0, m * DC : (m + 1) * DC], norm_c[:, :], scale_f[:, m : m + 1],
                                            None, ALU.mult)
                link(nc.vector.tensor_copy(scale_g[:, 0, 2 * DC :], scale_f[:, 2:3].to_broadcast([P, NG - 2 * DC])))
                link(nc.vector.tensor_copy(scale_g[:, 1:, :], scale_g[:, 0:1, :].to_broadcast([P, NE - 1, NG])))
                nc.vector.tensor_scalar(amax_f[:, 7:8], amax_f[:, 0:1], 1.0, None, ALU.mult).then_inc(s_scale_f, 1)

            def product_scales():
                nc.vector.tensor_scalar(silu_scale[:, :], pow_f[:, 0:1], 2.0**-W_EXP / X_SCALE, None, ALU.mult)
                nc.vector.tensor_scalar(gate_scale[:, :], scale_f[:, 0:1], 2.0**-21 / X_SCALE, None, ALU.mult)
                for c in range(DC):
                    nc.vector.tensor_scalar(router_c[:, c, :], router_c[:, c, :], norm_c[:, c : c + 1], None, ALU.mult)
                link(nc.vector.tensor_tensor(y_unscale[:, :], pow_f[:, 0:1], pow_f[:, 1:2], ALU.mult))
                link(nc.vector.tensor_tensor(y_unscale[:, :], y_unscale[:, :], pow_f[:, 2:3], ALU.mult))
                link(nc.vector.tensor_scalar(y_unscale[:, :], y_unscale[:, :], 2.0 ** (21 - 3 * W_EXP), None, ALU.mult))

            def split_lo(n):
                dve.wait_ge(s_w_hi, n + 1)
                nc.vector.scalar_tensor_tensor(w_split[:, bass.ds(n * 2 * GROUP + GROUP, GROUP)],
                                               w_raw[:, bass.ds(n * GROUP, GROUP)],
                                               scale_g[:, :, :].rearrange("p e g -> p (e g)")[:, bass.ds(n, 1)],
                                               w_split[:, bass.ds(n * 2 * GROUP, GROUP)], ALU.mult,
                                               ALU.subtract).then_inc(s_w_lo_v, 1)

            def x_lo(n):
                dve.wait_ge(s_xt_hi, n + 1)
                nc.vector.tensor_tensor(xT[:, 1, :, :, :].rearrange("p u c t -> p (u c t)"), psum_t[0][:, :],
                                        xT[:, 0, :, :, :].rearrange("p u c t -> p (u c t)"), ALU.subtract).then_inc(s_xt_lo, 1)

            def v_and_rotation(n, i, u):
                dve.wait_ge(s_v_hi, 2 * n + u + 1)
                at = bass.ds((2 * i + u) * 2 * HD, HD)
                lo = bass.ds((2 * i + u) * 2 * HD + HD, HD)
                bank = psum_s[:, u * 512 : u * 512 + 3 * HD]
                nc.vector.scalar_tensor_tensor(v_sb[:, lo], bank[:, 2 * HD :], QKV_SCALE, v_sb[:, at],
                                               ALU.mult, ALU.subtract)
                if not (isinstance(n, int) and n == 0):
                    dve.wait_ge(s_qk, 2 * n + u - 1)
                pairs = bank[:, 0 : 2 * HD].rearrange("p (m k two) -> p m k two", m=2, two=2)
                t = tab[:, bass.ds((2 * i + u) * 3 * HD // 2, 3 * HD // 2)].rearrange("p (c k) -> p c k", c=3)
                shape = [P, 2, 2, HD // 2]
                for odd in range(2):
                    ins = nc.vector.tensor_tensor(
                        rot[:, u, odd, :].rearrange("p (m c k) -> p m c k", m=2, c=2),
                        pairs[:, :, :, odd].unsqueeze(2).to_broadcast(shape),
                        t[:, odd : odd + 2, :].unsqueeze(1).to_broadcast(shape), ALU.mult)
                ins.then_inc(s_rot, 1)

            def qk_lo(n, i):
                dve.wait_ge(s_qk_hi, n + 1)
                at = bass.ds(i * 2 * P, 2 * P)
                nc.vector.tensor_tensor(qkT[:, 1, :, at], psum_t[1][:, :].rearrange("p (m t) -> p m t", m=2),
                                        qkT[:, 0, :, at], ALU.subtract).then_inc(s_qk_lo, 1)

            def p_lo(t, g):
                dve.wait_ge(s_p_hi, 4 * t + g + 1)
                at = slice(g * 512, (g + 1) * 512)
                nc.vector.scalar_tensor_tensor(pT[:, 1, at], psum_t[g % 2][:, :], P_SCALE, pT[:, 0, at],
                                               ALU.mult, ALU.subtract).then_inc(s_p_lo, 1)

            def half_max(t, h):
                dve.wait_ge(s_scores, 2 * t + h + 1)
                nc.vector.tensor_reduce(row_max[:, h : h + 1], psum_s[:, h * S // 2 : (h + 1) * S // 2], AX.X,
                                        ALU.max).then_inc(s_max, 1)

            def step(t, new, turn, fin, norm, amax, ready=None):
                if turn:
                    p_lo(t - 1, 0)
                    p_lo(t - 1, 1)
                if fin:
                    dve.wait_ge(s_o_part, t - 1)
                    if norm:
                        dve.wait_ge(s_to, t - 2)
                    nc.vector.scalar_tensor_tensor(o_tok, psum_o[:, 0:HD], row_rec, o_part, ALU.mult,
                                                   ALU.add).then_inc(s_o, 1)
                if turn:
                    dve.wait_ge(s_exp, 2 * t)
                    nc.vector.tensor_scalar(row_sum[:, 0:1], row_sum[:, 0:1], row_sum[:, 1:2], P_SCALE,
                                            ALU.add, ALU.mult).then_inc(s_sum, 1)
                if new:
                    half_max(t, 0)
                if turn:
                    dve.wait_ge(s_sum, t)
                    nc.vector.reciprocal(row_rec, row_sum[:, 0:1]).then_inc(s_rec, 1)
                if fin:
                    dve.wait_ge(s_o_hi, t - 1)
                    nc.vector.tensor_tensor(oT[:, 1, :], psum_y[:, 0:P], oT[:, 0, :], ALU.subtract).then_inc(s_o_lo, 1)
                if new:
                    half_max(t, 1)
                    dve.wait_ge(s_max, 2 * t + 2)
                    nc.vector.scalar_tensor_tensor(neg_max, row_max[:, 0:1], row_max[:, 1:2], neg_alpha[:, 0:1],
                                                   ALU.max, ALU.mult).then_inc(s_negmax, 1)
                if turn:
                    p_lo(t - 1, 2)
                    p_lo(t - 1, 3)
                if fin:
                    dve.wait_ge(s_proj, t - 1)
                    nc.vector.bn_stats(y_stats, psum_y[:, D : 2 * D]).then_inc(s_ystat, 1)
                    dve.wait_ge(s_ystat, t - 1)
                    dve.sem_inc(s_held, 1)
                    nc.vector.bn_aggr(y_mv, y_stats).then_inc(s_ymv, 1)
                    dve.wait_ge(s_ymv, t - 1)
                    nc.vector.tensor_scalar(y_var, y_mv[:, 1:2], attn_eps[:, 0:1], None, ALU.add)
                    nc.vector.tensor_scalar(y_negmean, y_mv[:, 0:1], -1.0, None, ALU.mult).then_inc(s_yvar, 1)
                if amax:
                    group_amax(t)
                if ready is not None:
                    first_stats(dve, 1, ready)

            def first_turn(p):
                if not (isinstance(p, int) and p == 0):
                    dve.wait_ge(s_tz, p)
                for v in range(2):
                    j = 2 * p + v
                    nc.vector.tensor_scalar(z_turn[:, v, :], x_sb[:, tile_of(j)], f_mean[:, 0, bass.ds(j, 1)],
                                            f_rstd[:, 0, bass.ds(j, 1)], ALU.subtract, ALU.mult).then_inc(s_zn, 1)

            def first_routing():
                dve.wait_ge(s_fconst, 3)
                link(nc.vector.tensor_copy(rank_down, rank_down.bitcast(I32)))
                link(nc.vector.tensor_copy(tile_row, tile_row.bitcast(I32)))
                shifted_logits(dve, link, 0, x_rows[:, 0:NT, :])
                softmax(dve, link, 0)
                for c in range(2):
                    pick_best(dve, link, 0, c)
                gate_values(dve, link, 0)

            def begin(b):
                dve.wait_ge(s_rstd_x, b + 1)
                link(nc.vector.tensor_scalar(rstd_x, rstd_x, X_SCALE, None, ALU.mult))
                nc.vector.scalar_tensor_tensor(shift_x, mean_x, -1.0, rstd_x, ALU.mult, ALU.mult).then_inc(s_shift_x, 1)

            for b in range(B):
                last = b == B - 1
                n0 = b * PAIRS
                if b == 0:
                    dve.wait_ge(s_tab, 16)
                    begin(b)
                    x_lo(n0)

                def pair(n, i, before, more):
                    v_and_rotation(n, i, 0)
                    if more:
                        x_lo(n + 1)
                    v_and_rotation(n, i, 1)
                    if before:
                        qk_lo(n - 1, i - 1)
                    if last:
                        first_turn(i)
                        split_lo(SPLITS * i + 1)

                pair(n0, 0, False, True)
                with dve.Fori(1, PAIRS - 1) as i:
                    pair(n0 + i, i, True, True)
                pair(n0 + PAIRS - 1, PAIRS - 1, True, False)
                qk_lo(n0 + PAIRS - 1, PAIRS - 1)
                if last:
                    first_routing()
                else:
                    for e in range(NE):
                        dve.wait_ge(s_raw[e], 48)
                t0 = b * NT
                step(t0, True, False, False, False, b == 0)
                if last:
                    for place_step in place:
                        place_step(dve, link, 0)
                step(t0 + 1, True, True, False, False, b == 0)
                step(t0 + 2, True, True, True, False, b == 0)
                with dve.Fori(3, NT) as i:
                    step(t0 + i, True, True, True, True, b == 0, i - 3 if last else None)
                step(t0 + NT, False, True, True, True, False, NT - 3 if last else None)
                if not last:
                    expert_amax()
                step(t0 + NT + 1, False, False, True, True, False, NT - 2 if last else None)
                if not last:
                    row_stats(b + 1)
                    row_variance()
                    expert_scales()
                    begin(b + 1)
                    with dve.Fori(0, QUADS) as q:
                        for g in range(slots):
                            first_stats(dve, 0, q * slots + g)
                    x_lo(n0 + PAIRS)
                    dve.wait_ge(s_fstat, NT)
                    variance(link, b, slice(0, NT))
                    product_scales()
                    first_mean_square(dve, link, b)
            for n in range(NE * NG - 2 * SPLITS, NE * NG):
                split_lo(n)

        @block.tensor
        def _(pe):
            pe.wait_ge(s_const, 5)
            pe.wait_ge(s_attn_w, 64)
            for m in range(4):
                for c in range(DC):
                    at = (m % 2) * D + c * P
                    last = nc.tensor.transpose(psum_t[m // 2][:, at : at + P], attn_raw[:, m, c * P : (c + 1) * P], ident[:, :])
                if m % 2:
                    last.then_inc(s_wt, 1)

            def turn_x(n):
                if isinstance(n, int) and n == 0:
                    pe.wait_ge(s_wt_lo, 4)
                else:
                    pe.wait_ge(s_xt_lo, n)
                for u in range(2):
                    pe.wait_ge(s_xn, 2 * n + u + 1)
                    for c in range(DC):
                        last = nc.tensor.transpose(psum_t[0][:, (u * DC + c) * P : (u * DC + c + 1) * P],
                                                   xn[:, u, c * P : (c + 1) * P], ident[:, :])
                last.then_inc(s_tx, 1)

            def qkv(n):
                pe.wait_ge(s_xt_lo, n + 1)
                for u in range(2):
                    if not (isinstance(n, int) and n == 0):
                        pe.wait_ge(s_rot, 2 * n + u - 1)
                    for k, (c, lx, lw) in enumerate([(c, a, w) for c in range(DC) for a, w in ((0, 0), (0, 1), (1, 0))]):
                        last = nc.tensor.matmul(psum_s[:, u * 512 : u * 512 + 3 * HD], xT[:, lx, u, c, :],
                                                wqkvT[:, c, lw, :], start=(k == 0), stop=(k == 3 * DC - 1))
                    last.then_inc(s_qkv, 1)

            def turn_qk(n):
                if not (isinstance(n, int) and n == 0):
                    pe.wait_ge(s_qk_lo, n)
                for u in range(2):
                    pe.wait_ge(s_qk, 2 * n + u + 1)
                    for m in range(2):
                        last = nc.tensor.transpose(psum_t[1][:, (2 * m + u) * P : (2 * m + u + 1) * P],
                                                   qk_tok[:, u, m * HD : (m + 1) * HD], ident[:, :])
                last.then_inc(s_tqk, 1)

            def turn_p(t, g):
                pe.wait_ge(s_exp, 2 * t + g // 2 + 1)
                for k in range(4):
                    kc = 4 * g + k
                    last = nc.tensor.transpose(psum_t[g % 2][:, k * P : (k + 1) * P], probs[:, kc * P : (kc + 1) * P], ident[:, :])
                last.then_inc(s_tp, 1)

            def scores(i, kb):
                for k, (lq, lk) in enumerate(((0, 0), (0, 1), (1, 0))):
                    last = nc.tensor.matmul(psum_s[:, kb * 512 : (kb + 1) * 512], qkT[:, lq, 0, bass.ds(i * P, P)],
                                            qkT[:, lk, 1, kb * 512 : (kb + 1) * 512], start=(k == 0), stop=(k == 2))
                return last

            def step(t, i, new, turn, fin, norm):
                if turn:
                    for g in range(2):
                        if fin:
                            pe.wait_ge(s_p_lo, 4 * t - 6 + g + 1)
                        turn_p(t - 1, g)
                if new:
                    for h in range(2):
                        if turn:
                            pe.wait_ge(s_exp, 2 * t - 1 + h)
                        scores(i, 2 * h)
                        scores(i, 2 * h + 1).then_inc(s_scores, 1)
                if fin:
                    pe.wait_ge(s_o, t - 1)
                    if norm:
                        pe.wait_ge(s_ynorm, t - 2)
                    nc.tensor.transpose(psum_y[:, 0:P], o_tok, ident[:, :]).then_inc(s_to, 1)
                if turn:
                    for g in range(2, 4):
                        pe.wait_ge(s_p_lo, 4 * (t - 1) + g - 1)
                        turn_p(t - 1, g)
                if fin:
                    pe.wait_ge(s_o_lo, t - 1)
                    for k, (lo, lw) in enumerate(((0, 0), (0, 1), (1, 0))):
                        last = nc.tensor.matmul(psum_y[:, D : 2 * D], oT[:, lo, :], woT[:, lw, :], start=(k == 0), stop=(k == 2))
                    last.then_inc(s_proj, 1)
                if turn:
                    if fin:
                        pe.wait_ge(s_o, t - 1)
                    for kc in range(NT):
                        if kc % 4 == 0:
                            pe.wait_ge(s_p_lo, 4 * (t - 1) + kc // 4 + 1)
                        at = slice(kc * P, (kc + 1) * P)
                        nc.tensor.matmul(psum_o[:, 0 : 2 * HD], pT[:, 0, at], v_sb[:, kc * 2 * HD : (kc + 1) * 2 * HD],
                                         start=(kc == 0), stop=False, skip_group_check=True)
                        last = nc.tensor.matmul(psum_o[:, 0:HD], pT[:, 1, at], v_tiles[:, kc, 0, :],
                                                start=False, stop=(kc == NT - 1), skip_group_check=True)
                    last.then_inc(s_pv, 1)

            for b in range(B):
                n0 = b * PAIRS
                if b == 0:
                    turn_x(n0)

                def pair(n, i, before, more):
                    qkv(n)
                    if b == B - 1:
                        if not (isinstance(i, int) and i < 2):
                            logits(pe, 0, i - 2, 0)
                        if before:
                            turn(pe, 0, i - 1, 0)
                    if more:
                        turn_x(n + 1)
                    if before:
                        turn_qk(n - 1)

                pair(n0, 0, False, True)
                pair(n0 + 1, 1, True, True)
                with pe.Fori(2, PAIRS - 1) as i:
                    pair(n0 + i, i, True, True)
                pair(n0 + PAIRS - 1, PAIRS - 1, True, False)
                turn_qk(n0 + PAIRS - 1)
                if b == B - 1:
                    logits(pe, 0, PAIRS - 2, 0)
                    turn(pe, 0, PAIRS - 1, 0)
                    logits(pe, 0, PAIRS - 1, 0)
                t0 = b * NT
                pe.wait_ge(s_qk_lo, n0 + PAIRS)
                pe.wait_ge(s_rot, 2 * (n0 + PAIRS))
                step(t0, 0, True, False, False, False)
                if b == B - 1:
                    counts(pe, 0)
                step(t0 + 1, 1, True, True, False, False)
                step(t0 + 2, 2, True, True, True, False)
                with pe.Fori(3, NT) as i:
                    step(t0 + i, i, True, True, True, True)
                step(t0 + NT, None, False, True, True, True)
                step(t0 + NT + 1, None, False, False, True, True)
                if b + 1 < B:
                    turn_x(n0 + PAIRS)

        used[0] = routing_words
        z_aug = take(B * NT * ZW)
        z_rows = z_aug.rearrange("p (t w) -> p t w", w=ZW)
        after_experts = used[0]
        x_tile = take(UNROLL * ZW).rearrange("p (u w) -> p u w", u=UNROLL)
        x_row = take(D)
        e_xT = take(2 * D // 2).bitcast(F16).rearrange("p (l c t) -> p l c t", l=2, c=DC)
        silu_a = take(FF)
        h_row = take(FF)
        hT = take(2 * FF // 2).bitcast(F16).rearrange("p (l c t) -> p l c t", l=2, c=FC)
        y_row = take(UNROLL * D).rearrange("p (u d) -> p u d", u=UNROLL)
        gathered = take(slots * 2 * D).rearrange("p (g k d) -> p g k d", g=slots, k=2)
        gathered_odd = arena[:, after_experts : after_experts + slots * 2 * D].rearrange("p (g k d) -> p g k d", g=slots, k=2)
        squares = take(D)
        sum_sq = take(NT)
        f_shift = f_tmp[:, 3, :]
        token_i = take(NT).bitcast(I32)
        cell_i = take(TILES).bitcast(I32)
        cell_row = take(TILES)
        spare_row = take(TILES)
        spare_dest = take(TILES)
        dest = take(UNROLL).bitcast(U32)

        psum_a, psum_b = psum_s[:, 0:FF], psum_s[:, 512 : 512 + FF]
        psum_h, psum_x = psum_s[:, 1024:1536], psum_s[:, 1536 : 1536 + D]
        psum_e = psum_o[:, 0:D]

        s_z = sem("z_ready")
        s_half = sem("z_first_expert_added")
        s_sq = sem("z_squared")
        s_ldx = [sem(f"x_tile_loaded{u}") for u in range(UNROLL)]
        s_xrow = sem("x_row_ready")
        s_te = sem("x_row_turned")
        s_ex_hi = sem("expert_xT_hi")
        s_ex_lo = sem("expert_xT_lo")
        s_a = sem("a_ready")
        s_b = sem("b_ready")
        s_silu = sem("silu_ready")
        s_h = sem("h_ready")
        s_th = sem("h_turned")
        s_h_hi = sem("hT_hi")
        s_h_lo = sem("hT_lo")
        s_e = sem("expert_out_ready")
        s_yrow = sem("y_row_ready")
        s_sty = [sem(f"y_row_stored{u}") for u in range(UNROLL)]
        s_gather = [sem(f"gathered{g}") for g in range(slots)]
        s_sent = [sem(f"y_row_sent{u}") for u in range(UNROLL)]
        s_dest = sem("destinations_ready")
        s_second = sem("second_destinations_ready")
        s_held_p = sem("pool_waits_held")
        s_tok = [sem(f"token_rows_loaded{q}") for q in range(NT // slots)]
        s_fshift = sem("last_shift_ready")
        s_out_t = sem("out_normalised")
        s_out_r = sem("out_tile_ready")
        s_out = sem("out_stored")


        def zrow(j):
            return bass.ds(j * ZW, D)

        def zfac(j):
            return bass.ds(j * ZW + D, 1)


        GROUPS = TILES // UNROLL
        assert GROUPS * UNROLL == TILES
        STAGED = 12 // UNROLL

        def previous(k, i, u):
            if u:
                return k, i, u - 1
            return (k - 1, GROUPS - 1, UNROLL - 1) if isinstance(i, int) and i == 0 else (k, i - 1, UNROLL - 1)

        def following(k, i, u):
            if u + 1 < UNROLL:
                return k, i, u + 1
            return (k + 1, 0, 0) if isinstance(i, int) and i == GROUPS - 1 else (k, i + 1, 0)

        def expert_pass(eng, k, group, quad, stage, last, start=None):
            group(0, start if k == 0 else None, k == 0, False)
            group(1, lambda u, when: quad(k, 0, u, when), False, False)
            with eng.Fori(2, 1 + QUADS) as i:
                group(i, lambda u, when: quad(k, i - 1, u, when), False, False)
            staged = STAGED if k < 3 else 2
            for g in range(staged):
                group(1 + QUADS + g, lambda u, when: stage(k, UNROLL * g + u, when), False, False)
            if k < 3:
                with eng.Fori(1 + QUADS + staged, GROUPS - 1) as i:
                    group(i, None, False, False)
            else:
                with eng.Fori(3 + QUADS, 3 + 2 * QUADS) as i:
                    group(i, lambda u, when: last(i - 3 - QUADS, u, when), False, False)
                for i in range(3 + 2 * QUADS, GROUPS - 1):
                    group(i, None, False, False)
            group(GROUPS - 1, None, False, k == END)

        block_stack.close()
        block2 = ctx.enter_context(nc.Block())

        @block2.sync
        def _(sp):
            def load(k, i, u):
                s = k * TILES + i * UNROLL + u
                if k == END and not isinstance(i, int):
                    sp.wait_ge(s_dest, (i - 1) * UNROLL + u + 1)
                elif not (isinstance(s, int) and s < UNROLL):
                    sp.wait_ge(s_xrow, s - UNROLL + 1)
                rows = bass.ds((i * UNROLL + u) * P, P)
                sp.dma_start(x_tile[:, u, :], sorted_rows[order[k][1]][rows, :]).then_inc(s_ldx[u], 16)

            def store(k, i, u):
                sp.wait_ge(s_yrow, k * TILES + i * UNROLL + u + 1)
                rows = bass.ds((i * UNROLL + u) * P, P)
                sp.dma_start(expert_rows[order[k][1]][rows, :], y_row[:, u, :]).then_inc(s_sty[u], 16)

            def all_scattered(k):
                sp.wait_ge(s_scat[order[k][1]], 16 * 2 * NT * (order[k][0] + 1))

            all_scattered(0)
            for u in range(UNROLL):
                load(0, 0, u)
            for k in range(len(order)):
                with sp.Fori(0, GROUPS - 1) as i:
                    for u in range(UNROLL):
                        load(k, i + 1, u)
                        if k < END:
                            store(k, i, u)
                if k + 1 < len(order):
                    all_scattered(k + 1)
                for u in range(UNROLL):
                    if k + 1 < len(order):
                        load(k + 1, 0, u)
                    if k < END:
                        store(k, GROUPS - 1, u)
            out_view = out.rearrange("b (t p) d -> p (b t) d", p=P)
            src = x_rows[:, :, 0:D]

            def load_tokens(q):
                if q > 1:
                    sp.wait_ge(s_z, (B + END) * NT + (q - 1) * slots)
                for c in range(2):
                    at = c * S + q * slots * P
                    sp.dma_start((gathered, gathered_odd)[q % 2][:, :, c, :],
                                 token_rows[at : at + slots * P, :].rearrange("(g p) d -> p g d", p=P)).then_inc(s_tok[q], 16)

            for u in range(UNROLL):
                sp.wait_ge(s_sent[u], 16 * GROUPS)
            sp.wait_ge(s_z, (B + END) * NT)
            for c in range(B * QUADS):
                t = c * slots
                if c < QUADS:
                    load_tokens(c)
                sp.wait_ge(s_out_r, t + slots)
                sp.dma_start(out_view[:, t : t + slots, :], src[:, t : t + slots, :]).then_inc(s_out, 16)
            sp.wait_ge(s_out, 16 * B * QUADS)

        @block2.gpsimd
        def _(pool):
            nc.gpsimd.iota(token_i, pattern=[[P, NT]], base=0, channel_multiplier=1).then_inc(s_fconst, 1)
            nc.gpsimd.iota(cell_i, pattern=[[P, TILES]], base=0, channel_multiplier=1).then_inc(s_fconst, 1)

            def scatter(r, h):
                pool.wait_ge(s_rows, r + 1)
                for c in range(2):
                    if c and r == END:
                        pool.wait_ge(s_scat[h], 16 * (2 * (r // B) + 1) * NT)
                        column = z_rows[:, h * NT : (h + 1) * NT, D + 1]
                        nc.gpsimd.tensor_scalar(column, column, float(S), 1.0, ALU.add, ALU.mult).then_inc(s_second, 1)
                        pool.wait_ge(s_second, 1)
                    for j in range(NT):
                        nc.gpsimd.indirect_dma_start(
                            sorted_rows[h][:, :], bass.IndirectOffsetOnAxis(ap=rows_of[:, h, c, j : j + 1], axis=0),
                            z_rows[:, h * NT + j, :], None).then_inc(s_scat[h], 16)

            def gather(k, q, gs=range(slots)):
                h = order[k][1]
                if q == 0:
                    for u in range(UNROLL):
                        pool.wait_ge(s_sty[u], 16 * GROUPS * (k + 1))
                for g in gs:
                    j = q * slots + g
                    if k or q:
                        pool.wait_ge(s_z, (B + k) * NT + j - slots + 1)
                    for c in range(2):
                        nc.gpsimd.indirect_dma_start(
                            gathered[:, g, c, :], None, expert_rows[h][:, :],
                            bass.IndirectOffsetOnAxis(ap=rows_of[:, h, c, j : j + 1], axis=0)).then_inc(s_gather[g], 16)

            def send(i, u):
                s = i * UNROLL + u
                pool.wait_ge(s_dest, s + 1)
                pool.wait_ge(s_yrow, END * TILES + s + 1)
                pool.sem_inc(s_held_p, 1)
                nc.gpsimd.indirect_dma_start(
                    token_rows[:, :], bass.IndirectOffsetOnAxis(ap=dest[:, u : u + 1], axis=0), y_row[:, u, :],
                    None).then_inc(s_sent[u], 16)

            every = slice(0, NT)
            layer_norm_root(pool, 2, 1, every)
            rms_root(pool, 1)
            scatter(1, 1)
            for h in range(B):
                for q in range(QUADS):
                    gather(h, q)
                rms_root(pool, B + h)
                scatter(B + h, h)
            gather(B, 0)
            for i in range(QUADS + 1):
                for u in range(UNROLL):
                    send(i, u)
                    if 0 < i < QUADS and u < 2:
                        gather(B, i, (2 * u, 2 * u + 1))
            layer_norm_root(pool, B + 1, 0, every)
            with pool.Fori(QUADS + 1, GROUPS) as i:
                for u in range(UNROLL):
                    send(i, u)
            for q in range(QUADS):
                tiles = slice(q * slots, (q + 1) * slots)
                layer_norm_root(pool, B + 2 + q, 1, tiles)
                pool.wait_ge(s_frstd, B + 2 + q)
                nc.gpsimd.tensor_tensor(f_shift[:, tiles], f_mean[:, 1, tiles], f_rstd[:, 1, tiles], ALU.mult).then_inc(s_fshift, 1)
                for g in range(slots if q < QUADS - 1 else slots // 2):
                    j = NT + q * slots + g
                    pool.wait_ge(s_out_t, j + 1)
                    nc.gpsimd.tensor_tensor(x_sb[:, tile_of(j)], x_sb[:, tile_of(j)], z_aug[:, zrow(j)], ALU.add).then_inc(s_out_r, 1)

        @block2.scalar
        def _(act):
            def square(r, j, first=False):
                act.wait_ge(s_z, r * NT + j + 1)
                if not first:
                    act.wait_ge(s_sq, (r - B) * NT + j)
                nc.scalar.activation(squares, z_aug[:, zrow(r % B * NT + j)], ACT.Square,
                                     accum_out=sum_sq[:, bass.ds(j, 1)]).then_inc(s_sq, 1)

            def quad(k, q, u, when):
                if k < 3 and u and when == "mid":
                    r = B + k - 1
                    for g in range(2 if k else 0):
                        j = q * slots + 2 * (u - 1) + g
                        square(r, j, k == 1 and isinstance(j, int) and j == 0)
                    copy_zT(act, r, 2 * q + u - 1, u - 1)

            def stage(k, step, when):
                if k < 3 and step == 2 and when == "mid":
                    exps(act, B + k - 1)

            def last(q, u, when):
                pass

            def experts(k):
                def x_hi(s):
                    act.wait_ge(s_te, s + 1)
                    nc.scalar.activation(e_xT[:, 0, :, :].rearrange("p c t -> p (c t)"), psum_x, ACT.Copy).then_inc(s_ex_hi, 1)

                def h_hi(s):
                    act.wait_ge(s_th, s + 1)
                    nc.scalar.activation(hT[:, 0, :, :].rearrange("p c t -> p (c t)"), psum_h, ACT.Copy).then_inc(s_h_hi, 1)

                def silu(s):
                    act.wait_ge(s_a, s + 1)
                    nc.scalar.activation(silu_a, psum_a, ACT.Silu, scale=silu_scale[:, 0:1]).then_inc(s_silu, 1)

                def y_copy(k, i, u):
                    act.wait_ge(s_e, (k * GROUPS + i) * UNROLL + u + 1)
                    start = isinstance(i, int) and i == 0
                    if k == END and not start:
                        act.wait_ge(s_sent[u], 16 * i)
                    elif not (k == 0 and start):
                        act.wait_ge(s_sty[u], 16 * (k * GROUPS + i))
                    nc.scalar.activation(y_row[:, u, :], psum_e, ACT.Copy).then_inc(s_yrow, 1)

                def group(i, join, first, final):
                    for u in range(UNROLL):
                        s = (k * GROUPS + i) * UNROLL + u
                        begin = first and u == 0
                        if begin:
                            x_hi(s)
                        else:
                            h_hi(s - 1)
                        silu(s)
                        if not (final and u == UNROLL - 1):
                            x_hi(s + 1)
                        if join:
                            join(u, "mid")
                        if not begin:
                            y_copy(*previous(k, i, u))
                    if final:
                        h_hi(s)
                        y_copy(k, i, UNROLL - 1)

                expert_pass(act, k, group, quad, stage, last)

            for k in range(len(order)):
                experts(k)
            for q in range(QUADS):
                act.wait_ge(s_fshift, q + 1)
                for g in range(slots):
                    j = q * slots + g
                    nc.scalar.activation(z_aug[:, zrow(NT + j)], z_aug[:, zrow(NT + j)], ACT.Identity,
                                         bias=f_shift[:, j : j + 1], scale=f_rstd[:, 1, j : j + 1]).then_inc(s_out_t, 1)

        @block2.vector
        def _(dve):
            def link(ins):
                dve_steps[0] += 1
                ins.then_inc(s_dve, 1)
                dve.wait_ge(s_dve, dve_steps[0])

            def to_turn(r, q, g):
                j = q * slots + g
                dve.wait_ge(s_z, r * NT + j + 1 if r >= B else 2 * q * slots + g + 1)
                dve.wait_ge(s_tz, r * PAIRS + 2 * q + g // 2 - 1)
                nc.vector.tensor_scalar(z_turn[:, g, :], z_aug[:, zrow(r % B * NT + j)], 1.0, None, ALU.mult).then_inc(s_zn, 1)

            def combine(k, q, gs):
                h = order[k][1]
                rows = gathered_odd if k == END and q % 2 else gathered
                for g in gs:
                    j = q * slots + g
                    if k == END:
                        dve.wait_ge(s_tok[q], 32)
                    else:
                        dve.wait_ge(s_gather[g], 32 * (k * QUADS + q + 1))
                    nc.vector.scalar_tensor_tensor(z_aug[:, zrow(h * NT + j)], rows[:, g, 0, :],
                                                   gates[:, h, 0, bass.ds(j, 1)], z_aug[:, zrow(h * NT + j)],
                                                   ALU.mult, ALU.add).then_inc(s_half, 1)
                for g in gs:
                    j = q * slots + g
                    dve.wait_ge(s_half, k * NT + j + 1)
                    nc.vector.scalar_tensor_tensor(z_aug[:, zrow(h * NT + j)], rows[:, g, 1, :],
                                                   gates[:, h, 1, bass.ds(j, 1)], z_aug[:, zrow(h * NT + j)],
                                                   ALU.mult, ALU.add).then_inc(s_z, 1)

            def final_stats(k, q, gs):
                h = order[k][1]
                for g in gs:
                    j = q * slots + g
                    dve.wait_ge(s_z, (B + k) * NT + j + 1)
                    dve.sem_inc(s_held, 1)
                    nc.vector.bn_stats(f_stats[:, bass.ds(j, 1), :].rearrange("p a k -> p (a k)"),
                                       z_aug[:, zrow(h * NT + j)]).then_inc(s_fstat, 1)

            def finish(k, q, gs):
                h = order[k][1]
                for g in gs:
                    j = q * slots + g
                    nc.vector.tensor_scalar(z_aug[:, zrow(h * NT + j)], z_aug[:, zrow(h * NT + j)],
                                            f_mean[:, h, bass.ds(j, 1)], f_rstd[:, h, bass.ds(j, 1)], ALU.subtract,
                                            ALU.mult).then_inc(s_out_t, 1)
                for g in gs:
                    j = q * slots + g
                    dve.wait_ge(s_out_t, h * NT + j + 1)
                    nc.vector.tensor_tensor(x_sb[:, tile_of(h * NT + j)], x_sb[:, tile_of(h * NT + j)],
                                            z_aug[:, zrow(h * NT + j)], ALU.add).then_inc(s_out_r, 1)

            def mean_square(r):
                dve.wait_ge(s_sq, (r - B + 1) * NT)
                nc.vector.tensor_scalar(mean_sq[:, r % B, :], sum_sq, 1.0 / D, RMS_EPS, ALU.mult, ALU.add).then_inc(s_ms, 1)

            def first_z(h, q, gs):
                for g in gs:
                    j = q * slots + g
                    nc.vector.tensor_scalar(z_aug[:, zrow(h * NT + j)], x_sb[:, tile_of(h * NT + j)],
                                            f_mean[:, h, bass.ds(j, 1)], f_rstd[:, h, bass.ds(j, 1)], ALU.subtract,
                                            ALU.mult).then_inc(s_z, 1)

            def start(u, when):
                if u == 0:
                    first_stats(dve, 1, NT - 1)
                elif u == 1:
                    dve.wait_ge(s_fstat, 2 * NT)
                    variance(link, 1, slice(0, NT))
                else:
                    first_mean_square(dve, link, 1)

            def quad(k, q, u, when):
                if k == 0 and u == 2:
                    first_z(0, q, range(slots))
                if u < 2:
                    gs = (2 * u, 2 * u + 1)
                    if k:
                        combine(k - 1, q, gs)
                    else:
                        first_z(1, q, gs)
                    if k < 3:
                        for g in gs:
                            to_turn(B + k - 1, q, g)
                    else:
                        final_stats(k - 1, q, gs)

            def stage(k, step, when):
                if k < 3:
                    r = B + k - 1
                    if step == 0 and k:
                        mean_square(r)
                    elif step == 0:
                        dve.wait_ge(s_z, B * NT)
                        dve.sem_inc(s_held, 1)
                    elif step == 1:
                        shifted_logits(dve, link, r, z_rows[:, r % B * NT : (r % B + 1) * NT, :])
                    elif step == 3:
                        softmax(dve, link, r)
                    elif step in (4, 5):
                        pick_best(dve, link, r, step - 4)
                    elif step > 5:
                        (gate_values, *place)[step - 6](dve, link, r)
                elif step == 0:
                    dve.wait_ge(s_fstat, (B + 1) * NT)
                    variance(link, 0, slice(0, NT))
                elif step == 4:
                    dve.wait_ge(s_frstd, B + 1)

            def last(q, u, when):
                if u < 2:
                    finish(len(order) - B, q, (2 * u, 2 * u + 1))

            def experts(k):
                def x_rows(k, i, u):
                    s = (k * GROUPS + i) * UNROLL + u
                    dve.wait_ge(s_ldx[u], 16 * (k * GROUPS + i + 1))
                    if not (isinstance(s, int) and s == 0):
                        dve.wait_ge(s_te, s)
                    values, factor, less = x_tile[:, u, 0:D], x_tile[:, u, D : D + 1], x_tile[:, u, D + 1 : D + 2]
                    if order[k][1] == 0:
                        ins = nc.vector.tensor_scalar(x_row, values, less, factor, ALU.subtract, ALU.mult)
                    else:
                        ins = nc.vector.tensor_scalar(x_row, values, factor, None, ALU.mult)
                    ins.then_inc(s_xrow, 1)

                def destination(i, u):
                    if not (isinstance(i, int) and i == 0):
                        dve.wait_ge(s_sent[u], 16 * i)
                    nc.vector.tensor_tensor(dest[:, u : u + 1], x_tile[:, u, D + 1 : D + 2],
                                            spare_dest[:, bass.ds(i * UNROLL + u, 1)], ALU.max).then_inc(s_dest, 1)

                def x_lo(s):
                    dve.wait_ge(s_ex_hi, s + 1)
                    nc.vector.tensor_tensor(e_xT[:, 1, :, :].rearrange("p c t -> p (c t)"), psum_x,
                                            e_xT[:, 0, :, :].rearrange("p c t -> p (c t)"), ALU.subtract).then_inc(s_ex_lo, 1)

                def h_lo(s):
                    dve.wait_ge(s_h_hi, s + 1)
                    nc.vector.tensor_tensor(hT[:, 1, :, :].rearrange("p c t -> p (c t)"), psum_h,
                                            hT[:, 0, :, :].rearrange("p c t -> p (c t)"), ALU.subtract).then_inc(s_h_lo, 1)

                def gate(s):
                    dve.wait_ge(s_b, s + 1)
                    dve.wait_ge(s_silu, s + 1)
                    nc.vector.scalar_tensor_tensor(h_row, psum_b, gate_scale[:, 0:1], silu_a, ALU.mult,
                                                   ALU.mult).then_inc(s_h, 1)

                def group(i, join, first, final):
                    for u in range(UNROLL):
                        s = (k * GROUPS + i) * UNROLL + u
                        begin = first and u == 0
                        more = not (final and u == UNROLL - 1)
                        if begin:
                            x_rows(k, i, 0)
                            x_lo(s)
                        if more:
                            x_rows(*following(k, i, u))
                        if not begin:
                            h_lo(s - 1)
                        gate(s)
                        if more:
                            x_lo(s + 1)
                        if k == END:
                            destination(i, u)
                        if join:
                            join(u, "end")
                    if final:
                        h_lo(s)

                expert_pass(dve, k, group, quad, stage, last, start)

            dve.wait_ge(s_fconst, 5)
            link(nc.vector.memset(z_rows[:, :, D:ZW], 0.0))
            link(nc.vector.tensor_copy(z_rows[:, NT : 2 * NT, D + 1], token_i))
            link(nc.vector.tensor_copy(cell_row, cell_i))
            link(nc.vector.tensor_scalar(spare_row, cell_row, 2.0 * S, None, ALU.add))
            for k in range(len(order)):
                experts(k)
            k = len(order) - 1
            for q in range(QUADS):
                combine(k, q, range(slots))
                final_stats(k, q, range(slots))
                dve.wait_ge(s_fstat, (B + 1) * NT + (q + 1) * slots)
                variance(link, 1, slice(q * slots, (q + 1) * slots), -0.5)
            for j in range(2 * NT - slots // 2, 2 * NT):
                dve.wait_ge(s_out_t, j + 1)
                nc.vector.tensor_tensor(x_sb[:, tile_of(j)], x_sb[:, tile_of(j)], z_aug[:, zrow(j)], ALU.add).then_inc(s_out_r, 1)

        @block2.tensor
        def _(pe):
            def quad(k, q, u, when):
                if k < 3:
                    r = B + k - 1
                    if when == "mid":
                        if u == 2:
                            logits(pe, r, 2 * q, 0)
                        if u:
                            turn(pe, r, 2 * q + u - 1, u - 1)
                    elif u == 2:
                        logits(pe, r, 2 * q + 1, 1)

            def stage(k, step, when):
                if k < 3 and step == 6 and when == "mid":
                    counts(pe, B + k - 1)

            def last(q, u, when):
                pass

            def experts(k):
                def expert(k, i, u):
                    return pe.value_load(expert_of[0:1, order[k][1], bass.ds(i * UNROLL + u, 1)], min_val=0,
                                         max_val=NE - 1)

                def turn_x(n):
                    pe.wait_ge(s_xrow, n + 1)
                    for c in range(DC):
                        last = nc.tensor.transpose(psum_x[:, c * P : (c + 1) * P], x_row[:, c * P : (c + 1) * P], ident[:, :])
                    last.then_inc(s_te, 1)

                def inner(n, e):
                    pe.wait_ge(s_ex_lo, n + 1)
                    for m, (bank, signal) in enumerate(((psum_a, s_a), (psum_b, s_b))):
                        for q, (c, lx, lw) in enumerate([(c, a, w) for c in range(DC) for a, w in ((0, 0), (1, 0), (0, 1))]):
                            at = ((m * DC + c) * 2 + lw) * GROUP
                            last = nc.tensor.matmul(bank, e_xT[:, lx, c, :], w_split[:, bass.ds(e * EW + at, FF)],
                                                    start=(q == 0), stop=(q == 3 * DC - 1))
                        last.then_inc(signal, 1)

                def turn_h(n):
                    pe.wait_ge(s_h, n + 1)
                    for c in range(FC):
                        last = nc.tensor.transpose(psum_h[:, c * P : (c + 1) * P], h_row[:, c * P : (c + 1) * P], ident[:, :])
                    last.then_inc(s_th, 1)

                def outer(n, e):
                    pe.wait_ge(s_h_lo, n + 1)
                    if not (isinstance(n, int) and n == 0):
                        pe.wait_ge(s_yrow, n)
                    for q, (c, lh, lw) in enumerate([(c, a, w) for c in range(FC) for a, w in ((0, 0), (1, 0), (0, 1))]):
                        per = GROUP // D
                        at = ((2 * DC + c // per) * 2 + lw) * GROUP + c % per * D
                        last = nc.tensor.matmul(psum_e, hT[:, lh, c, :], w_split[:, bass.ds(e * EW + at, D)],
                                                start=(q == 0), stop=(q == 3 * FC - 1))
                    last.then_inc(s_e, 1)

                def group(i, join, first, final):
                    if isinstance(i, int) and i == 0:
                        pe.wait_ge(s_eid, k + 1)
                    for u in range(UNROLL):
                        n = (k * GROUPS + i) * UNROLL + u
                        begin = first and u == 0
                        if begin:
                            turn_x(n)
                        else:
                            turn_h(n - 1)
                        e = expert(k, i, u)
                        inner(n, e)
                        if not (final and u == UNROLL - 1):
                            turn_x(n + 1)
                        if join:
                            join(u, "mid")
                        if not begin:
                            outer(n - 1, before_e if u else expert(*previous(k, i, u)))
                        if join:
                            join(u, "end")
                        before_e = e
                    if final:
                        turn_h(n)
                        outer(n, before_e)

                expert_pass(pe, k, group, quad, stage, last)

            for k in range(len(order)):
                experts(k)


_INS = ["L0_attn_x", "L0_attn_wq", "L0_attn_wk", "L0_attn_wv", "L0_attn_wo", "L0_ffn_norm_w", "L0_ffn_router_w",
        "L0_ffn_w1", "L0_ffn_w3", "L0_ffn_w2"]


def kernel(**inputs):
    import concourse.bacc as _bacc
    from concourse.bass_utils import run_bass_kernel_spmd as _run

    nc = _bacc.Bacc("TRN2", target_bir_lowering=False, num_devices=1)
    arrays, args = {}, []
    named = [(name, np.ascontiguousarray(inputs[name])) for name in _INS] + [("rope", rope_table())]
    for name, a in named:
        arrays[f"in_{name}"] = a
        args.append(nc.dram_tensor(f"in_{name}", a.shape, mybir.dt.from_np(a.dtype), kind="ExternalInput").ap())
    args.append(nc.dram_tensor("out_0", (B, S, D), F32, kind="ExternalOutput").ap())
    args.append([nc.dram_tensor(f"sorted_rows{h}", (ROWS, ZW), F32, kind="Internal").ap() for h in range(B)])
    args.append([nc.dram_tensor(f"expert_rows{h}", (ROWS, D), F32, kind="Internal").ap() for h in range(B)])
    args.append(nc.dram_tensor("token_rows", (2 * S + ROWS, D), F32, kind="Internal").ap())
    sandwich_kernel(nc, *args)
    r = _run(nc, [arrays], core_ids=[0])
    return r.results[0]["out_0"]
```
